# Optimizing a Trainium2 kernel written in Bass

```python
import numpy as np
import jax
import jax.numpy as jnp

def _softmax(x, axis=-1):
    return jax.nn.softmax(x, axis=axis)

def _gelu(x):
    return jax.nn.gelu(x, approximate=True)

def _silu(x):
    return jax.nn.silu(x)

def _sigmoid(x):
    return jax.nn.sigmoid(x)

def _layernorm(x, axis=-1, eps=1e-05):
    m = jnp.mean(x, axis=axis, keepdims=True)
    v = jnp.var(x, axis=axis, keepdims=True)
    return (x - m) / jnp.sqrt(v + eps)

def _scatter_add(tgt, idx, src, axis=0):
    return tgt.at[idx].add(src)

def _segment_sum(src, seg, n):
    return jax.ops.segment_sum(src, seg, n)
kernel_name = 'mk_perceiver_d1_seqx_r8_0213b2'

def setup_inputs(seed: int=0):
    np.random.seed(seed)
    _w = jnp.asarray

    def _rec_inputs():
        import jax
        import jax.numpy as jnp
        _rk = jax.random.key(seed)
        x = -0.0005146 + 1 * jax.random.normal(jax.random.fold_in(_rk, 1), (16, 32, 512), jnp.float32)
        _lenS = 32 - jax.random.randint(jax.random.fold_in(_rk, 7), (16,), 0, max(1, 32 // 4) + 1, jnp.int32)
        _lenS2 = 512 - jax.random.randint(jax.random.fold_in(_rk, 8), (16,), 0, max(1, 512 // 4) + 1, jnp.int32)
        _ctx_4096P = jax.random.normal(jax.random.fold_in(_rk, 11), (16, 16, 512), jnp.float32)
        _ctx_4096c = jax.random.dirichlet(jax.random.fold_in(_rk, 511), 0.3 * jnp.ones((16,), jnp.float32), (16, 512))
        _ctx_4096t = jnp.einsum('bsk,bkd->bsd', _ctx_4096c, _ctx_4096P)
        _ctx_4096t = _ctx_4096t * jax.lax.rsqrt(jnp.mean(jnp.square(_ctx_4096t)) + 1e-12) * 0.953939
        ctx_4096 = -0.0142356 + 1.00583 * (_ctx_4096t + 0.3 * jax.random.normal(jax.random.fold_in(_rk, 611), (16, 512, 512), jnp.float32))
        return (x, ctx_4096)
    x, ctx_4096 = _rec_inputs()

    def _L0_xattn_setup():
        import jax, jax.numpy as jnp
        import numpy as np
        K = 10
        NUM_BITS = 10
        M_METHODS = 4

        def _quantize(coords, num_bits=NUM_BITS):
            cmin = coords.min(axis=1, keepdims=True)
            cmax = coords.max(axis=1, keepdims=True)
            scale = (2 ** num_bits - 1) / (cmax - cmin + 1e-06)
            q = jnp.floor((coords - cmin) * scale)
            return jnp.clip(q, 0, 2 ** num_bits - 1).astype(jnp.int32)

        def _morton_key(q):
            x, y, z = (q[..., 0], q[..., 1], q[..., 2])
            key = jnp.zeros(x.shape, dtype=jnp.int32)
            for b in range(NUM_BITS):
                key = key | (x >> b & 1) << 3 * b + 2 | (y >> b & 1) << 3 * b + 1 | (z >> b & 1) << 3 * b
            return key

        def _hilbert_key(q, num_bits=NUM_BITS):
            n = 3
            X = [q[..., i] for i in range(n)]
            M = 1 << num_bits - 1
            Q = M
            while Q > 1:
                P = Q - 1
                for i in range(n):
                    cond = X[i] & Q > 0
                    t = (X[0] ^ X[i]) & P
                    new_X0 = jnp.where(cond, X[0] ^ P, X[0] ^ t)
                    if i != 0:
                        X[i] = jnp.where(cond, X[i], X[i] ^ t)
                    X[0] = new_X0
                Q >>= 1
            for i in range(1, n):
                X[i] = X[i] ^ X[i - 1]
            t = jnp.zeros_like(X[0])
            Q = M
            while Q > 1:
                t = jnp.where(X[n - 1] & Q > 0, t ^ Q - 1, t)
                Q >>= 1
            X = [xi ^ t for xi in X]
            key = jnp.zeros(X[0].shape, dtype=jnp.int32)
            for b in range(num_bits - 1, -1, -1):
                for i in range(n):
                    key = key << 1 | X[i] >> b & 1
            return key

        def _sorted_indices(coords_bn3):
            q = _quantize(coords_bn3)
            qt = q[..., jnp.array([1, 0, 2])]
            keys = [_morton_key(q), _morton_key(qt), _hilbert_key(q), _hilbert_key(qt)]
            return [jnp.argsort(kk, axis=1) for kk in keys]

        def _window_inds(sorted_idx, k=K):
            B, N = sorted_idx.shape
            i = jnp.arange(N)
            start = jnp.maximum(0, i - k // 2)
            end = jnp.minimum(N, i + k // 2 + 1)
            pos = jnp.minimum(start[:, None] + jnp.arange(k)[None, :], (end - 1)[:, None])
            return jnp.take(sorted_idx, pos, axis=1)

        def _get_graph_features(feats, inds_list, perm, W_lin, b_lin, k=K):
            B, N, C = feats.shape
            center = feats[:, :, None, :]
            gather = jax.vmap(lambda f, idx: f[idx])
            per_method = []
            for inds in inds_list:
                neigh = gather(feats, inds)
                gf = jnp.concatenate([jnp.broadcast_to(center, (B, N, k, C)), neigh - center], axis=-1)
                per_method.append(gf)
            allf = jnp.stack(per_method, axis=-1)
            allf = allf[..., perm]
            total = 2 * C * M_METHODS
            x = allf.reshape(B * N, k, total)
            x16 = x.astype(jnp.float16).astype(jnp.float32)
            headdim = min(32, total)
            nheads = total // headdim
            qh = x16.reshape(B * N, k, nheads, headdim)
            scores = jnp.einsum('bihd,bjhd->bhij', qh, qh) / np.float32(np.sqrt(headdim))
            attn = jax.nn.softmax(scores, axis=-1)
            out = jnp.einsum('bhij,bjhd->bihd', attn, qh).reshape(B * N, k, total)
            fused = out @ W_lin.T + b_lin
            return fused.reshape(B, N, k, 64)

        def _instance_norm(x, axes):
            mu = x.mean(axis=axes, keepdims=True)
            var = x.var(axis=axes, keepdims=True)
            return (x - mu) / jnp.sqrt(var + 1e-05)

        def _lrelu(x):
            return jnp.where(x > 0, x, 0.2 * x)
        key = jax.random.key(seed)
        ks = jax.random.split(key, 8)
        B, N, C = (2, 512, 32)
        tot = M_METHODS * 2 * C
        s = 0.02
        return {'coords': jax.random.normal(ks[0], (B, 3, N), jnp.float32), 'feats': jax.random.normal(ks[1], (B, C, N), jnp.float32), 'W_lin1': jax.random.normal(ks[2], (64, tot), jnp.float32) * s, 'b_lin1': jnp.zeros((64,), jnp.float32), 'W_lin2': jax.random.normal(ks[3], (64, tot), jnp.float32) * s, 'b_lin2': jnp.zeros((64,), jnp.float32), 'W_conv1': jax.random.normal(ks[4], (C, 2 * C), jnp.float32) * s, 'W_conv2': jax.random.normal(ks[5], (2 * C, 2 * C), jnp.float32) * s, 'W_conv3': jax.random.normal(ks[6], (C, 4 * C), jnp.float32) * s}
    _L0_xattn_all = _L0_xattn_setup()
    _L0_xattn_in = {k: v for k, v in _L0_xattn_all.items() if k in ('W_lin1', 'b_lin1', 'W_lin2', 'b_lin2', 'W_conv1', 'W_conv2', 'W_conv3')}
    del _L0_xattn_all

    def _L0_attn_setup():
        import jax, jax.numpy as jnp
        import numpy as np
        H = 32
        DN = 128
        DR = 64
        DV = 128
        DQ = DN + DR
        HID = 512
        NEG_INF = -1e+30
        key = jax.random.key(seed)
        k0, k1, k2, k3 = jax.random.split(key, 4)
        B, S = (4, 128)
        hidden_states = jax.random.normal(k0, (B, S, HID), dtype=jnp.float32)
        wq = jax.random.normal(k1, (HID, H * DQ), dtype=jnp.float32) * 0.02
        wkv = jax.random.normal(k2, (HID, H * (DN + DV) + DR), dtype=jnp.float32) * 0.02
        wo = jax.random.normal(k3, (H * DV, HID), dtype=jnp.float32) * 0.02
        return {'hidden_states': hidden_states, 'wq': wq, 'wkv': wkv, 'wo': wo}
    _L0_attn_all = _L0_attn_setup()
    _L0_attn_in = {k: v for k, v in _L0_attn_all.items() if k in ('wq', 'wkv', 'wo')}
    del _L0_attn_all

    def _L0_ffn_setup():
        import jax, jax.numpy as jnp
        import numpy as np
        DIM = 512
        INTER = 128
        E = 16
        GROUPS = 4
        LIM = 2
        K = 2
        SHARED_INTER = 2 * INTER
        SCALE = 1.0
        key = jax.random.key(seed)
        ks = jax.random.split(key, 16)

        def n(k, shape, s=0.02):
            return jax.random.normal(k, shape, jnp.float32) * s
        return {'x': jax.random.normal(ks[0], (1, 256, DIM), jnp.float32), 'router_w': n(ks[1], (DIM, E)), 'router_b': n(ks[2], (E,)), 'router_bias': n(ks[3], (E,), 1.0), 'ew1': n(ks[4], (E, DIM, INTER)), 'eb1': n(ks[5], (E, INTER)), 'ew2': n(ks[6], (E, DIM, INTER)), 'eb2': n(ks[7], (E, INTER)), 'ew3': n(ks[8], (E, INTER, DIM)), 'eb3': n(ks[9], (E, DIM)), 'sw1': n(ks[10], (DIM, SHARED_INTER)), 'sb1': n(ks[11], (SHARED_INTER,)), 'sw2': n(ks[12], (DIM, SHARED_INTER)), 'sb2': n(ks[13], (SHARED_INTER,)), 'sw3': n(ks[14], (SHARED_INTER, DIM)), 'sb3': n(ks[15], (DIM,))}
    _L0_ffn_all = _L0_ffn_setup()
    _L0_ffn_in = {k: v for k, v in _L0_ffn_all.items() if k in ('router_w', 'router_b', 'router_bias', 'ew1', 'eb1', 'ew2', 'eb2', 'ew3', 'eb3', 'sw1', 'sb1', 'sw2', 'sb2', 'sw3', 'sb3')}
    del _L0_ffn_all
    return {'x': x, 'ctx_4096': ctx_4096, 'L0_xattn_W_lin1': _L0_xattn_in['W_lin1'], 'L0_xattn_b_lin1': _L0_xattn_in['b_lin1'], 'L0_xattn_W_lin2': _L0_xattn_in['W_lin2'], 'L0_xattn_b_lin2': _L0_xattn_in['b_lin2'], 'L0_xattn_W_conv1': _L0_xattn_in['W_conv1'], 'L0_xattn_W_conv2': _L0_xattn_in['W_conv2'], 'L0_xattn_W_conv3': _L0_xattn_in['W_conv3'], 'L0_attn_wq': _L0_attn_in['wq'], 'L0_attn_wkv': _L0_attn_in['wkv'], 'L0_attn_wo': _L0_attn_in['wo'], 'L0_ffn_router_w': _L0_ffn_in['router_w'], 'L0_ffn_router_b': _L0_ffn_in['router_b'], 'L0_ffn_router_bias': _L0_ffn_in['router_bias'], 'L0_ffn_ew1': _L0_ffn_in['ew1'], 'L0_ffn_eb1': _L0_ffn_in['eb1'], 'L0_ffn_ew2': _L0_ffn_in['ew2'], 'L0_ffn_eb2': _L0_ffn_in['eb2'], 'L0_ffn_ew3': _L0_ffn_in['ew3'], 'L0_ffn_eb3': _L0_ffn_in['eb3'], 'L0_ffn_sw1': _L0_ffn_in['sw1'], 'L0_ffn_sb1': _L0_ffn_in['sb1'], 'L0_ffn_sw2': _L0_ffn_in['sw2'], 'L0_ffn_sb2': _L0_ffn_in['sb2'], 'L0_ffn_sw3': _L0_ffn_in['sw3'], 'L0_ffn_sb3': _L0_ffn_in['sb3']}

def reference(x, ctx_4096, L0_xattn_W_lin1, L0_xattn_b_lin1, L0_xattn_W_lin2, L0_xattn_b_lin2, L0_xattn_W_conv1, L0_xattn_W_conv2, L0_xattn_W_conv3, L0_attn_wq, L0_attn_wkv, L0_attn_wo, L0_ffn_router_w, L0_ffn_router_b, L0_ffn_router_bias, L0_ffn_ew1, L0_ffn_eb1, L0_ffn_ew2, L0_ffn_eb2, L0_ffn_ew3, L0_ffn_eb3, L0_ffn_sw1, L0_ffn_sb1, L0_ffn_sw2, L0_ffn_sb2, L0_ffn_sw3, L0_ffn_sb3):
    import jax
    import jax.numpy as jnp

    def _L0_xattn_ref(coords, feats, W_lin1, b_lin1, W_lin2, b_lin2, W_conv1, W_conv2, W_conv3):
        import jax, jax.numpy as jnp
        import numpy as np
        K = 10
        NUM_BITS = 10
        M_METHODS = 4

        def _quantize(coords, num_bits=NUM_BITS):
            cmin = coords.min(axis=1, keepdims=True)
            cmax = coords.max(axis=1, keepdims=True)
            scale = (2 ** num_bits - 1) / (cmax - cmin + 1e-06)
            q = jnp.floor((coords - cmin) * scale)
            return jnp.clip(q, 0, 2 ** num_bits - 1).astype(jnp.int32)

        def _morton_key(q):
            x, y, z = (q[..., 0], q[..., 1], q[..., 2])
            key = jnp.zeros(x.shape, dtype=jnp.int32)
            for b in range(NUM_BITS):
                key = key | (x >> b & 1) << 3 * b + 2 | (y >> b & 1) << 3 * b + 1 | (z >> b & 1) << 3 * b
            return key

        def _hilbert_key(q, num_bits=NUM_BITS):
            n = 3
            X = [q[..., i] for i in range(n)]
            M = 1 << num_bits - 1
            Q = M
            while Q > 1:
                P = Q - 1
                for i in range(n):
                    cond = X[i] & Q > 0
                    t = (X[0] ^ X[i]) & P
                    new_X0 = jnp.where(cond, X[0] ^ P, X[0] ^ t)
                    if i != 0:
                        X[i] = jnp.where(cond, X[i], X[i] ^ t)
                    X[0] = new_X0
                Q >>= 1
            for i in range(1, n):
                X[i] = X[i] ^ X[i - 1]
            t = jnp.zeros_like(X[0])
            Q = M
            while Q > 1:
                t = jnp.where(X[n - 1] & Q > 0, t ^ Q - 1, t)
                Q >>= 1
            X = [xi ^ t for xi in X]
            key = jnp.zeros(X[0].shape, dtype=jnp.int32)
            for b in range(num_bits - 1, -1, -1):
                for i in range(n):
                    key = key << 1 | X[i] >> b & 1
            return key

        def _sorted_indices(coords_bn3):
            q = _quantize(coords_bn3)
            qt = q[..., jnp.array([1, 0, 2])]
            keys = [_morton_key(q), _morton_key(qt), _hilbert_key(q), _hilbert_key(qt)]
            return [jnp.argsort(kk, axis=1) for kk in keys]

        def _window_inds(sorted_idx, k=K):
            B, N = sorted_idx.shape
            i = jnp.arange(N)
            start = jnp.maximum(0, i - k // 2)
            end = jnp.minimum(N, i + k // 2 + 1)
            pos = jnp.minimum(start[:, None] + jnp.arange(k)[None, :], (end - 1)[:, None])
            return jnp.take(sorted_idx, pos, axis=1)

        def _get_graph_features(feats, inds_list, perm, W_lin, b_lin, k=K):
            B, N, C = feats.shape
            center = feats[:, :, None, :]
            gather = jax.vmap(lambda f, idx: f[idx])
            per_method = []
            for inds in inds_list:
                neigh = gather(feats, inds)
                gf = jnp.concatenate([jnp.broadcast_to(center, (B, N, k, C)), neigh - center], axis=-1)
                per_method.append(gf)
            allf = jnp.stack(per_method, axis=-1)
            allf = allf[..., perm]
            total = 2 * C * M_METHODS
            x = allf.reshape(B * N, k, total)
            x16 = x.astype(jnp.float16).astype(jnp.float32)
            headdim = min(32, total)
            nheads = total // headdim
            qh = x16.reshape(B * N, k, nheads, headdim)
            scores = jnp.einsum('bihd,bjhd->bhij', qh, qh) / np.float32(np.sqrt(headdim))
            attn = jax.nn.softmax(scores, axis=-1)
            out = jnp.einsum('bhij,bjhd->bihd', attn, qh).reshape(B * N, k, total)
            fused = out @ W_lin.T + b_lin
            return fused.reshape(B, N, k, 64)

        def _instance_norm(x, axes):
            mu = x.mean(axis=axes, keepdims=True)
            var = x.var(axis=axes, keepdims=True)
            return (x - mu) / jnp.sqrt(var + 1e-05)

        def _lrelu(x):
            return jnp.where(x > 0, x, 0.2 * x)
        inds_sorted = _sorted_indices(coords.transpose(0, 2, 1))
        inds_list = [_window_inds(s) for s in inds_sorted]
        perm1 = jnp.array([2, 0, 3, 1])
        perm2 = jnp.array([1, 3, 0, 2])
        f0 = feats.transpose(0, 2, 1)
        g1 = _get_graph_features(f0, inds_list, perm1, W_lin1, b_lin1)
        h1 = jnp.einsum('oc,bnkc->bonk', W_conv1, g1)
        h1 = _lrelu(_instance_norm(h1, (2, 3)))
        feats1 = h1.max(axis=-1)
        g2 = _get_graph_features(feats1.transpose(0, 2, 1), inds_list, perm2, W_lin2, b_lin2)
        h2 = jnp.einsum('oc,bnkc->bonk', W_conv2, g2)
        h2 = _lrelu(_instance_norm(h2, (2, 3)))
        feats2 = h2.max(axis=-1)
        f3 = jnp.concatenate([feats, feats1, feats2], axis=1)
        h3 = jnp.einsum('oc,bcn->bon', W_conv3, f3)
        return _lrelu(_instance_norm(h3, (2,)))

    def _L0_attn_ref(hidden_states, wq, wkv, wo):
        import jax, jax.numpy as jnp
        import numpy as np
        H = 32
        DN = 128
        DR = 64
        DV = 128
        DQ = DN + DR
        HID = 512
        NEG_INF = -1e+30
        B, S, D = hidden_states.shape
        q = jnp.einsum('bsd,de->bse', hidden_states, wq).reshape(B, S, H, DQ)
        kv = jnp.einsum('bsd,de->bse', hidden_states, wkv)
        k = kv[..., :H * DN].reshape(B, S, H, DN)
        v = kv[..., H * DN:H * (DN + DV)].reshape(B, S, H, DV)
        scale = DQ ** (-0.5)
        scores = jnp.einsum('bqhd,bkhd->bhqk', q[..., :DN], k) * scale
        causal = jnp.tril(jnp.ones((S, S), dtype=bool))
        scores = jnp.where(causal[None, None], scores, NEG_INF)
        probs = jax.nn.softmax(scores, axis=-1)
        attn = jnp.einsum('bhqk,bkhd->bqhd', probs, v).reshape(B, S, H * DV)
        return jnp.einsum('bse,ed->bsd', attn, wo)

    def _L0_ffn_ref(x, router_w, router_b, router_bias, ew1, eb1, ew2, eb2, ew3, eb3, sw1, sb1, sw2, sb2, sw3, sb3):
        import jax, jax.numpy as jnp
        import numpy as np
        DIM = 512
        INTER = 128
        E = 16
        GROUPS = 4
        LIM = 2
        K = 2
        SHARED_INTER = 2 * INTER
        SCALE = 1.0
        shape = x.shape
        xt = x.reshape(-1, DIM)
        T = xt.shape[0]
        logits = xt @ router_w + router_b
        scores = jax.nn.softmax(logits.astype(jnp.float32), axis=-1) + router_bias
        g = scores.reshape(T, GROUPS, E // GROUPS)
        _, gidx = jax.lax.top_k(g.max(axis=-1), LIM)
        keep = jnp.zeros((T, GROUPS), bool).at[jnp.arange(T)[:, None], gidx].set(True)
        masked = jnp.where(keep[:, :, None], g, -jnp.inf).reshape(T, E)
        _, idx = jax.lax.top_k(masked, K)
        vals = (jnp.take_along_axis(scores, idx, axis=1) * SCALE).astype(x.dtype)
        gate = jnp.zeros((T, E), x.dtype).at[jnp.arange(T)[:, None], idx].add(vals)

        def step(y, p):
            w1, b1, w2, b2, w3, b3, ge = p
            h = jax.nn.silu(xt @ w1 + b1) * (xt @ w2 + b2)
            return (y + ge[:, None] * (h @ w3 + b3), None)
        y, _ = jax.lax.scan(step, jnp.zeros_like(xt), (ew1, eb1, ew2, eb2, ew3, eb3, gate.T))
        z = jax.nn.silu(xt @ sw1 + sb1) * (xt @ sw2 + sb2) @ sw3 + sb3
        return (y + z).reshape(shape)
    x = x + _L0_xattn_ref(ctx_4096, _layernorm(x, axis=-1), L0_xattn_W_lin1, L0_xattn_b_lin1, L0_xattn_W_lin2, L0_xattn_b_lin2, L0_xattn_W_conv1, L0_xattn_W_conv2, L0_xattn_W_conv3)
    x = x + _L0_attn_ref(_layernorm(x, axis=-1), L0_attn_wq, L0_attn_wkv, L0_attn_wo)
    x = x + _L0_ffn_ref(_layernorm(x, axis=-1), L0_ffn_router_w, L0_ffn_router_b, L0_ffn_router_bias, L0_ffn_ew1, L0_ffn_eb1, L0_ffn_ew2, L0_ffn_eb2, L0_ffn_ew3, L0_ffn_eb3, L0_ffn_sw1, L0_ffn_sb1, L0_ffn_sw2, L0_ffn_sb2, L0_ffn_sw3, L0_ffn_sb3)
    return x

_drawn_inputs = setup_inputs


def setup_inputs(seed=0):
    import zlib

    import numpy as np

    out = dict(_drawn_inputs(seed))
    spreads = {'L0_xattn_b_lin1': (0.0, 2.0), 'L0_xattn_b_lin2': (0.0, 2.0)}
    factors = {'L0_ffn_router_w': 8.0,
     'L0_ffn_router_b': 200.0,
     'L0_ffn_eb1': 8.0,
     'L0_ffn_eb2': 8.0,
     'L0_ffn_sb1': 42.669,
     'L0_ffn_sb2': 41.403,
     'L0_ffn_sb3': 3.558}
    for name, (base, spread) in spreads.items():
        noise = np.random.default_rng([zlib.crc32(name.encode()), seed]).standard_normal(out[name].shape)
        drawn = base * np.exp(spread * noise) if base else spread * noise
        out[name] = jnp.asarray(drawn.astype(out[name].dtype))
    for name, factor in factors.items():
        out[name] = (out[name] * factor).astype(out[name].dtype)
    return out
```

```python
from contextlib import ExitStack

import concourse.bass as bass
from concourse import mybir

F32 = mybir.dt.float32
F16 = mybir.dt.float16
BF16 = mybir.dt.bfloat16
I32 = mybir.dt.int32
ALU = mybir.AluOpType
ACT = mybir.ActivationFunctionType
AX = mybir.AxisListType

P = 128
B, C, N = 16, 32, 512
TOK = B * C
NT = TOK // P
NC = N // P
K = 10
METHODS = 4
BITS = 10
HD = 32
GH = C * METHODS // HD
PB = 3
NG = 11
GB = 16
NBLK = NG * GB
NPAD = NBLK * PB
PERM = ([2, 0, 3, 1], [1, 3, 0, 2])
OUTC = (32, 64)
LN_EPS = 1e-5
WSCALE = 256.0
NEG = -1e30


def window(t, start, dims):
    a = t[:, start:start + 1]
    return bass.AP(a.tensor, a.offset, [list(a.ap[0])] + [list(d) for d in dims])


class Chain:

    def __init__(self, eng, sem):
        self.eng, self.sem, self.n = eng, sem, 0

    def __call__(self, ins):
        self.n += 1
        ins.then_inc(self.sem, 1)
        self.eng.wait_ge(self.sem, self.n)


class Memory:
    def __init__(self, nc, ctx):
        self.nc, self.ctx = nc, ctx

    def sb(self, name, shape, dt=F32):
        return self.ctx.enter_context(self.nc.sbuf_tensor(name, shape, dt))

    def ps(self, name):
        return self.ctx.enter_context(self.nc.psum_tensor(name, [P, 512], F32))

    def sem(self, name):
        return self.ctx.enter_context(self.nc.semaphore(name))


def prepare(nc, a, keep, scratch):
    with ExitStack() as ctx:
        m = Memory(nc, ctx)
        xt = m.sb("p_x", [P, NT, N])
        ft = m.sb("p_f", [P, NT, N])
        stats = m.sb("p_stats", [P, NT, 6])
        mv = m.sb("p_mv", [P, NT, 2])
        veps = m.sb("p_veps", [P, NT])
        rstd = m.sb("p_rstd", [P, NT])
        mhalf = m.sb("p_mhalf", [P, NT])
        R48 = 3 * B
        co = m.sb("p_co", [R48, N])
        cmin = m.sb("p_cmin", [R48, 1])
        cmax = m.sb("p_cmax", [R48, 1])
        top = m.sb("p_top", [R48, 1])
        cscale = m.sb("p_cscale", [R48, 1])
        dq = m.sb("p_dq", [R48, 10])
        qv = m.sb("p_qv", [R48, N])
        qi = m.sb("p_qi", [R48, N], I32)
        qf = m.sb("p_qf", [R48, N])
        gt = m.sb("p_gt", [R48, N])
        X = m.sb("p_X", [P, 3, NC, 2, B], I32)
        Y = m.sb("p_Y", [P, 3, NC, 2, B], I32)
        mk = m.sb("p_mk", [P, NC, 2, B], I32)
        mn = m.sb("p_mn", [P, NC, 2, B], I32)
        uu = m.sb("p_uu", [P, NC, 2, B], I32)
        tt = m.sb("p_tt", [P, NC, 2, B], I32)
        sp = m.sb("p_sp", [P, 3, NC, 2, B], I32)
        kt = m.sb("p_kt", [P, NC, METHODS, B], I32)
        kr = m.sb("p_kr", [METHODS * B, N])
        wl = [m.sb(f"p_wl{i}", [64, 256]) for i in range(2)]
        wr = [m.sb(f"p_wr{i}", [64, 2, GH, METHODS, 8]) for i in range(2)]
        wct = [m.sb(f"p_wct{i}", [64, P]) for i in range(2)]
        bl = [m.sb(f"p_bl{i}", [64, 1]) for i in range(2)]
        wf = m.sb("p_wf", [P, 2, 2, 64])
        ps_q = m.ps("pp_q")
        ps_k = m.ps("pp_k")
        ps_w = m.ps("pp_w")

        s_x = m.sem("x_loaded")
        s_c = m.sem("coords_loaded")
        s_w = m.sem("small_weights_loaded")
        s_feat = m.sem("features_ready")
        s_fout = m.sem("features_stored")
        s_var = m.sem("variance_ready")
        s_rstd = m.sem("rstd_ready")
        s_id = m.sem("identity_ready")
        s_q = m.sem("quantised")
        s_qt = m.sem("coords_transposed")
        s_key = m.sem("keys_ready")
        s_kt = m.sem("keys_transposed")
        s_kr = m.sem("key_rows_ready")
        s_wr = m.sem("weights_reordered")
        s_wp = m.sem("weight_product_ready")
        s_d = m.sem("prepare_dve_step")
        s_g = m.sem("prepare_pool_step")
        block = ctx.enter_context(nc.Block())

        @block.sync
        def _(sp_):
            for t in range(NT):
                sp_.dma_start(xt[:, t, :], a["x"].rearrange("b c n -> (b c) n")[t * P:(t + 1) * P, :]).then_inc(s_x, 16)
            for c in range(3):
                sp_.dma_start(co[c * B:(c + 1) * B, :], a["ctx_4096"][:, c, :]).then_inc(s_c, 16)
            for t in range(NT):
                sp_.wait_ge(s_feat, t + 1)
                sp_.dma_start(scratch["feats"][t * P:(t + 1) * P, :], ft[:, t, :]).then_inc(s_fout, 16)
            sp_.wait_ge(s_kr, 1)
            sp_.dma_start(scratch["keys"].rearrange("m b n -> (m b) n"), kr[:, :]).then_inc(s_fout, 16)
            sp_.wait_ge(s_fout, 16 * (NT + 1))

        @block.gpsimd
        def _(pool):
            link = Chain(pool, s_g)
            link(pool.memset(keep["ident"][:, :], 0.0))
            pool.affine_select(out=keep["ident"][:, :], in_=keep["ident"][:, :], compare_op=ALU.not_equal, fill=1.0,
                               base=0, pattern=[[-1, P]], channel_multiplier=1).then_inc(s_id, 1)
            link(pool.memset(mhalf[:, :], -0.5))
            for t in range(NT):
                pool.wait_ge(s_var, t + 1)
                pool.tensor_tensor(rstd[:, t:t + 1], veps[:, t:t + 1], mhalf[:, t:t + 1], ALU.pow).then_inc(s_rstd, 1)
            pool.iota(keep["iota"][:, :], pattern=[[1, N]], base=0, channel_multiplier=0,
                      allow_small_or_imprecise_dtypes=True)
            link(pool.memset(keep["tri"][:, :], 1.0))
            link(pool.affine_select(out=keep["tri"][:, :], in_=keep["tri"][:, :], compare_op=ALU.is_gt, fill=0.0,
                                    base=0, pattern=[[-1, P]], channel_multiplier=1))
            ind = keep["ind"]
            link(pool.memset(ind[:, :], 1.0))
            iv = ind[:, :].rearrange("p (h c) -> p h c", h=GH)
            link(pool.affine_select(out=iv, in_=iv, compare_op=ALU.is_ge, fill=0.0, base=0,
                                    pattern=[[0, GH], [1, 32]], channel_multiplier=-K))
            link(pool.affine_select(out=iv, in_=iv, compare_op=ALU.is_ge, fill=0.0, base=K - 1,
                                    pattern=[[0, GH], [-1, 32]], channel_multiplier=K))
            off = keep["off"]
            link(pool.memset(off[:, :], 0.0))
            ov = off[:, :].rearrange("p (u c) -> p u c", u=GB)
            link(pool.affine_select(out=ov, in_=ov, compare_op=ALU.is_ge, fill=NEG, base=0,
                                    pattern=[[0, GB], [1, 32]], channel_multiplier=-K))
            link(pool.affine_select(out=ov, in_=ov, compare_op=ALU.is_ge, fill=NEG, base=K - 1,
                                    pattern=[[0, GB], [-1, 32]], channel_multiplier=K))
            for l, o in enumerate(OUTC):
                t = keep["same"][l]
                link(pool.memset(t[:, :], 0.0))
                for d in range(-(P // o) + 1, P // o):
                    link(pool.affine_select(out=t[:, :], in_=t[:, :], compare_op=ALU.not_equal, fill=1.0,
                                            base=-d * o, pattern=[[-1, P]], channel_multiplier=1))
            for cg in range(4):
                t = keep["gather"][:, cg, :]
                link(pool.memset(t, 0.0))
                v = t.rearrange("p (h m c) -> p h m c", h=GH, m=METHODS)
                link(pool.affine_select(out=v, in_=v, compare_op=ALU.not_equal, fill=1.0, base=-32 * cg,
                                        pattern=[[-8, GH], [0, METHODS], [-1, 8]], channel_multiplier=1))

        @block.scalar
        def _(act):
            with nc.allow_non_contiguous_dma(reason="small weights, transposed once"):
                for i, (w, cv, b) in enumerate((("L0_xattn_W_lin1", "L0_xattn_W_conv1", "L0_xattn_b_lin1"),
                                                ("L0_xattn_W_lin2", "L0_xattn_W_conv2", "L0_xattn_b_lin2"))):
                    act.dma_start(wl[i][:, :], a[w]).then_inc(s_w, 16)
                    o = OUTC[i]
                    for r in range(P // o):
                        act.dma_start(wct[i][:, r * o:(r + 1) * o], a[cv].rearrange("o e -> e o")).then_inc(s_w, 16)
                    act.dma_start(bl[i][:, :], a[b].rearrange("(e u) -> e u", u=1)).then_inc(s_w, 16)
                for i in range(2):
                    for h in range(GH):
                        act.wait_ge(s_d, 1)
                        act.dma_start(keep["w3"][32 * h:32 * h + 8, i, :],
                                      a["L0_xattn_W_conv3"][:, 32 * i + 8 * h:32 * i + 8 * h + 8].rearrange("o c -> c o")).then_inc(s_w, 16)
                for r in range(2):
                    act.dma_start(keep["w3"][64 * r:64 * r + 64, 2 + r, :],
                                  a["L0_xattn_W_conv3"][:, 64:128].rearrange("o c -> c o")).then_inc(s_w, 16)
            act.wait_ge(s_w, 16 * (4 + 2 + 4 + 8 + 2))

        @block.tensor
        def _(pe):
            pe.wait_ge(s_id, 1)
            pe.wait_ge(s_q, 1)
            for j in range(NC):
                last = pe.transpose(ps_q[:, j * 64:j * 64 + R48], qf[:, j * P:(j + 1) * P], keep["ident"][0:R48, 0:R48])
            last.then_inc(s_qt, 1)
            pe.wait_ge(s_key, 1)
            for j in range(NC):
                last = pe.transpose(ps_k[0:METHODS * B, j * P:(j + 1) * P],
                                    keep["keys"][:, j].rearrange("p m b -> p (m b)"), keep["ident"][:, :])
            last.then_inc(s_kt, 1)
            pe.wait_ge(s_wr, 1)
            for i, o in enumerate(OUTC):
                for part in range(2):
                    at = (2 * i + part) * 64
                    pe.matmul(ps_w[:, at:at + o], wr[i][:, part].rearrange("e h m c -> e (h m c)"), wct[i][:, 0:o],
                              start=True, stop=True)
                last = pe.matmul(ps_w[:, 256 + i:257 + i], wct[i][:, :], bl[i][:, :], start=True, stop=True)
            last.then_inc(s_wp, 1)

        @block.vector
        def _(dve):
            link = Chain(dve, s_d)
            link(dve.memset(keep["w3"][:, :, :], 0.0))
            link(dve.memset(top[:, :], float(2 ** BITS - 1)))
            dve.wait_ge(s_c, 48)
            link(dve.tensor_reduce(out=cmin[:, :], in_=co[:, :], axis=AX.X, op=ALU.min))
            link(dve.tensor_reduce(out=cmax[:, :], in_=co[:, :], axis=AX.X, op=ALU.max))
            link(dve.tensor_scalar(out=cmax[:, :], in0=cmax[:, :], scalar1=cmin[:, 0:1], scalar2=1e-6,
                                   op0=ALU.subtract, op1=ALU.add))
            num, rng, inv, quo, rh, rl, qh, ql, res, prod = (dq[:, i:i + 1] for i in range(10))
            link(dve.tensor_copy(rng, cmax[:, :]))
            link(dve.reciprocal(inv, rng))
            link(dve.tensor_tensor(quo, top[:, :], inv, ALU.mult))
            for whole, high, low in ((rng, rh, rl), (quo, qh, ql)):
                link(dve.tensor_scalar(out=high.bitcast(I32), in0=whole.bitcast(I32), scalar1=-4096, scalar2=None,
                                       op0=ALU.bitwise_and))
                link(dve.tensor_tensor(low, whole, high, ALU.subtract))
            link(dve.tensor_copy(res, top[:, :]))
            for x_, y_ in ((qh, rh), (qh, rl), (ql, rh), (ql, rl)):
                link(dve.tensor_tensor(prod, x_, y_, ALU.mult))
                link(dve.tensor_tensor(res, res, prod, ALU.subtract))
            link(dve.tensor_tensor(res, res, inv, ALU.mult))
            link(dve.tensor_tensor(cscale[:, :], quo, res, ALU.add))
            link(dve.tensor_scalar(out=qv[:, :], in0=co[:, :], scalar1=cmin[:, 0:1], scalar2=cscale[:, 0:1],
                                   op0=ALU.subtract, op1=ALU.mult))
            link(dve.tensor_copy(qi[:, :], qv[:, :]))
            link(dve.tensor_copy(qf[:, :], qi[:, :]))
            link(dve.tensor_tensor(gt[:, :], qf[:, :], qv[:, :], ALU.is_gt))
            link(dve.tensor_tensor(qf[:, :], qf[:, :], gt[:, :], ALU.subtract))
            dve.tensor_scalar(out=qf[:, :], in0=qf[:, :], scalar1=0.0, scalar2=float(2 ** BITS - 1),
                              op0=ALU.max, op1=ALU.min).then_inc(s_q, 1)
            for t in range(NT):
                dve.wait_ge(s_x, 16 * NT)
                link(dve.bn_stats(out=stats[:, t, :], in_=xt[:, t, :]))
                link(dve.bn_aggr(out=mv[:, t, :], in_=stats[:, t, :]))
                dve.tensor_scalar(out=veps[:, t:t + 1], in0=mv[:, t, 1:2], scalar1=LN_EPS, scalar2=None,
                                  op0=ALU.add).then_inc(s_var, 1)
            for t in range(NT):
                dve.wait_ge(s_rstd, t + 1)
                dve.tensor_scalar(out=ft[:, t, :], in0=xt[:, t, :], scalar1=mv[:, t, 0:1], scalar2=rstd[:, t:t + 1],
                                  op0=ALU.subtract, op1=ALU.mult).then_inc(s_feat, 1)
            dve.wait_ge(s_qt, 1)
            for v, order in enumerate(((0, 1, 2), (1, 0, 2))):
                for i, c in enumerate(order):
                    src = ps_q[:, 0:NC * 64].rearrange("p (j q) -> p j q", j=NC)[:, :, c * B:(c + 1) * B]
                    link(dve.tensor_copy(X[:, i, :, v, :], src))

            def spread(src, dst):
                cur = src
                for sh, mask in ((16, 0x030000FF), (8, 0x0300F00F), (4, 0x030C30C3), (2, 0x09249249)):
                    link(dve.scalar_tensor_tensor(out=dst, in0=cur, scalar=sh, in1=cur,
                                                  op0=ALU.logical_shift_left, op1=ALU.bitwise_or))
                    link(dve.tensor_scalar(out=dst, in0=dst, scalar1=mask, scalar2=None, op0=ALU.bitwise_and))
                    cur = dst

            def interleave(kind):
                link(dve.scalar_tensor_tensor(out=uu[:], in0=sp[:, 0], scalar=2, in1=sp[:, 2],
                                              op0=ALU.logical_shift_left, op1=ALU.bitwise_or))
                link(dve.scalar_tensor_tensor(out=uu[:], in0=sp[:, 1], scalar=1, in1=uu[:],
                                              op0=ALU.logical_shift_left, op1=ALU.bitwise_or))
                link(dve.tensor_scalar(out=tt[:], in0=uu[:], scalar1=2, scalar2=31,
                                       op0=ALU.logical_shift_left, op1=ALU.arith_shift_right))
                link(dve.tensor_scalar(out=tt[:], in0=tt[:], scalar1=-1, scalar2=-1073741825,
                                       op0=ALU.bitwise_xor, op1=ALU.bitwise_and))
                link(dve.tensor_tensor(kt[:, :, 2 * kind:2 * kind + 2, :], uu[:], tt[:], ALU.bitwise_xor))

            spread(X[:], sp[:])
            interleave(0)
            q = BITS - 1
            while q >= 1:
                low = (1 << q) - 1
                for i in range(3):
                    link(dve.tensor_scalar(out=mk[:], in0=X[:, i], scalar1=31 - q, scalar2=31,
                                           op0=ALU.logical_shift_left, op1=ALU.arith_shift_right))
                    if i:
                        link(dve.tensor_scalar(out=mn[:], in0=mk[:], scalar1=-1, scalar2=low,
                                               op0=ALU.bitwise_xor, op1=ALU.bitwise_and))
                        link(dve.tensor_tensor(uu[:], X[:, 0], X[:, i], ALU.bitwise_xor))
                        link(dve.tensor_tensor(uu[:], uu[:], mn[:], ALU.bitwise_and))
                        link(dve.tensor_tensor(X[:, i], X[:, i], uu[:], ALU.bitwise_xor))
                        link(dve.tensor_tensor(X[:, 0], X[:, 0], uu[:], ALU.bitwise_xor))
                    link(dve.scalar_tensor_tensor(out=X[:, 0], in0=mk[:], scalar=low, in1=X[:, 0],
                                                  op0=ALU.bitwise_and, op1=ALU.bitwise_xor))
                q -= 1
            for i in (1, 2):
                link(dve.tensor_tensor(X[:, i], X[:, i], X[:, i - 1], ALU.bitwise_xor))
            link(dve.memset(mn[:], 0))
            for q in range(BITS - 1, 0, -1):
                link(dve.tensor_scalar(out=mk[:], in0=X[:, 2], scalar1=31 - q, scalar2=31,
                                       op0=ALU.logical_shift_left, op1=ALU.arith_shift_right))
                link(dve.scalar_tensor_tensor(out=mn[:], in0=mk[:], scalar=(1 << q) - 1, in1=mn[:],
                                              op0=ALU.bitwise_and, op1=ALU.bitwise_xor))
            for i in range(3):
                link(dve.tensor_tensor(Y[:, i], X[:, i], mn[:], ALU.bitwise_xor))
            spread(Y[:], sp[:])
            interleave(1)
            dve.tensor_copy(keep["keys"][:, :, :, :], kt[:].bitcast(F32)).then_inc(s_key, 1)
            dve.wait_ge(s_kt, 1)
            dve.tensor_copy(kr[:, :], ps_k[0:METHODS * B, :]).then_inc(s_kr, 1)
            dve.wait_ge(s_w, 16 * (4 + 2 + 4 + 8 + 2))
            for i in range(2):
                for part in range(2):
                    src = wl[i][:, part * P:(part + 1) * P].rearrange("e (h c m) -> e h m c", h=GH, m=METHODS)
                    last = dve.tensor_copy(wr[i][:, part], src)
                    if i == part == 1:
                        last.then_inc(s_wr, 1)
            dve.wait_ge(s_wp, 1)
            for i, o in enumerate(OUTC):
                for part in range(2):
                    at = (2 * i + part) * 64
                    hi, lo = keep["wc"][i][:, part, 0, :], keep["wc"][i][:, part, 1, :]
                    link(dve.tensor_scalar(out=wf[:, i, part, 0:o], in0=ps_w[:, at:at + o], scalar1=WSCALE, scalar2=None,
                                           op0=ALU.mult))
                    link(dve.tensor_copy(hi, wf[:, i, part, 0:o]))
                    link(dve.tensor_tensor(lo, wf[:, i, part, 0:o], hi, ALU.subtract))
                link(dve.tensor_copy(keep["bias"][i][:, :], ps_w[:, 256 + i:257 + i]))


def cross_attention(nc, a, keep, scratch, nb=B):
    with ExitStack() as ctx:
        m = Memory(nc, ctx)
        krow = m.sb("krow", [P, METHODS, N])
        kcol = m.sb("kcol", [P, NC, METHODS])
        cnt = m.sb("cnt", [P, 3, METHODS, NC])
        rank = m.sb("rank", [P, METHODS, NC])
        junk = m.sb("junk", [P, 3, N], BF16)
        perm = m.sb("perm", [P, METHODS, NC, N], BF16)
        ctr = [m.sb(f"ctr{l}", [P, NPAD]) for l in range(2)]
        ctr16 = [m.sb(f"ctr16_{l}", [P, NPAD], F16) for l in range(2)]
        ftf = m.sb("ftf", [P, NC, C])
        ftr = m.sb("ftr", [P, NC, C])
        ft3 = m.sb("ft3", [P, NC, 3, C], BF16)
        srt = m.sb("srt", [P, NC, GH, METHODS, 8])
        ext = m.sb("ext", [P, NPAD + 16])
        dif = m.sb("dif", [P, NBLK, 32], F16)
        dbd = m.sb("dbd", [P, NBLK, GH, 32], F16)
        e = m.sb("e", [P, 3, 512])
        pt = m.sb("pt", [P, 2, 512])
        ys = m.sb("ys", [P, 2, GB, 64])
        hs = m.sb("hs", [P, 2, 240])
        sq = m.sb("sq", [P, 240])
        mx = m.sb("mx", [P, 2, GB])
        zs = m.sb("zs", [P, 2, GB])
        hm = m.sb("hm", [P, 264])
        fo = m.sb("fo", [P, 264])
        f02 = m.sb("f02", [P, 264])
        sums = m.sb("sums", [P, 2, NG])
        s12 = m.sb("s12", [P, 2])
        st = m.sb("st", [P, 6])
        mhalf = m.sb("mhalf", [P, 1])
        xb = m.sb("xb", [C, N])
        h3 = m.sb("h3", [C, N])
        z02 = m.sb("z02", [C, N])
        bst = m.sb("bst", [C, 6])
        bmv = m.sb("bmv", [C, 2])
        ps_s = [m.ps(f"ps_s{i}") for i in range(2)]
        ps_y = [m.ps(f"ps_y{i}") for i in range(2)]
        ps_h = [m.ps(f"ps_h{i}") for i in range(2)]
        ps_a = m.ps("ps_a")
        ps_b = m.ps("ps_b")
        ps_p = [ps_s[0], ps_s[1], ps_h[0], ps_h[1]]

        names = ("krow_loaded", "center_loaded", "x_loaded_b", "ranks_done", "layer_input_used", "out_stored",
                 "input_transposed", "split_ready", "sorted_ready", "sums_ready", "sorted_t_ready", "ext_ready",
                 "dif_ready", "ctr16_ready", "scores_ready", "scores_used", "probs_exp", "y_ready", "y_used",
                 "ys_ready", "rz_ready", "probs_ready", "pt_ready", "h_ready", "h_used", "h_max_done", "tot_ready", "s12_ready",
                 "veps_ready", "rstd_ready", "fo_ready", "ctr2_in_psum", "ctr2_ready", "h3_ready", "h3_copied",
                 "out_ready", "zero_ready", "hs_stats_ready")
        S = {n: m.sem("b_" + n) for n in names}
        s_d = m.sem("cross_dve_step")
        s_a = m.sem("cross_act_step")
        s_g = m.sem("cross_pool_step")
        block = ctx.enter_context(nc.Block())
        SC = float(HD) ** -0.5

        def jblocks(l, g):
            cgs = P // OUTC[l]
            jc, jg = NBLK // cgs, GB // cgs
            return [(cg, jj, cg * jc + g * jg + jj) for cg in range(cgs) for jj in range(jg)]

        @block.sync
        def _(sp):
            def load(b):
                src = scratch["keys"][:, b, :]
                sp.dma_start(krow[:, :, :], bass.AP(src.tensor, src.offset, [[0, P]] + [list(k) for k in src.ap])).then_inc(S["krow_loaded"], 16)

            def load_center(b):
                for h in range(GH):
                    src = scratch["feats"].rearrange("(b h c) n -> b h c n", h=GH, c=8)[b, h]
                    sp.dma_start(ctr[0][32 * h:32 * h + 32, 0:N],
                                 bass.AP(src.tensor, src.offset, [[0, METHODS]] + [list(k) for k in src.ap])).then_inc(S["center_loaded"], 16)
                sp.dma_start(xb[:, :], a["x"][b]).then_inc(S["x_loaded_b"], 16)

            with sp.Fori(0, nb) as b:
                sp.wait_ge(S["ranks_done"], b + 1)
                load(b)
                sp.wait_ge(S["out_ready"], b + 1)
                load_center(b)
                sp.wait_ge(S["out_ready"], b + 2)
                sp.dma_start(scratch["x1"].rearrange("(b c) n -> b c n", c=C)[b], h3[:, :]).then_inc(S["out_stored"], 16)
            sp.wait_ge(S["out_stored"], 16 * nb)

        @block.gpsimd
        def _(pool):
            link = Chain(pool, s_g)
            link(pool.memset(mhalf[:, :], -0.5))
            for l in range(2):
                pool.memset(ctr[l][:, N:NPAD], 0.0)
                pool.memset(ctr16[l][:, N:NPAD], 0.0)
            pool.memset(ext[:, :], 0.0)
            pool.memset(dif[:, :, :], 0.0)
            pool.memset(dbd[:, :, :, :], 0.0).then_inc(S["zero_ready"], 1)
            with pool.Fori(0, nb) as b:
                for l in range(2):
                    for g in range(NG):
                        s = l * NG + g
                        pool.wait_ge(S["rz_ready"], 2 * NG * b + s + 1)
                        ev = e[:, g % 3, :].rearrange("p (u c) -> p u c", u=GB)
                        pool.tensor_tensor(ev, ev, zs[:, g % 2, :].unsqueeze(2).to_broadcast([P, GB, 32]), ALU.mult).then_inc(S["probs_ready"], 1)
                    pool.wait_ge(S["veps_ready"], 3 * b + l + 1)
                    pool.tensor_tensor(st[:, 4:5], st[:, 3:4], mhalf[:, :], ALU.pow).then_inc(S["rstd_ready"], 1)
                pool.wait_ge(S["veps_ready"], 3 * b + 3)
                pool.tensor_tensor(st[0:C, 4:5], st[0:C, 3:4], mhalf[0:C, :], ALU.pow).then_inc(S["rstd_ready"], 1)

        @block.scalar
        def _(act):
            with act.Fori(0, nb) as b:
                for l in range(2):
                    O = OUTC[l]
                    cgs = P // O
                    jg = GB // cgs
                    if l == 0:
                        act.wait_ge(S["center_loaded"], 64 * b + 64)
                    else:
                        act.wait_ge(S["ctr2_ready"], b + 1)
                    act.activation(ctr16[l][:, 0:N], ctr[l][:, 0:N], ACT.Copy).then_inc(S["ctr16_ready"], 1)
                    act.wait_ge(S["sorted_t_ready"], 2 * b + l + 1)
                    act.activation(ext[:, 5:5 + N], ps_b[:, :], ACT.Copy).then_inc(S["ext_ready"], 1)

                    def h_out(g):
                        s = l * NG + g
                        act.wait_ge(S["h_ready"], 2 * NG * b + s + 1)
                        act.wait_ge(S["h_max_done"], 2 * NG * b + s + 1)
                        act.activation(hs[:, g % 2, 0:jg * PB * K], ps_h[g % 2][:, 0:jg * PB * K], ACT.Identity,
                                       accum_out=sums[:, 0, g:g + 1]).then_inc(S["h_used"], 1)
                        act.wait_ge(S["h_used"], 2 * NG * b + s + 3)
                        act.activation(sq[:, 0:jg * PB * K], hs[:, g % 2, 0:jg * PB * K], ACT.Square,
                                       accum_out=sums[:, 1, g:g + 1]).then_inc(S["hs_stats_ready"], 1)

                    for g in range(NG):
                        s = l * NG + g
                        act.wait_ge(S["scores_used"], 2 * NG * b + s + 3)
                        ev = e[:, g % 3, :]
                        act.activation(ev, ev, ACT.Exp, scale=SC).then_inc(S["probs_exp"], 1)
                        units = 1 if l == 0 else 2
                        for u in range(units):
                            n = g if l == 0 else NG + 2 * g + u
                            act.wait_ge(S["y_ready"], 3 * NG * b + n + 1)
                            if u == 0 and g >= 2:
                                act.wait_ge(S["h_ready"], 2 * NG * b + s - 1)
                            k = GB // units
                            act.activation(ys[:, g % 2, u * k:(u + 1) * k, 0:O],
                                           ps_y[n % 2][:, :].rearrange("p (u o) -> p u o", u=k), ACT.Copy).then_inc(S["y_used"], 1)
                        if g >= 3:
                            h_out(g - 3)
                    for g in range(NG - 3, NG):
                        h_out(g)
                act.wait_ge(S["h3_ready"], b + 1)
                act.activation(h3[:, :], ps_a[0:C, :], ACT.Copy).then_inc(S["h3_copied"], 1)

        @block.tensor
        def _(pe):
            ident = keep["ident"]
            pe.wait_ge(S["zero_ready"], 1)
            with pe.Fori(0, nb) as b:
                for l in range(2):
                    O = OUTC[l]
                    cgs = P // O
                    jg = GB // cgs
                    jp = jg * PB
                    if l == 0:
                        pe.wait_ge(S["center_loaded"], 64 * b + 64)
                    else:
                        pe.wait_ge(S["ctr2_ready"], b + 1)
                    for j in range(NC):
                        last = pe.transpose(ps_a[:, j * P:(j + 1) * P], ctr[l][:, j * P:(j + 1) * P], ident[:, :])
                    last.then_inc(S["input_transposed"], 1)
                    pe.wait_ge(S["split_ready"], 2 * b + l + 1)
                    for rc in range(NC):
                        for p in range(METHODS):
                            for j in range(NC):
                                last = pe.matmul(ps_p[rc][:, 96 * p:96 * p + 96], perm[:, PERM[l][p], j, rc * P:(rc + 1) * P],
                                                 ft3[:, j].rearrange("p a c -> p (a c)"), start=j == 0, stop=j == NC - 1)
                        last.then_inc(S["sorted_ready"], 1)
                    for rc in range(NC):
                        pe.wait_ge(S["sums_ready"], 2 * NC * b + NC * l + rc + 1)
                        last = pe.transpose(ps_b[:, rc * P:(rc + 1) * P], srt[:, rc].rearrange("p h m c -> p (h m c)"), ident[:, :])
                    last.then_inc(S["sorted_t_ready"], 1)

                    def pv(g):
                        s = l * NG + g
                        pe.wait_ge(S["pt_ready"], 2 * NG * b + s + 1)
                        pe.wait_ge(S["y_used"], 3 * NG * b + (g + 1 if l == 0 else NG + 2 * g + 2) + 2)
                        pe.wait_ge(S["h_used"], 2 * NG * b + s + 1)
                        hb = ps_h[g % 2]
                        for cg in range(cgs):
                            pts = (cg * (NBLK // cgs) + g * jg) * PB
                            rows = slice(cg * O, cg * O + O)
                            mv = ctr16[l][:, pts:pts + jp].unsqueeze(2).to_broadcast([P, jp, K])
                            ov = hb[rows, 0:jp * K].rearrange("p (i k) -> p i k", k=K)
                            pe.matmul(ov, keep["wc"][l][:, 0, 0, :], mv, start=True, stop=False, skip_group_check=True)
                            pe.matmul(ov, keep["wc"][l][:, 0, 1, :], mv, start=False, stop=False, skip_group_check=True)
                            for jj in range(jg):
                                u = cg * jg + jj
                                last = pe.matmul(hb[rows, jj * 30:jj * 30 + 30], ys[:, g % 2, u, 0:O], pt[:, g % 2, u * 32:u * 32 + 30],
                                                 start=False, stop=jj == jg - 1, skip_group_check=True)
                        last.then_inc(S["h_ready"], 1)

                    pe.wait_ge(S["dif_ready"], 2 * b + l + 1)
                    pe.wait_ge(S["ctr16_ready"], 2 * b + l + 1)
                    for g in range(NG):
                        s = l * NG + g
                        pe.wait_ge(S["scores_used"], 2 * NG * b + s + 1)
                        sb_ = ps_s[g % 2]
                        pe.matmul(sb_[:, :], keep["ind"][:, :], keep["off"][:, :], start=True, stop=False, skip_group_check=True)
                        for u, (cg, jj, j) in enumerate(jblocks(l, g)):
                            bd = dbd[:, j].rearrange("p h c -> p (h c)")
                            last_s = pe.matmul(sb_[:, u * 32:u * 32 + 32], bd, dif[:, j, :], start=False, stop=u == GB - 1, skip_group_check=True)
                            n = g if l == 0 else NG + 2 * g + u // 8
                            k = GB if l == 0 else 8
                            if u % k == 0:
                                pe.wait_ge(S["y_used"], 3 * NG * b + n + 1)
                            yo = ps_y[n % 2][:, (u % k) * O:(u % k) * O + O]
                            pe.matmul(yo, bd, keep["wc"][l][:, 1, 0, :], start=True, stop=False)
                            last = pe.matmul(yo, bd, keep["wc"][l][:, 1, 1, :], start=False, stop=True)
                            if u % k == k - 1:
                                last.then_inc(S["y_ready"], 1)
                            if u == GB - 1:
                                last_s.then_inc(S["scores_ready"], 1)
                        if g >= 2:
                            pv(g - 2)
                    pv(NG - 2)
                    pv(NG - 1)
                    pe.wait_ge(S["s12_ready"], 2 * b + l + 1)
                    pe.matmul(ps_a[:, 0:2], keep["same"][l][:, :], s12[:, :], start=True, stop=True).then_inc(S["tot_ready"], 1)
                    pe.wait_ge(S["fo_ready"], 2 * b + l + 1)
                    if l == 0:
                        for cg in range(4):
                            at = cg * (NPAD // 4)
                            w = min(NPAD // 4, N - at)
                            last = pe.matmul(ps_b[:, at:at + w], keep["gather"][:, cg, :], fo[:, 0:w], start=True, stop=True)
                        last.then_inc(S["ctr2_in_psum"], 1)
                    else:
                        for i in range(2):
                            pe.matmul(ps_a[0:C, :], keep["w3"][:, i, :], ctr[i][:, 0:N], start=i == 0, stop=False, skip_group_check=True)
                        for r in range(2):
                            at = r * (NPAD // 2)
                            w = min(NPAD // 2, N - at)
                            last = pe.matmul(ps_a[0:C, at:at + w], keep["w3"][:, 2 + r, :], fo[:, 0:w], start=False, stop=r == 1, skip_group_check=True)
                        last.then_inc(S["h3_ready"], 1)

        @block.vector
        def _(dve):
            dve.sem_inc(S["scores_used"], 2)
            dve.sem_inc(S["y_used"], 2)
            dve.sem_inc(S["h_used"], 2)
            dve.sem_inc(S["h_max_done"], 2)
            dve.sem_inc(S["ranks_done"], 1)
            dve.sem_inc(S["out_ready"], 1)
            dve.wait_ge(S["zero_ready"], 1)
            with dve.Fori(0, nb) as b:
                dve.sem_clear(s_d)
                link = Chain(dve, s_d)
                dve.wait_ge(S["krow_loaded"], 16 * b + 16)
                link(dve.tensor_copy(kcol[:, :, :], keep["keys"][:, :, :, bass.ds(b, 1)].rearrange("p j m b -> p j (m b)")))
                for j in range(NC):
                    for c in range(METHODS):
                        key = kcol[:, j, c:c + 1]
                        if j:
                            dve.tensor_scalar(out=junk[:, 0, 0:j * P], in0=krow[:, c, 0:j * P], scalar1=key, scalar2=None, op0=ALU.is_le,
                                              op1=ALU.add, accum_out=cnt[:, 0, c, j:j + 1])
                        dve.tensor_scalar(out=junk[:, 1, j * P:N], in0=krow[:, c, j * P:N], scalar1=key, scalar2=None, op0=ALU.is_lt,
                                          op1=ALU.add, accum_out=cnt[:, 1, c, j:j + 1])
                        link(dve.scalar_tensor_tensor(out=junk[:, 2, 0:P], in0=krow[:, c, j * P:(j + 1) * P], scalar=key,
                                                      in1=keep["tri"][:, :], op0=ALU.is_equal, op1=ALU.mult,
                                                      accum_out=cnt[:, 2, c, j:j + 1]))
                link(dve.tensor_tensor(rank[:, :, :], cnt[:, 1], cnt[:, 2], ALU.add))
                dve.tensor_tensor(rank[:, :, 1:NC], rank[:, :, 1:NC], cnt[:, 0, :, 1:NC], ALU.add).then_inc(S["ranks_done"], 1)
                dve.wait_ge(S["ranks_done"], b + 2)
                for c in range(METHODS):
                    for j in range(NC):
                        last = dve.tensor_scalar(out=perm[:, c, j, :], in0=keep["iota"][:, :], scalar1=rank[:, c, j:j + 1],
                                                 scalar2=None, op0=ALU.is_equal)
                link(last)
                for l in range(2):
                    O = OUTC[l]
                    cgs = P // O
                    jg = GB // cgs
                    npt = NPAD // cgs
                    dve.wait_ge(S["input_transposed"], 2 * b + l + 1)
                    src = ps_a[:, :].rearrange("p (j h m c) -> p j h m c", j=NC, h=GH, m=METHODS)[:, :, :, 0, :]
                    link(dve.tensor_copy(ftf[:, :, :].rearrange("p j (h c) -> p j h c", h=GH), src))
                    link(dve.tensor_copy(ft3[:, :, 0, :], ftf[:, :, :]))
                    link(dve.tensor_tensor(ftr[:, :, :], ftf[:, :, :], ft3[:, :, 0, :], ALU.subtract))
                    link(dve.tensor_copy(ft3[:, :, 1, :], ftr[:, :, :]))
                    link(dve.tensor_tensor(ftr[:, :, :], ftr[:, :, :], ft3[:, :, 1, :], ALU.subtract))
                    dve.tensor_copy(ft3[:, :, 2, :], ftr[:, :, :]).then_inc(S["split_ready"], 1)
                    for rc in range(NC):
                        dve.wait_ge(S["sorted_ready"], 2 * NC * b + NC * l + rc + 1)
                        for p in range(METHODS):
                            src = ps_p[rc][:, 96 * p:96 * p + 96].rearrange("p (a h c) -> p h c a", a=3, h=GH)
                            last = dve.tensor_reduce(out=srt[:, rc, :, p, :], in_=src, axis=AX.X, op=ALU.add)
                        last.then_inc(S["sums_ready"], 1)
                    dve.wait_ge(S["ext_ready"], 2 * b + l + 1)
                    link(dve.tensor_copy(ext[:, 5 + N:10 + N], ext[:, 4 + N:5 + N].to_broadcast([P, 5])))
                    c3 = ctr[l][:, :].rearrange("p (j i) -> p j i", i=PB)
                    d4 = dif[:, :, 0:30].rearrange("p j (i k) -> p j i k", i=PB)
                    full, rest = N // PB, N % PB
                    link(dve.tensor_tensor(d4[:, 0:full], window(ext, 0, [[3, full], [1, PB], [1, K]]),
                                           c3[:, 0:full].unsqueeze(3).to_broadcast([P, full, PB, K]), ALU.subtract))
                    link(dve.tensor_tensor(d4[:, full, 0:rest], window(ext, full * PB, [[1, rest], [1, K]]),
                                           c3[:, full, 0:rest].unsqueeze(2).to_broadcast([P, rest, K]), ALU.subtract))
                    for j, n in ((0, 3), (1, 2)):
                        link(dve.tensor_tensor(d4[:, j, 0:n], window(ext, 5, [[0, n], [1, K]]),
                                               c3[:, j, 0:n].unsqueeze(2).to_broadcast([P, n, K]), ALU.subtract))
                    for i in range(4):
                        w = K - 6 - i
                        link(dve.tensor_tensor(d4[:, i // PB, i % PB, 6 + i:K], ext[:, 10 + i:11 + i].to_broadcast([P, w]),
                                               ctr[l][:, i:i + 1].to_broadcast([P, w]), ALU.subtract))
                    for h in range(GH):
                        rows = slice(32 * h, 32 * h + 32)
                        last = dve.tensor_copy(dbd[rows, :, h, :], dif[rows, :, :])
                    last.then_inc(S["dif_ready"], 1)

                    def z_sum(g):
                        s = l * NG + g
                        dve.wait_ge(S["probs_exp"], 2 * NG * b + s + 1)
                        link(dve.tensor_reduce(out=zs[:, g % 2, :], in_=e[:, g % 3, :].rearrange("p (u c) -> p u c", u=GB),
                                               axis=AX.X, op=ALU.add))
                        dve.reciprocal(zs[:, g % 2, :], zs[:, g % 2, :]).then_inc(S["rz_ready"], 1)

                    def flip(g):
                        s = l * NG + g
                        dve.wait_ge(S["probs_ready"], 2 * NG * b + s + 1)
                        if g >= 2:
                            dve.wait_ge(S["h_ready"], 2 * NG * b + s - 1)
                        dve.transpose(pt[:, g % 2, :], e[:, g % 3, :]).then_inc(S["pt_ready"], 1)

                    def h_max(g):
                        s = l * NG + g
                        dve.wait_ge(S["h_used"], 2 * NG * b + s + 3)
                        jp = jg * PB
                        dve.tensor_reduce(out=hm[:, g * jp:(g + 1) * jp], in_=hs[:, g % 2, 0:jp * K].rearrange("p (i k) -> p i k", k=K),
                                          axis=AX.X, op=ALU.max).then_inc(S["h_max_done"], 1)

                    for g in range(NG + 4):
                        if g < NG:
                            s = l * NG + g
                            dve.wait_ge(S["scores_ready"], 2 * NG * b + s + 1)
                            sv = ps_s[g % 2][:, :].rearrange("p (u c) -> p u c", u=GB)
                            link(dve.tensor_reduce(out=mx[:, g % 2, :], in_=sv, axis=AX.X, op=ALU.max))
                            dve.tensor_tensor(e[:, g % 3, :].rearrange("p (u c) -> p u c", u=GB), sv,
                                              mx[:, g % 2, :].unsqueeze(2).to_broadcast([P, GB, 32]), ALU.subtract).then_inc(S["scores_used"], 1)
                        if 1 <= g <= NG:
                            z_sum(g - 1)
                        if 2 <= g <= NG + 1:
                            flip(g - 2)
                        if g >= 4:
                            h_max(g - 4)
                    dve.wait_ge(S["hs_stats_ready"], 2 * NG * b + (l + 1) * NG)
                    dve.tensor_reduce(out=s12[:, :], in_=sums[:, :, :], axis=AX.X, op=ALU.add).then_inc(S["s12_ready"], 1)
                    dve.wait_ge(S["tot_ready"], 2 * b + l + 1)
                    cntk = float(N * K)
                    link(dve.tensor_scalar(out=st[:, 0:1], in0=ps_a[:, 0:1], scalar1=1.0 / (cntk * WSCALE), scalar2=None, op0=ALU.mult))
                    link(dve.tensor_scalar(out=st[:, 1:2], in0=ps_a[:, 1:2], scalar1=1.0 / (cntk * WSCALE * WSCALE), scalar2=LN_EPS,
                                           op0=ALU.mult, op1=ALU.add))
                    link(dve.tensor_tensor(st[:, 2:3], st[:, 0:1], st[:, 0:1], ALU.mult))
                    dve.tensor_tensor(st[:, 3:4], st[:, 1:2], st[:, 2:3], ALU.subtract).then_inc(S["veps_ready"], 1)
                    link(dve.tensor_tensor(st[:, 0:1], st[:, 0:1], keep["bias"][l][:, :], ALU.add))
                    link(dve.tensor_scalar(out=hm[:, 0:npt], in0=hm[:, 0:npt], scalar1=1.0 / WSCALE, scalar2=keep["bias"][l][:, 0:1],
                                           op0=ALU.mult, op1=ALU.add))
                    dve.wait_ge(S["rstd_ready"], 3 * b + l + 1)
                    link(dve.tensor_scalar(out=hm[:, 0:npt], in0=hm[:, 0:npt], scalar1=st[:, 0:1], scalar2=st[:, 4:5],
                                           op0=ALU.subtract, op1=ALU.mult))
                    link(dve.tensor_scalar(out=f02[:, 0:npt], in0=hm[:, 0:npt], scalar1=0.2, scalar2=None, op0=ALU.mult))
                    dve.tensor_tensor(fo[:, 0:npt], hm[:, 0:npt], f02[:, 0:npt], ALU.max).then_inc(S["fo_ready"], 1)
                    if l == 0:
                        dve.wait_ge(S["ctr2_in_psum"], b + 1)
                        dve.tensor_copy(ctr[1][:, 0:N], ps_b[:, :]).then_inc(S["ctr2_ready"], 1)
                        dve.wait_ge(S["ctr2_ready"], b + 1)
                dve.wait_ge(S["h3_copied"], b + 1)
                link(dve.bn_stats(out=bst[:, :], in_=h3[:, :]))
                link(dve.bn_aggr(out=bmv[:, :], in_=bst[:, :]))
                dve.tensor_scalar(out=st[0:C, 3:4], in0=bmv[:, 1:2], scalar1=LN_EPS, scalar2=None, op0=ALU.add).then_inc(S["veps_ready"], 1)
                dve.wait_ge(S["rstd_ready"], 3 * b + 3)
                link(dve.tensor_scalar(out=h3[:, :], in0=h3[:, :], scalar1=bmv[:, 0:1], scalar2=st[0:C, 4:5], op0=ALU.subtract, op1=ALU.mult))
                link(dve.tensor_scalar(out=z02[:, :], in0=h3[:, :], scalar1=0.2, scalar2=None, op0=ALU.mult))
                link(dve.tensor_tensor(h3[:, :], h3[:, :], z02[:, :], ALU.max))
                dve.wait_ge(S["x_loaded_b"], 16 * b + 16)
                dve.tensor_tensor(h3[:, :], h3[:, :], xb[:, :], ALU.add).then_inc(S["out_ready"], 1)
                dve.wait_ge(S["out_ready"], b + 2)
                dve.wait_ge(S["out_stored"], 16 * b + 16)


def constants(nc, ctx):
    m = Memory(nc, ctx)
    return {
        "ident": m.sb("ident", [P, P]),
        "iota": m.sb("iota", [P, N], F16),
        "tri": m.sb("tri", [P, P]),
        "ind": m.sb("ind", [P, P], BF16),
        "off": m.sb("off", [P, 512], BF16),
        "same": [m.sb(f"same{l}", [P, P]) for l in range(2)],
        "gather": m.sb("gather", [P, 4, P]),
        "w3": m.sb("w3", [P, 4, C]),
        "keys": m.sb("keycols", [P, NC, METHODS, B]),
        "wc": [m.sb(f"wc{l}", [P, 2, 2, OUTC[l]], F16) for l in range(2)],
        "bias": [m.sb(f"bias{l}", [P, 1]) for l in range(2)],
    }


def layernorm_transposed(dve, pool_hook, link, src, mv, stats, veps, rstd_ready, rstd, dst, var_ready):
    for t in range(NT):
        link(dve.bn_stats(out=stats[:, t, :], in_=src[:, t, :]))
        link(dve.bn_aggr(out=mv[:, t, :], in_=stats[:, t, :]))
        dve.tensor_scalar(out=veps[:, t:t + 1], in0=mv[:, t, 1:2], scalar1=LN_EPS, scalar2=None,
                          op0=ALU.add).then_inc(var_ready, 1)
    for t in range(NT):
        dve.wait_ge(rstd_ready, t + 1)
        dve.tensor_scalar(out=dst[:, t, :], in0=src[:, t, :], scalar1=mv[:, t, 0:1], scalar2=rstd[:, t:t + 1],
                          op0=ALU.subtract, op1=ALU.mult).then_inc(pool_hook, 1)


def self_attention(nc, a, keep, scratch):
    H, DN, DQ, DV = 32, 128, 192, 128
    HS = 4
    PAIRS = H // HS // 2
    HC = HS * DN
    SCALE = float(DQ) ** -0.5
    with ExitStack() as ctx:
        m = Memory(nc, ctx)
        hn = m.sb("a_hn", [P, NT, N])
        hT = m.sb("a_hT", [P, NC, TOK])
        stats = m.sb("a_stats", [P, NT, 6])
        mv = m.sb("a_mv", [P, NT, 2])
        veps = m.sb("a_veps", [P, NT])
        rstd = m.sb("a_rstd", [P, NT])
        mhalf = m.sb("a_mhalf", [P, NT])
        wq = m.sb("a_wq", [P, 2, NC, HS, DN])
        wk = m.sb("a_wk", [P, 2, NC, HC])
        wv = m.sb("a_wv", [P, 2, NC, HC])
        wo = m.sb("a_wo", [P, 2, HS, N])
        qT = m.sb("a_qT", [P, HS, TOK])
        kT = m.sb("a_kT", [P, HS, TOK])
        v = m.sb("a_v", [P, NT, HC])
        sc = m.sb("a_sc", [P, HS * NT, C])
        mx = m.sb("a_mx", [P, HS * NT])
        zs = m.sb("a_zs", [P, HS * NT])
        pbd = m.sb("a_pbd", [P, HS, NT, P])
        oT = m.sb("a_oT", [P, HS, TOK])
        causal = m.sb("a_causal", [P, C])
        x1, x2 = keep["x1"], keep["x2"]
        ps_out = [m.ps(f"a_out{t}") for t in range(NT)]
        ps_w = [m.ps(f"a_proj{i}") for i in range(2)]
        ps_s = m.ps("a_scores")
        ps_o = m.ps("a_heads")

        S = {n: m.sem("a_" + n) for n in (
            "x_loaded", "var_ready", "rstd_ready", "hn_ready", "hT_in_psum", "hT_ready", "causal_ready", "w_loaded_even",
            "w_loaded_odd", "w_used", "proj_ready", "proj_copied", "scores_ready", "scores_used", "shifted", "exp_ready", "pt_ready",
            "heads_ready", "heads_copied", "out_ready", "zero_ready")}
        loaded = (S["w_loaded_even"], S["w_loaded_odd"])
        s_d, s_g = m.sem("self_dve_step"), m.sem("self_pool_step")
        block = ctx.enter_context(nc.Block())
        NP_ = 2 * HS + NT

        @block.sync
        def _(sp):
            for t in range(NT):
                sp.dma_start(x1[:, t, :], scratch["x1"][t * P:(t + 1) * P, :]).then_inc(S["x_loaded"], 16)
            wq_d = a["L0_attn_wq"].rearrange("(k p) (s h d) -> s p k h d", p=P, h=HS, d=DQ)
            wk_d = a["L0_attn_wkv"][:, 0:H * DN].rearrange("(k p) (s d) -> s p k d", p=P, d=HC)
            wv_d = a["L0_attn_wkv"][:, H * DN:H * (DN + DV)].rearrange("(k p) (s d) -> s p k d", p=P, d=HC)
            wo_d = a["L0_attn_wo"].rearrange("(s h p) n -> s p h n", p=P, h=HS)
            with sp.Fori(0, PAIRS) as i:
                for r in range(2):
                    sp.wait_ge(S["w_used"], 2 * i + r + 1)
                    for k in range(NC):
                        sp.dma_start(wq[:, r, k], wq_d[2 * i + r][:, k, :, 0:DN]).then_inc(loaded[r], 16)
                    sp.dma_start(wk[:, r], wk_d[2 * i + r]).then_inc(loaded[r], 16)
                    sp.dma_start(wv[:, r], wv_d[2 * i + r]).then_inc(loaded[r], 16)
                    sp.dma_start(wo[:, r], wo_d[2 * i + r]).then_inc(loaded[r], 16)

        @block.gpsimd
        def _(pool):
            link = Chain(pool, s_g)
            link(pool.memset(mhalf[:, :], -0.5))
            link(pool.memset(causal[:, :], 0.0))
            for r in range(P // C):
                last = pool.affine_select(out=causal[r * C:(r + 1) * C, :], in_=causal[r * C:(r + 1) * C, :], compare_op=ALU.is_ge,
                                          fill=NEG, base=0, pattern=[[-1, C]], channel_multiplier=1)
            last.then_inc(S["causal_ready"], 1)
            pool.wait_ge(S["causal_ready"], 1)
            pool.memset(pbd[:, :, :, :], 0.0).then_inc(S["zero_ready"], 1)
            for t in range(NT):
                pool.wait_ge(S["var_ready"], t + 1)
                pool.tensor_tensor(rstd[:, t:t + 1], veps[:, t:t + 1], mhalf[:, t:t + 1], ALU.pow).then_inc(S["rstd_ready"], 1)

        @block.tensor
        def _(pe):
            for k in range(NC):
                for t in range(NT):
                    pe.wait_ge(S["hn_ready"], t + 1)
                    last = pe.transpose(ps_out[k][:, t * P:(t + 1) * P], hn[:, t, k * P:(k + 1) * P], keep["ident"][:, :])
                last.then_inc(S["hT_in_psum"], 1)
            pe.wait_ge(S["hT_ready"], NC)
            for t in range(NT):
                pe.matmul(ps_out[t][:, :], keep["ident"][:, :], x1[:, t, :], start=True, stop=False, skip_group_check=True)
            with pe.Fori(0, PAIRS) as i:
                for r in range(2):
                    pe.wait_ge(loaded[r], 7 * 16 * i + 7 * 16)
                    for w in range(2 * HS):
                        h = w % HS
                        pe.wait_ge(S["proj_copied"], NP_ * (2 * i + r) + w + 1)
                        for k in range(NC):
                            lhs = wq[:, r, k, h, :] if w < HS else wk[:, r, k, h * DN:(h + 1) * DN]
                            last = pe.matmul(ps_w[w % 2][:, :], lhs, hT[:, k, :], start=k == 0, stop=k == NC - 1)
                        last.then_inc(S["proj_ready"], 1)
                    pe.wait_ge(S["proj_copied"], NP_ * (2 * i + r) + 2 * HS + 2)
                    pe.wait_ge(S["scores_used"], 2 * i + r + 1)
                    for h in range(HS):
                        for t in range(NT):
                            for q in range(P // C):
                                tok = slice(t * P + q * C, t * P + q * C + C)
                                at = (h * NT + t) * C
                                last = pe.matmul(ps_s[q * C:(q + 1) * C, at:at + C], qT[:, h, tok], kT[:, h, tok], start=True, stop=True)
                    last.then_inc(S["scores_ready"], 1)
                    for t in range(NT):
                        w = 2 * HS + t
                        pe.wait_ge(S["proj_copied"], NP_ * (2 * i + r) + w + 1)
                        for k in range(NC):
                            last = pe.matmul(ps_w[w % 2][:, :], hT[:, k, t * P:(t + 1) * P], wv[:, r, k, :], start=k == 0, stop=k == NC - 1)
                        last.then_inc(S["proj_ready"], 1)
                    pe.wait_ge(S["pt_ready"], 2 * i + r + 1)
                    pe.wait_ge(S["proj_copied"], NP_ * (2 * i + r) + NP_ + 2)
                    for h in range(HS):
                        pe.wait_ge(S["heads_copied"], HS * (2 * i + r) + h + 1)
                        for t in range(NT):
                            last = pe.matmul(ps_o[:, t * P:(t + 1) * P], v[:, t, h * DV:(h + 1) * DV], pbd[:, h, t, :], start=True, stop=True)
                        last.then_inc(S["heads_ready"], 1)
                    pe.wait_ge(S["heads_copied"], HS * (2 * i + r) + HS + 1)
                    for t in range(NT):
                        for h in range(HS):
                            last = pe.matmul(ps_out[t][:, :], oT[:, h, t * P:(t + 1) * P], wo[:, r, h, :], start=False, stop=False,
                                             skip_group_check=True)
                    last.then_inc(S["w_used"], 1)

        @block.scalar
        def _(act):
            with act.Fori(0, PAIRS) as i:
                for r in range(2):
                    def copy(w):
                        act.wait_ge(S["proj_ready"], NP_ * (2 * i + r) + w + 1)
                        dst = qT[:, w, :] if w < HS else kT[:, w - HS, :] if w < 2 * HS else v[:, w - 2 * HS, :]
                        act.activation(dst, ps_w[w % 2][:, :], ACT.Copy).then_inc(S["proj_copied"], 1)

                    for w in range(2 * HS):
                        copy(w)
                    act.wait_ge(S["shifted"], 2 * i + r + 1)
                    act.activation(sc[:, :, :], sc[:, :, :], ACT.Exp, scale=SCALE).then_inc(S["exp_ready"], 1)
                    for t in range(NT):
                        copy(2 * HS + t)
                    for h in range(HS):
                        act.wait_ge(S["heads_ready"], HS * (2 * i + r) + h + 1)
                        act.activation(oT[:, h, :], ps_o[:, :], ACT.Copy).then_inc(S["heads_copied"], 1)

        @block.vector
        def _(dve):
            dve.sem_inc(S["w_used"], 2)
            dve.sem_inc(S["proj_copied"], 2)
            dve.sem_inc(S["scores_used"], 1)
            dve.sem_inc(S["heads_copied"], 1)
            link = Chain(dve, s_d)
            dve.wait_ge(S["x_loaded"], 16 * NT)
            layernorm_transposed(dve, S["hn_ready"], link, x1, mv, stats, veps, S["rstd_ready"], rstd, hn, S["var_ready"])
            for k in range(NC):
                dve.wait_ge(S["hT_in_psum"], k + 1)
                dve.tensor_copy(hT[:, k, :], ps_out[k][:, :]).then_inc(S["hT_ready"], 1)
            dve.wait_ge(S["causal_ready"], 1)
            dve.wait_ge(S["zero_ready"], 1)
            G = HS * NT
            with dve.Fori(0, PAIRS) as i:
                dve.sem_clear(s_d)
                link = Chain(dve, s_d)
                for r in range(2):
                    dve.wait_ge(S["scores_ready"], 2 * i + r + 1)
                    sv = ps_s[:, :].rearrange("p (g c) -> p g c", g=G)
                    dve.tensor_tensor(sc[:, :, :], sv, causal[:, :].unsqueeze(1).to_broadcast([P, G, C]), ALU.add).then_inc(S["scores_used"], 1)
                    dve.wait_ge(S["scores_used"], 2 * i + r + 2)
                    link(dve.tensor_reduce(out=mx[:, :], in_=sc[:, :, :], axis=AX.X, op=ALU.max))
                    dve.tensor_tensor(sc[:, :, :], sc[:, :, :], mx[:, :].unsqueeze(2).to_broadcast([P, G, C]), ALU.subtract).then_inc(S["shifted"], 1)
                    dve.wait_ge(S["exp_ready"], 2 * i + r + 1)
                    link(dve.tensor_reduce(out=zs[:, :], in_=sc[:, :, :], axis=AX.X, op=ALU.add))
                    link(dve.reciprocal(zs[:, :], zs[:, :]))
                    link(dve.tensor_tensor(sc[:, :, :], sc[:, :, :], zs[:, :].unsqueeze(2).to_broadcast([P, G, C]), ALU.mult))
                    for q in range(P // C):
                        rows = slice(q * C, (q + 1) * C)
                        last = dve.transpose(pbd[rows, :, :, q * C:(q + 1) * C].rearrange("p h t c -> p (h t) c"), sc[rows, :, :])
                    last.then_inc(S["pt_ready"], 1)
            dve.wait_ge(S["w_used"], 2 * PAIRS + 2)
            for t in range(NT):
                last = dve.tensor_copy(x2[:, t, :], ps_out[t][:, :])
            last.then_inc(S["out_ready"], 1)
            dve.wait_ge(S["out_ready"], 1)


def experts(nc, a, keep, scratch, out):
    E, GROUPS, INTER = 16, 4, 128
    with ExitStack() as ctx:
        m = Memory(nc, ctx)
        hn = m.sb("e_hn", [P, NT, N])
        hT = m.sb("e_hT", [P, NC, TOK])
        stats = m.sb("e_stats", [P, NT, 6])
        mv = m.sb("e_mv", [P, NT, 2])
        veps = m.sb("e_veps", [P, NT])
        rstd = m.sb("e_rstd", [P, NT])
        mhalf = m.sb("e_mhalf", [P, NT])
        rw = m.sb("e_rw", [P, NC, E])
        rb = m.sb("e_rb", [P, E])
        rbias = m.sb("e_rbias", [P, E])
        lg = m.sb("e_lg", [P, NT, E])
        gmax = m.sb("e_gmax", [P, NT, GROUPS])
        first = m.sb("e_first", [P, E])
        cand = m.sb("e_cand", [P, NT, E])
        pick = m.sb("e_pick", [P, NT, E])
        both = m.sb("e_both", [P, NT, E])
        gkeep = m.sb("e_gkeep", [P, NT, GROUPS])
        left = m.sb("e_left", [P, NT, E])
        t1 = m.sb("e_t1", [P, NT])
        t2 = m.sb("e_t2", [P, NT])
        gate = m.sb("e_gate", [P, NT, E + 1])
        gateT = m.sb("e_gateT", [E + 1, TOK])
        b3 = m.sb("e_b3", [E + 1, N])
        w1 = m.sb("e_w1", [P, 2, NC, INTER])
        w2 = m.sb("e_w2", [P, 2, NC, INTER])
        w3 = m.sb("e_w3", [P, 2, N])
        b1 = m.sb("e_b1", [P, 2, 1])
        b2 = m.sb("e_b2", [P, 2, 1])
        gb = m.sb("e_gb", [P, 2, TOK])
        up = m.sb("e_up", [P, 2, TOK])
        hh = m.sb("e_hh", [P, 2, TOK])
        y = m.sb("e_y", [P, NT, N])
        x2 = keep["x2"]
        ps_y = [m.ps(f"e_y{t}") for t in range(NT)]
        ps_u = [m.ps(f"e_u{i}") for i in range(2)]
        ps_v = [m.ps(f"e_v{i}") for i in range(2)]
        S = {n: m.sem("e_" + n) for n in (
            "small_loaded", "var_ready", "rstd_ready", "hn_ready", "hT_in_psum", "hT_ready", "logits_ready", "first_ready",
            "shifted", "exp_ready", "gate_ready", "gateT_in_psum", "gateT_ready", "gateT_stored", "w_loaded_even", "w_loaded_odd", "h_ready",
            "silu_ready", "gated_ready", "down_done", "bias_done", "y_ready", "stored")}
        loaded = (S["w_loaded_even"], S["w_loaded_odd"])
        s_d, s_g = m.sem("moe_dve_step"), m.sem("moe_pool_step")
        block = ctx.enter_context(nc.Block())
        NL = 6

        def bcast_rows(src):
            return bass.AP(src.tensor, src.offset, [[0, P]] + [list(k) for k in src.ap])

        @block.sync
        def _(sp):
            sp.dma_start(rw[:, :, :], a["L0_ffn_router_w"].rearrange("(k p) e -> p k e", p=P)).then_inc(S["small_loaded"], 16)
            sp.dma_start(rb[:, :], bcast_rows(a["L0_ffn_router_b"])).then_inc(S["small_loaded"], 16)
            sp.dma_start(rbias[:, :], bcast_rows(a["L0_ffn_router_bias"])).then_inc(S["small_loaded"], 16)
            sp.dma_start(b3[0:E, :], a["L0_ffn_eb3"]).then_inc(S["small_loaded"], 16)
            sp.dma_start(b3[E:E + 1, :], a["L0_ffn_sb3"].rearrange("(u n) -> u n", u=1)).then_inc(S["small_loaded"], 16)
            sp.wait_ge(S["gateT_ready"], 1)
            sp.dma_start(scratch["gates"], gateT[:, :]).then_inc(S["gateT_stored"], 16)
            sp.wait_ge(S["gateT_stored"], 16)

            def load(r, count, w1s, w2s, w3s, b1s, b2s, gs):
                sp.wait_ge(S["down_done"], count + 1)
                sp.dma_start(w1[:, r], w1s).then_inc(loaded[r], 16)
                sp.dma_start(w2[:, r], w2s).then_inc(loaded[r], 16)
                sp.dma_start(w3[:, r], w3s).then_inc(loaded[r], 16)
                with nc.allow_non_contiguous_dma(reason="a bias column"):
                    sp.dma_start(b1[:, r], b1s).then_inc(loaded[r], 16)
                    sp.dma_start(b2[:, r], b2s).then_inc(loaded[r], 16)
                sp.dma_start(gb[:, r], bcast_rows(gs)).then_inc(loaded[r], 16)

            col = lambda s: s.rearrange("(p u) -> p u", u=1)
            with sp.Fori(0, E // 2) as i:
                for r in range(2):
                    e = 2 * i + r
                    load(r, e, a["L0_ffn_ew1"].rearrange("e (k p) n -> e p k n", p=P)[e],
                         a["L0_ffn_ew2"].rearrange("e (k p) n -> e p k n", p=P)[e], a["L0_ffn_ew3"][e],
                         col(a["L0_ffn_eb1"][e]), col(a["L0_ffn_eb2"][e]), scratch["gates"][e])
            for r in range(2):
                cols = slice(r * INTER, (r + 1) * INTER)
                load(r, E + r, a["L0_ffn_sw1"][:, cols].rearrange("(k p) n -> p k n", p=P),
                     a["L0_ffn_sw2"][:, cols].rearrange("(k p) n -> p k n", p=P), a["L0_ffn_sw3"][cols, :],
                     col(a["L0_ffn_sb1"][cols]), col(a["L0_ffn_sb2"][cols]), scratch["gates"][E])
            for t in range(NT):
                sp.wait_ge(S["y_ready"], t + 1)
                sp.dma_start(out.rearrange("b c n -> (b c) n")[t * P:(t + 1) * P, :], y[:, t, :]).then_inc(S["stored"], 16)
            sp.wait_ge(S["stored"], 16 * NT)

        @block.gpsimd
        def _(pool):
            link = Chain(pool, s_g)
            link(pool.memset(mhalf[:, :], -0.5))
            for t in range(NT):
                pool.wait_ge(S["var_ready"], t + 1)
                pool.tensor_tensor(rstd[:, t:t + 1], veps[:, t:t + 1], mhalf[:, t:t + 1], ALU.pow).then_inc(S["rstd_ready"], 1)
            pool.iota(first[:, :], pattern=[[-1, E]], base=E, channel_multiplier=0,
                      allow_small_or_imprecise_dtypes=True).then_inc(S["first_ready"], 1)

        @block.tensor
        def _(pe):
            for k in range(NC):
                for t in range(NT):
                    pe.wait_ge(S["hn_ready"], t + 1)
                    last = pe.transpose(ps_y[k][:, t * P:(t + 1) * P], hn[:, t, k * P:(k + 1) * P], keep["ident"][:, :])
                last.then_inc(S["hT_in_psum"], 1)
            pe.wait_ge(S["hT_ready"], NC)
            pe.wait_ge(S["small_loaded"], 80)
            for t in range(NT):
                for k in range(NC):
                    last = pe.matmul(ps_u[0][:, t * E:(t + 1) * E], hT[:, k, t * P:(t + 1) * P], rw[:, k, :], start=k == 0, stop=k == NC - 1)
            last.then_inc(S["logits_ready"], 1)
            pe.wait_ge(S["gate_ready"], 1)
            for t in range(NT):
                last = pe.transpose(ps_v[0][0:E + 1, t * P:(t + 1) * P], gate[:, t, :], keep["ident"][:, :])
            last.then_inc(S["gateT_in_psum"], 1)
            pe.wait_ge(S["gateT_ready"], 1)
            for t in range(NT):
                pe.matmul(ps_y[t][:, :], gateT[:, t * P:(t + 1) * P], b3[:, :], start=True, stop=False, skip_group_check=True)

            def expert(r, n, nl):
                pe.wait_ge(loaded[r], nl)
                pe.wait_ge(S["gated_ready"], n + 1)
                for w, ps in ((w1, ps_u[r]), (w2, ps_v[r])):
                    for k in range(NC):
                        last = pe.matmul(ps[:, :], w[:, r, k, :], hT[:, k, :], start=k == 0, stop=k == NC - 1)
                last.then_inc(S["h_ready"], 1)
                pe.wait_ge(S["gated_ready"], n + 3)
                for t in range(NT):
                    last = pe.matmul(ps_y[t][:, :], hh[:, r, t * P:(t + 1) * P], w3[:, r, :], start=False, stop=False, skip_group_check=True)
                last.then_inc(S["down_done"], 1)

            with pe.Fori(0, E // 2) as i:
                for r in range(2):
                    expert(r, 2 * i + r, 16 * NL * i + 16 * NL)
            for r in range(2):
                expert(r, E + r, 16 * NL * (E // 2 + 1))

        @block.scalar
        def _(act):
            act.wait_ge(S["shifted"], 1)
            act.activation(lg[:, :, :], lg[:, :, :], ACT.Exp).then_inc(S["exp_ready"], 1)

            def expert(r, n, nl):
                act.wait_ge(loaded[r], nl)
                act.wait_ge(S["h_ready"], n + 1)
                act.wait_ge(S["gated_ready"], n + 1)
                act.activation(up[:, r, :], ps_u[r][:, :], ACT.Silu, bias=b1[:, r, 0:1]).then_inc(S["silu_ready"], 1)

            with act.Fori(0, E // 2) as i:
                for r in range(2):
                    expert(r, 2 * i + r, 16 * NL * i + 16 * NL)
            for r in range(2):
                expert(r, E + r, 16 * NL * (E // 2 + 1))

        @block.vector
        def _(dve):
            dve.sem_inc(S["down_done"], 2)
            dve.sem_inc(S["gated_ready"], 2)
            link = Chain(dve, s_d)
            layernorm_transposed(dve, S["hn_ready"], link, x2, mv, stats, veps, S["rstd_ready"], rstd, hn, S["var_ready"])
            for k in range(NC):
                dve.wait_ge(S["hT_in_psum"], k + 1)
                dve.tensor_copy(hT[:, k, :], ps_y[k][:, :]).then_inc(S["hT_ready"], 1)
            dve.wait_ge(S["small_loaded"], 80)
            dve.wait_ge(S["logits_ready"], 1)
            wide = lambda v, n: v.unsqueeze(2).to_broadcast([P, NT, n])
            link(dve.tensor_tensor(lg[:, :, :], ps_u[0][:, 0:NT * E].rearrange("p (t e) -> p t e", t=NT),
                                   rb[:, :].unsqueeze(1).to_broadcast([P, NT, E]), ALU.add))
            link(dve.tensor_reduce(out=t1[:, :], in_=lg[:, :, :], axis=AX.X, op=ALU.max))
            dve.tensor_tensor(lg[:, :, :], lg[:, :, :], wide(t1[:, :], E), ALU.subtract).then_inc(S["shifted"], 1)
            dve.wait_ge(S["exp_ready"], 1)
            link(dve.tensor_reduce(out=t1[:, :], in_=lg[:, :, :], axis=AX.X, op=ALU.add))
            link(dve.reciprocal(t2[:, :], t1[:, :]))
            link(dve.tensor_tensor(lg[:, :, :], lg[:, :, :], wide(t2[:, :], E), ALU.mult))
            link(dve.tensor_tensor(lg[:, :, :], lg[:, :, :], rbias[:, :].unsqueeze(1).to_broadcast([P, NT, E]), ALU.add))
            dve.wait_ge(S["first_ready"], 1)

            def top1(vals, n, into):
                fr = first[:, 0:n].unsqueeze(1).to_broadcast([P, NT, n])
                link(dve.tensor_reduce(out=t1[:, :], in_=vals, axis=AX.X, op=ALU.max))
                link(dve.tensor_tensor(cand[:, :, 0:n], vals, wide(t1[:, :], n), ALU.is_equal))
                link(dve.tensor_tensor(cand[:, :, 0:n], cand[:, :, 0:n], fr, ALU.mult))
                link(dve.tensor_reduce(out=t2[:, :], in_=cand[:, :, 0:n], axis=AX.X, op=ALU.max))
                link(dve.tensor_tensor(into, cand[:, :, 0:n], wide(t2[:, :], n), ALU.is_equal))

            def top2(vals, n, into):
                top1(vals, n, into)
                link(dve.tensor_scalar(out=left[:, :, 0:n], in0=into, scalar1=2 * NEG, scalar2=None, op0=ALU.mult))
                link(dve.tensor_tensor(left[:, :, 0:n], left[:, :, 0:n], vals, ALU.add))
                top1(left[:, :, 0:n], n, pick[:, :, 0:n])
                link(dve.tensor_tensor(into, into, pick[:, :, 0:n], ALU.add))

            GE = E // GROUPS
            link(dve.tensor_reduce(out=gmax[:, :, :], in_=lg[:, :, :].rearrange("p t (g e) -> p t g e", g=GROUPS), axis=AX.X, op=ALU.max))
            top2(gmax[:, :, :], GROUPS, gkeep[:, :, :])
            kb = gkeep[:, :, :].unsqueeze(3).to_broadcast([P, NT, GROUPS, GE])
            bv = both[:, :, :].rearrange("p t (g e) -> p t g e", g=GROUPS)
            link(dve.tensor_tensor(bv, lg[:, :, :].rearrange("p t (g e) -> p t g e", g=GROUPS), kb, ALU.mult))
            link(dve.tensor_scalar(out=gkeep[:, :, :], in0=gkeep[:, :, :], scalar1=1.0, scalar2=-NEG, op0=ALU.subtract, op1=ALU.mult))
            link(dve.tensor_tensor(bv, bv, kb, ALU.add))
            link(dve.memset(gate[:, :, :], 1.0))
            top2(both[:, :, :], E, gate[:, :, 0:E])
            dve.tensor_tensor(gate[:, :, 0:E], gate[:, :, 0:E], lg[:, :, :], ALU.mult).then_inc(S["gate_ready"], 1)
            dve.wait_ge(S["gateT_in_psum"], 1)
            dve.tensor_copy(gateT[:, :], ps_v[0][0:E + 1, :]).then_inc(S["gateT_ready"], 1)

            def expert(r, n, nl, link):
                dve.wait_ge(loaded[r], nl)
                dve.wait_ge(S["h_ready"], n + 1)
                dve.wait_ge(S["silu_ready"], n + 1)
                dve.wait_ge(S["down_done"], n + 1)
                link(dve.scalar_tensor_tensor(out=hh[:, r, :], in0=ps_v[r][:, :], scalar=b2[:, r, 0:1], in1=up[:, r, :],
                                              op0=ALU.add, op1=ALU.mult))
                dve.tensor_tensor(hh[:, r, :], hh[:, r, :], gb[:, r, :], ALU.mult).then_inc(S["gated_ready"], 1)

            with dve.Fori(0, E // 2) as i:
                dve.sem_clear(s_d)
                link = Chain(dve, s_d)
                for r in range(2):
                    expert(r, 2 * i + r, 16 * NL * i + 16 * NL, link)
            for r in range(2):
                expert(r, E + r, 16 * NL * (E // 2 + 1), link)
            dve.wait_ge(S["down_done"], E + 2 + 2)
            for t in range(NT):
                dve.tensor_tensor(y[:, t, :], ps_y[t][:, :], x2[:, t, :], ALU.add).then_inc(S["y_ready"], 1)


_INS = ["x", "ctx_4096"] + ["L0_xattn_" + n for n in ("W_lin1", "b_lin1", "W_lin2", "b_lin2", "W_conv1", "W_conv2", "W_conv3")] + [
    "L0_attn_wq", "L0_attn_wkv", "L0_attn_wo"] + ["L0_ffn_" + n for n in (
        "router_w", "router_b", "router_bias", "ew1", "eb1", "ew2", "eb2", "ew3", "eb3", "sw1", "sb1", "sw2", "sb2", "sw3", "sb3")]


def build(nc, a, out):
    scratch = {
        "feats": nc.dram_tensor("feats_rows", [TOK, N], F32, kind="Internal").ap(),
        "keys": nc.dram_tensor("key_rows", [METHODS, B, N], F32, kind="Internal").ap(),
        "x1": nc.dram_tensor("x1_rows", [TOK, N], F32, kind="Internal").ap(),
        "gates": nc.dram_tensor("gate_rows", [17, TOK], F32, kind="Internal").ap(),
    }
    with ExitStack() as ctx:
        with ExitStack() as graph:
            keep = constants(nc, graph)
            prepare(nc, a, keep, scratch)
            cross_attention(nc, a, keep, scratch)
        m = Memory(nc, ctx)
        late = {n: m.sb("late_" + n, s) for n, s in (("x1", [P, NT, N]), ("x2", [P, NT, N]), ("ident", [P, P]))}
        identity(nc, late["ident"])
        self_attention(nc, a, late, scratch)
        experts(nc, a, late, scratch, out)


def identity(nc, t):
    with nc.semaphore("late_ident") as done, nc.Block() as block:
        @block.gpsimd
        def _(pool):
            pool.memset(t[:, :], 0.0).then_inc(done, 1)
            pool.wait_ge(done, 1)
            pool.affine_select(out=t[:, :], in_=t[:, :], compare_op=ALU.not_equal, fill=1.0, base=0,
                               pattern=[[-1, P]], channel_multiplier=1).then_inc(done, 1)
            pool.wait_ge(done, 2)


def kernel(**inputs):
    import numpy as np
    import concourse.bacc as bacc
    from concourse.bass_utils import run_bass_kernel_spmd

    nc = bacc.Bacc("TRN2", target_bir_lowering=False, num_devices=1)
    arrays, args = {}, {}
    for name in _INS:
        arrays[name] = np.ascontiguousarray(inputs[name])
        args[name] = nc.dram_tensor(name, arrays[name].shape, F32, kind="ExternalInput").ap()
    out = nc.dram_tensor("out", (B, C, N), F32, kind="ExternalOutput").ap()
    build(nc, args, out)
    r = run_bass_kernel_spmd(nc, [arrays], core_ids=[0])
    return r.results[0]["out"]
```

```python
from contextlib import ExitStack

import concourse.bass as bass
from concourse import mybir

F32 = mybir.dt.float32
F16 = mybir.dt.float16
BF16 = mybir.dt.bfloat16
I32 = mybir.dt.int32
ALU = mybir.AluOpType
ACT = mybir.ActivationFunctionType
AX = mybir.AxisListType

P = 128
B, C, N = 16, 32, 512
TOK = B * C
NT = TOK // P
NC = N // P
K = 10
METHODS = 4
BITS = 10
HD = 32
GH = C * METHODS // HD
PB = 3
NG = 11
GB = 16
NBLK = NG * GB
NPAD = NBLK * PB
PERM = ([2, 0, 3, 1], [1, 3, 0, 2])
OUTC = (32, 64)
LN_EPS = 1e-5
WSCALE = 256.0
NEG = -1e30


def window(t, start, dims):
    a = t[:, start:start + 1]
    return bass.AP(a.tensor, a.offset, [list(a.ap[0])] + [list(d) for d in dims])


class Chain:

    def __init__(self, eng, sem):
        self.eng, self.sem, self.n = eng, sem, 0

    def __call__(self, ins):
        self.n += 1
        ins.then_inc(self.sem, 1)
        self.eng.wait_ge(self.sem, self.n)


class Memory:
    def __init__(self, nc, ctx):
        self.nc, self.ctx = nc, ctx

    def sb(self, name, shape, dt=F32):
        return self.ctx.enter_context(self.nc.sbuf_tensor(name, shape, dt))

    def ps(self, name):
        return self.ctx.enter_context(self.nc.psum_tensor(name, [P, 512], F32))

    def sem(self, name):
        return self.ctx.enter_context(self.nc.semaphore(name))


def prepare(nc, a, keep, scratch):
    with ExitStack() as ctx:
        m = Memory(nc, ctx)
        xt = m.sb("p_x", [P, NT, N])
        ft = m.sb("p_f", [P, NT, N])
        stats = m.sb("p_stats", [P, NT, 6])
        mv = m.sb("p_mv", [P, NT, 2])
        veps = m.sb("p_veps", [P, NT])
        rstd = m.sb("p_rstd", [P, NT])
        mhalf = m.sb("p_mhalf", [P, NT])
        R48 = 3 * B
        co = m.sb("p_co", [R48, N])
        cmin = m.sb("p_cmin", [R48, 1])
        cmax = m.sb("p_cmax", [R48, 1])
        top = m.sb("p_top", [R48, 1])
        cscale = m.sb("p_cscale", [R48, 1])
        dq = m.sb("p_dq", [R48, 10])
        qv = m.sb("p_qv", [R48, N])
        qi = m.sb("p_qi", [R48, N], I32)
        qf = m.sb("p_qf", [R48, N])
        gt = m.sb("p_gt", [R48, N])
        X = m.sb("p_X", [P, 3, NC, 2, B], I32)
        Y = m.sb("p_Y", [P, 3, NC, 2, B], I32)
        mk = m.sb("p_mk", [P, NC, 2, B], I32)
        mn = m.sb("p_mn", [P, NC, 2, B], I32)
        uu = m.sb("p_uu", [P, NC, 2, B], I32)
        tt = m.sb("p_tt", [P, NC, 2, B], I32)
        sp = m.sb("p_sp", [P, 3, NC, 2, B], I32)
        kt = m.sb("p_kt", [P, NC, METHODS, B], I32)
        kr = m.sb("p_kr", [METHODS * B, N])
        wl = [m.sb(f"p_wl{i}", [64, 256]) for i in range(2)]
        wr = [m.sb(f"p_wr{i}", [64, 2, GH, METHODS, 8]) for i in range(2)]
        wct = [m.sb(f"p_wct{i}", [64, P]) for i in range(2)]
        bl = [m.sb(f"p_bl{i}", [64, 1]) for i in range(2)]
        wf = m.sb("p_wf", [P, 2, 2, 64])
        ps_q = m.ps("pp_q")
        ps_k = m.ps("pp_k")
        ps_w = m.ps("pp_w")

        s_x = m.sem("x_loaded")
        s_c = m.sem("coords_loaded")
        s_w = m.sem("small_weights_loaded")
        s_feat = m.sem("features_ready")
        s_fout = m.sem("features_stored")
        s_var = m.sem("variance_ready")
        s_rstd = m.sem("rstd_ready")
        s_id = m.sem("identity_ready")
        s_q = m.sem("quantised")
        s_qt = m.sem("coords_transposed")
        s_key = m.sem("keys_ready")
        s_kt = m.sem("keys_transposed")
        s_kr = m.sem("key_rows_ready")
        s_wr = m.sem("weights_reordered")
        s_wp = m.sem("weight_product_ready")
        s_d = m.sem("prepare_dve_step")
        s_g = m.sem("prepare_pool_step")
        block = ctx.enter_context(nc.Block())

        @block.sync
        def _(sp_):
            for t in range(NT):
                sp_.dma_start(xt[:, t, :], a["x"].rearrange("b c n -> (b c) n")[t * P:(t + 1) * P, :]).then_inc(s_x, 16)
            for c in range(3):
                sp_.dma_start(co[c * B:(c + 1) * B, :], a["ctx_4096"][:, c, :]).then_inc(s_c, 16)
            for t in range(NT):
                sp_.wait_ge(s_feat, t + 1)
                sp_.dma_start(scratch["feats"][C + t * P:C + (t + 1) * P, :], ft[:, t, :]).then_inc(s_fout, 16)
                sp_.dma_start(scratch["x"][C + t * P:C + (t + 1) * P, :], xt[:, t, :]).then_inc(s_fout, 16)
            sp_.dma_start(scratch["feats"][0:C, :], ft[0:C, 0, :]).then_inc(s_fout, 16)
            sp_.dma_start(scratch["feats"][C + TOK:2 * C + TOK, :], ft[0:C, 0, :]).then_inc(s_fout, 16)
            sp_.dma_start(scratch["x"][0:C, :], xt[0:C, 0, :]).then_inc(s_fout, 16)
            sp_.wait_ge(s_kr, 1)
            for c in range(METHODS):
                sp_.dma_start(scratch["keys"][c, 0:B], kr[c * B:(c + 1) * B, :]).then_inc(s_fout, 16)
                sp_.dma_start(scratch["keys"][c, B:B + 1], kr[c * B:c * B + 1, :]).then_inc(s_fout, 16)
            sp_.wait_ge(s_fout, 16 * (2 * NT + 3 + 2 * METHODS))

        @block.gpsimd
        def _(pool):
            link = Chain(pool, s_g)
            link(pool.memset(keep["ident"][:, :], 0.0))
            pool.affine_select(out=keep["ident"][:, :], in_=keep["ident"][:, :], compare_op=ALU.not_equal, fill=1.0,
                               base=0, pattern=[[-1, P]], channel_multiplier=1).then_inc(s_id, 1)
            link(pool.memset(mhalf[:, :], -0.5))
            for t in range(NT):
                pool.wait_ge(s_var, t + 1)
                pool.tensor_tensor(rstd[:, t:t + 1], veps[:, t:t + 1], mhalf[:, t:t + 1], ALU.pow).then_inc(s_rstd, 1)
            pool.iota(keep["iota"][:, :], pattern=[[1, N]], base=0, channel_multiplier=0,
                      allow_small_or_imprecise_dtypes=True)
            link(pool.memset(keep["tri"][:, :], 1.0))
            link(pool.affine_select(out=keep["tri"][:, :], in_=keep["tri"][:, :], compare_op=ALU.is_gt, fill=0.0,
                                    base=0, pattern=[[1, P]], channel_multiplier=-1))
            ind = keep["ind"]
            link(pool.memset(ind[:, :], 1.0))
            iv = ind[:, :].rearrange("p (h c) -> p h c", h=GH)
            link(pool.affine_select(out=iv, in_=iv, compare_op=ALU.is_ge, fill=0.0, base=0,
                                    pattern=[[0, GH], [1, 32]], channel_multiplier=-K))
            link(pool.affine_select(out=iv, in_=iv, compare_op=ALU.is_ge, fill=0.0, base=K - 1,
                                    pattern=[[0, GH], [-1, 32]], channel_multiplier=K))
            off = keep["off"]
            link(pool.memset(off[:, :], 0.0))
            ov = off[:, :].rearrange("p (u c) -> p u c", u=GB)
            link(pool.affine_select(out=ov, in_=ov, compare_op=ALU.is_ge, fill=NEG, base=0,
                                    pattern=[[0, GB], [1, 32]], channel_multiplier=-K))
            link(pool.affine_select(out=ov, in_=ov, compare_op=ALU.is_ge, fill=NEG, base=K - 1,
                                    pattern=[[0, GB], [-1, 32]], channel_multiplier=K))
            for l, o in enumerate(OUTC):
                t = keep["same"][l]
                link(pool.memset(t[:, :], 0.0))
                for d in range(-(P // o) + 1, P // o):
                    link(pool.affine_select(out=t[:, :], in_=t[:, :], compare_op=ALU.not_equal, fill=1.0,
                                            base=-d * o, pattern=[[-1, P]], channel_multiplier=1))
            for cg in range(4):
                t = keep["gather"][:, cg, :]
                link(pool.memset(t, 0.0))
                v = t.rearrange("p (h m c) -> p h m c", h=GH, m=METHODS)
                link(pool.affine_select(out=v, in_=v, compare_op=ALU.not_equal, fill=1.0, base=-32 * cg,
                                        pattern=[[-8, GH], [0, METHODS], [-1, 8]], channel_multiplier=1))

        @block.scalar
        def _(act):
            with nc.allow_non_contiguous_dma(reason="small weights, transposed once"):
                for i, (w, cv, b) in enumerate((("L0_xattn_W_lin1", "L0_xattn_W_conv1", "L0_xattn_b_lin1"),
                                                ("L0_xattn_W_lin2", "L0_xattn_W_conv2", "L0_xattn_b_lin2"))):
                    act.dma_start(wl[i][:, :], a[w]).then_inc(s_w, 16)
                    o = OUTC[i]
                    for r in range(P // o):
                        act.dma_start(wct[i][:, r * o:(r + 1) * o], a[cv].rearrange("o e -> e o")).then_inc(s_w, 16)
                    act.dma_start(bl[i][:, :], a[b].rearrange("(e u) -> e u", u=1)).then_inc(s_w, 16)
                act.wait_ge(s_d, 1)
                act.dma_start(keep["w3f"][:, :], a["L0_xattn_W_conv3"][:, 0:C].rearrange("o c -> c o")).then_inc(s_w, 16)
                for i in range(1, 2):
                    for h in range(GH):
                        act.dma_start(keep["w3"][32 * h:32 * h + 8, i, :],
                                      a["L0_xattn_W_conv3"][:, 32 * i + 8 * h:32 * i + 8 * h + 8].rearrange("o c -> c o")).then_inc(s_w, 16)
                for r in range(2):
                    act.dma_start(keep["w3"][64 * r:64 * r + 64, 2 + r, :],
                                  a["L0_xattn_W_conv3"][:, 64:128].rearrange("o c -> c o")).then_inc(s_w, 16)
            act.wait_ge(s_w, 16 * (4 + 2 + 4 + 4 + 1 + 2))

        @block.tensor
        def _(pe):
            pe.wait_ge(s_id, 1)
            pe.wait_ge(s_q, 1)
            for j in range(NC):
                last = pe.transpose(ps_q[:, j * 64:j * 64 + R48], qf[:, j * P:(j + 1) * P], keep["ident"][0:R48, 0:R48])
            last.then_inc(s_qt, 1)
            pe.wait_ge(s_key, 1)
            for j in range(NC):
                last = pe.transpose(ps_k[0:METHODS * B, j * P:(j + 1) * P],
                                    kt[:, j].rearrange("p m b -> p (m b)").bitcast(F32), keep["ident"][:, :])
            last.then_inc(s_kt, 1)
            pe.wait_ge(s_wr, 1)
            for i, o in enumerate(OUTC):
                for part in range(2):
                    at = (2 * i + part) * 64
                    pe.matmul(ps_w[:, at:at + o], wr[i][:, part].rearrange("e h m c -> e (h m c)"), wct[i][:, 0:o],
                              start=True, stop=True)
                last = pe.matmul(ps_w[:, 256 + i:257 + i], wct[i][:, :], bl[i][:, :], start=True, stop=True)
            last.then_inc(s_wp, 1)

        @block.vector
        def _(dve):
            link = Chain(dve, s_d)
            link(dve.memset(keep["w3"][:, :, :], 0.0))
            link(dve.memset(top[:, :], float(2 ** BITS - 1)))
            dve.wait_ge(s_c, 48)
            link(dve.tensor_reduce(out=cmin[:, :], in_=co[:, :], axis=AX.X, op=ALU.min))
            link(dve.tensor_reduce(out=cmax[:, :], in_=co[:, :], axis=AX.X, op=ALU.max))
            link(dve.tensor_scalar(out=cmax[:, :], in0=cmax[:, :], scalar1=cmin[:, 0:1], scalar2=1e-6,
                                   op0=ALU.subtract, op1=ALU.add))
            num, rng, inv, quo, rh, rl, qh, ql, res, prod = (dq[:, i:i + 1] for i in range(10))
            link(dve.tensor_copy(rng, cmax[:, :]))
            link(dve.reciprocal(inv, rng))
            link(dve.tensor_tensor(quo, top[:, :], inv, ALU.mult))
            for whole, high, low in ((rng, rh, rl), (quo, qh, ql)):
                link(dve.tensor_scalar(out=high.bitcast(I32), in0=whole.bitcast(I32), scalar1=-4096, scalar2=None,
                                       op0=ALU.bitwise_and))
                link(dve.tensor_tensor(low, whole, high, ALU.subtract))
            link(dve.tensor_copy(res, top[:, :]))
            for x_, y_ in ((qh, rh), (qh, rl), (ql, rh), (ql, rl)):
                link(dve.tensor_tensor(prod, x_, y_, ALU.mult))
                link(dve.tensor_tensor(res, res, prod, ALU.subtract))
            link(dve.tensor_tensor(res, res, inv, ALU.mult))
            link(dve.tensor_tensor(cscale[:, :], quo, res, ALU.add))
            link(dve.tensor_scalar(out=qv[:, :], in0=co[:, :], scalar1=cmin[:, 0:1], scalar2=cscale[:, 0:1],
                                   op0=ALU.subtract, op1=ALU.mult))
            link(dve.tensor_copy(qi[:, :], qv[:, :]))
            link(dve.tensor_copy(qf[:, :], qi[:, :]))
            link(dve.tensor_tensor(gt[:, :], qf[:, :], qv[:, :], ALU.is_gt))
            link(dve.tensor_tensor(qf[:, :], qf[:, :], gt[:, :], ALU.subtract))
            dve.tensor_scalar(out=qf[:, :], in0=qf[:, :], scalar1=0.0, scalar2=float(2 ** BITS - 1),
                              op0=ALU.max, op1=ALU.min).then_inc(s_q, 1)
            for t in range(NT):
                dve.wait_ge(s_x, 16 * NT)
                link(dve.bn_stats(out=stats[:, t, :], in_=xt[:, t, :]))
                link(dve.bn_aggr(out=mv[:, t, :], in_=stats[:, t, :]))
                dve.tensor_scalar(out=veps[:, t:t + 1], in0=mv[:, t, 1:2], scalar1=LN_EPS, scalar2=None,
                                  op0=ALU.add).then_inc(s_var, 1)
            for t in range(NT):
                dve.wait_ge(s_rstd, t + 1)
                dve.tensor_scalar(out=ft[:, t, :], in0=xt[:, t, :], scalar1=mv[:, t, 0:1], scalar2=rstd[:, t:t + 1],
                                  op0=ALU.subtract, op1=ALU.mult).then_inc(s_feat, 1)
            dve.wait_ge(s_qt, 1)
            for v, order in enumerate(((0, 1, 2), (1, 0, 2))):
                for i, c in enumerate(order):
                    src = ps_q[:, 0:NC * 64].rearrange("p (j q) -> p j q", j=NC)[:, :, c * B:(c + 1) * B]
                    link(dve.tensor_copy(X[:, i, :, v, :], src))

            def spread(src, dst):
                cur = src
                for sh, mask in ((16, 0x030000FF), (8, 0x0300F00F), (4, 0x030C30C3), (2, 0x09249249)):
                    link(dve.scalar_tensor_tensor(out=dst, in0=cur, scalar=sh, in1=cur,
                                                  op0=ALU.logical_shift_left, op1=ALU.bitwise_or))
                    link(dve.tensor_scalar(out=dst, in0=dst, scalar1=mask, scalar2=None, op0=ALU.bitwise_and))
                    cur = dst

            def interleave(kind):
                link(dve.scalar_tensor_tensor(out=uu[:], in0=sp[:, 0], scalar=2, in1=sp[:, 2],
                                              op0=ALU.logical_shift_left, op1=ALU.bitwise_or))
                link(dve.scalar_tensor_tensor(out=uu[:], in0=sp[:, 1], scalar=1, in1=uu[:],
                                              op0=ALU.logical_shift_left, op1=ALU.bitwise_or))
                link(dve.tensor_scalar(out=tt[:], in0=uu[:], scalar1=2, scalar2=31,
                                       op0=ALU.logical_shift_left, op1=ALU.arith_shift_right))
                link(dve.tensor_scalar(out=tt[:], in0=tt[:], scalar1=-1, scalar2=-1073741825,
                                       op0=ALU.bitwise_xor, op1=ALU.bitwise_and))
                link(dve.tensor_tensor(kt[:, :, 2 * kind:2 * kind + 2, :], uu[:], tt[:], ALU.bitwise_xor))

            spread(X[:], sp[:])
            interleave(0)
            q = BITS - 1
            while q >= 1:
                low = (1 << q) - 1
                for i in range(3):
                    link(dve.tensor_scalar(out=mk[:], in0=X[:, i], scalar1=31 - q, scalar2=31,
                                           op0=ALU.logical_shift_left, op1=ALU.arith_shift_right))
                    if i:
                        link(dve.tensor_scalar(out=mn[:], in0=mk[:], scalar1=-1, scalar2=low,
                                               op0=ALU.bitwise_xor, op1=ALU.bitwise_and))
                        link(dve.tensor_tensor(uu[:], X[:, 0], X[:, i], ALU.bitwise_xor))
                        link(dve.tensor_tensor(uu[:], uu[:], mn[:], ALU.bitwise_and))
                        link(dve.tensor_tensor(X[:, i], X[:, i], uu[:], ALU.bitwise_xor))
                        link(dve.tensor_tensor(X[:, 0], X[:, 0], uu[:], ALU.bitwise_xor))
                    link(dve.scalar_tensor_tensor(out=X[:, 0], in0=mk[:], scalar=low, in1=X[:, 0],
                                                  op0=ALU.bitwise_and, op1=ALU.bitwise_xor))
                q -= 1
            for i in (1, 2):
                link(dve.tensor_tensor(X[:, i], X[:, i], X[:, i - 1], ALU.bitwise_xor))
            link(dve.memset(mn[:], 0))
            for q in range(BITS - 1, 0, -1):
                link(dve.tensor_scalar(out=mk[:], in0=X[:, 2], scalar1=31 - q, scalar2=31,
                                       op0=ALU.logical_shift_left, op1=ALU.arith_shift_right))
                link(dve.scalar_tensor_tensor(out=mn[:], in0=mk[:], scalar=(1 << q) - 1, in1=mn[:],
                                              op0=ALU.bitwise_and, op1=ALU.bitwise_xor))
            for i in range(3):
                link(dve.tensor_tensor(Y[:, i], X[:, i], mn[:], ALU.bitwise_xor))
            spread(Y[:], sp[:])
            interleave(1)
            dve.tensor_copy(keep["keys"][:, :, :, 0:B], kt[:].bitcast(F32)).then_inc(s_key, 1)
            link(dve.memset(keep["keys"][:, :, :, B:B + 1], 1.0))
            dve.wait_ge(s_kt, 1)
            dve.tensor_copy(kr[:, :], ps_k[0:METHODS * B, :]).then_inc(s_kr, 1)
            dve.wait_ge(s_w, 16 * (4 + 2 + 4 + 4 + 1 + 2))
            for i in range(2):
                for part in range(2):
                    src = wl[i][:, part * P:(part + 1) * P].rearrange("e (h c m) -> e h m c", h=GH, m=METHODS)
                    last = dve.tensor_copy(wr[i][:, part], src)
                    if i == part == 1:
                        last.then_inc(s_wr, 1)
            dve.wait_ge(s_wp, 1)
            for i, o in enumerate(OUTC):
                for part in range(2):
                    at = (2 * i + part) * 64
                    hi, lo = keep["wc"][i][:, part, 0, :], keep["wc"][i][:, part, 1, :]
                    link(dve.tensor_scalar(out=wf[:, i, part, 0:o], in0=ps_w[:, at:at + o], scalar1=WSCALE, scalar2=None,
                                           op0=ALU.mult))
                    link(dve.tensor_copy(hi, wf[:, i, part, 0:o]))
                    link(dve.tensor_tensor(lo, wf[:, i, part, 0:o], hi, ALU.subtract))
                link(dve.tensor_copy(keep["bias"][i][:, :], ps_w[:, 256 + i:257 + i]))


def cross_attention(nc, a, keep, scratch, nb=B):
    with ExitStack() as ctx:
        m = Memory(nc, ctx)
        T = 2 * NG
        krow = m.sb("krow", [P, METHODS, N])
        kcol = m.sb("kcol", [P, NC, METHODS])
        tie = m.sb("tie", [P, NC, METHODS, P], BF16)
        rank = [m.sb(f"rank{i}", [P, METHODS, NC]) for i in range(2)]
        perm = m.sb("perm", [P, METHODS, NC, N], BF16)
        ones = m.sb("ones", [P, 1], BF16)
        ctr = [m.sb(f"ctr{l}", [P, NPAD]) for l in range(2)]
        ctr16 = [m.sb(f"ctr16_{l}", [P, NPAD], F16) for l in range(2)]
        ftf = m.sb("ftf", [P, NC, C])
        ftr = m.sb("ftr", [P, NC, C])
        ft3 = m.sb("ft3", [P, NC, 3, C], BF16)
        srt = m.sb("srt", [P, NC, P])
        ext = m.sb("ext", [P, NPAD + 16])
        dif = [m.sb(f"dif{l}", [P, NBLK, 32], F16) for l in range(2)]
        dbd = [m.sb(f"dbd{l}", [P, NBLK, GH, 32], F16) for l in range(2)]
        own = m.sb("own", [P, PB])
        fs = m.sb("fs", [P, 2, GB, K])
        mx = m.sb("mx", [P, 2, GB])
        e = m.sb("e", [P, 3, GB, K])
        zs = m.sb("zs", [P, 2, GB])
        oz = m.sb("oz", [P, 2, GB, PB])
        pn = m.sb("pn", [P, 2, GB, 32])
        pt = m.sb("pt", [P, 2, 512])
        ys = m.sb("ys", [P, 4, GB, 64])
        hs = m.sb("hs", [P, 2, 240])
        sq = m.sb("sq", [P, 240])
        hm = [m.sb(f"hm{l}", [P, NPAD * OUTC[l] // P]) for l in range(2)]
        f02 = m.sb("f02", [P, 264])
        fo = [m.sb(f"fo{l}", [P, NPAD * OUTC[l] // P]) for l in range(2)]
        sums = [m.sb(f"sums{l}", [P, 2, NG]) for l in range(2)]
        s12 = m.sb("s12", [P, 2, 2])
        st = [m.sb(f"st{l}", [P, 6]) for l in range(2)]
        mhalf = m.sb("mhalf", [P, 1])
        fin0 = m.sb("fin0", [C, N])
        xb = m.sb("xb", [C, N])
        h3 = m.sb("h3", [C, N])
        z02 = m.sb("z02", [C, N])
        xo = m.sb("xo", [C, N])
        bst = m.sb("bst", [C, 6])
        bmv = m.sb("bmv", [C, 4])
        ps_s = [m.ps(f"ps_s{i}") for i in range(2)]
        ps_y = [m.ps(f"ps_y{i}") for i in range(2)]
        ps_h = [m.ps(f"ps_h{i}") for i in range(2)]
        ps_a = m.ps("ps_a")
        ps_b = m.ps("ps_b")

        names = (
            "keys_loaded", "input_loaded", "final_loaded", "out_stored",
            "scores_ready", "scores_folded", "shifted", "exp_ready", "y_ready", "y_copied", "own_scaled", "probs_ready",
            "pt_ready", "h_ready", "h_copied", "h_summed", "h_max_done",
            "compared", "counted", "ranks_ready",
            "s12_ready", "totals_ready", "norm_ready", "h3_ready", "h3_copied", "var3_ready", "rstd3_ready",
            "ctr1_in_psum", "ctr1_ready", "out_ready", "zero_ready",
            "passed_first", "passed_last")
        S = {n: m.sem("b_" + n) for n in names}
        L = {n: [m.sem(f"b{l}_{n}") for l in range(2)] for n in (
            "input_transposed", "split_ready", "perm_ready", "sorted_in_psum", "sorted_copied", "sorted_t_in_psum",
            "ext_ready", "dif_ready", "ctr16_ready", "var_ready", "rstd_ready")}
        s_d = m.sem("cross_dve_step")
        s_g = m.sem("cross_pool_step")
        block = ctx.enter_context(nc.Block())
        SC = float(HD) ** -0.5
        L0, L1 = range(0, NG), range(NG, T)

        def layer(s):
            l = s // NG
            cgs = P // OUTC[l]
            return l, s % NG, cgs, GB // cgs, GB // cgs * PB

        def yunit(s, u):
            return s if s < NG else NG + 2 * (s - NG) + u // 8

        YU = 3 * NG

        def all_pass(eng, name):
            eng.sem_inc(S[name], 1)
            eng.wait_ge(S[name], 4)


        @block.sync
        def _(sp):
            def rows(name, b):
                return scratch[name].rearrange("(b c) n -> b c n", c=C)[b]

            def load_ahead(t):
                src = scratch["keys"].rearrange("m b n -> b m n")[t + 1]
                if not (isinstance(t, int) and t < 0):
                    sp.wait_ge(S["ranks_ready"], t + 1)
                sp.dma_start(krow[:, :, :], bass.AP(src.tensor, src.offset, [[0, P]] + [list(k) for k in src.ap])).then_inc(S["keys_loaded"], 16)
                if not (isinstance(t, int) and t < 0):
                    sp.wait_ge(L["dif_ready"][0], t + 1)
                    sp.wait_ge(L["ctr16_ready"][0], t + 1)
                for h in range(GH):
                    src = scratch["feats"].rearrange("(b h c) n -> b h c n", h=GH, c=8)[t + 2, h]
                    sp.dma_start(ctr[0][32 * h:32 * h + 32, 0:N],
                                 bass.AP(src.tensor, src.offset, [[0, METHODS]] + [list(k) for k in src.ap])).then_inc(S["input_loaded"], 16)

            def load_final(t):
                sp.wait_ge(S["out_ready"], t)
                sp.dma_start(fin0[:, :], rows("feats", t - 1)).then_inc(S["final_loaded"], 16)
                sp.dma_start(xb[:, :], rows("x", t - 1)).then_inc(S["final_loaded"], 16)

            def store(t):
                sp.wait_ge(S["out_ready"], t + 1)
                sp.dma_start(rows("x1", t - 1), xo[:, :]).then_inc(S["out_stored"], 16)

            load_ahead(-1)
            load_ahead(0)
            with sp.Fori(1, nb) as t:
                load_final(t)
                load_ahead(t)
                store(t)
            load_final(nb)
            store(nb)
            load_final(nb + 1)
            store(nb + 1)
            sp.wait_ge(S["out_stored"], 16 * (nb + 2))

        @block.gpsimd
        def _(pool):
            link = Chain(pool, s_g)
            pool.memset(mhalf[:, :], -0.5)
            pool.memset(ctr[0][:, N:NPAD], 0.0)
            pool.memset(ctr[1][:, :], 0.0)
            for l in range(2):
                pool.memset(ctr16[l][:, N:NPAD], 0.0)
                pool.memset(dif[l][:, :, :], 0.0)
                pool.memset(dbd[l][:, :, :, :], 0.0)
            pool.memset(hm[1][:, :], 0.0)
            pool.memset(sums[1][:, :, :], 0.0)
            pool.memset(ext[:, :], 0.0)
            pool.memset(ones[:, :], 1.0)
            pool.memset(pn[:, :, :, :], 0.0)
            link(pool.memset(own[:, :], 1.0))
            for h in range(GH):
                ov = own[32 * h:32 * h + 32, :]
                link(pool.affine_select(out=ov, in_=ov, compare_op=ALU.is_ge, fill=0.0, base=0,
                                        pattern=[[-K, PB]], channel_multiplier=1))
                pool.affine_select(out=ov, in_=ov, compare_op=ALU.is_ge, fill=0.0, base=K - 1,
                                   pattern=[[K, PB]], channel_multiplier=-1).then_inc(S["zero_ready"], 1)
                pool.wait_ge(S["zero_ready"], h + 1)
            
            def norms(l, n):
                pool.wait_ge(L["var_ready"][l], n)
                pool.tensor_tensor(st[l][:, 4:5], st[l][:, 3:4], mhalf[:, :], ALU.pow).then_inc(L["rstd_ready"][l], 1)

            def norm3(n):
                pool.wait_ge(S["var3_ready"], n)
                pool.tensor_tensor(bmv[:, 3:4], bmv[:, 2:3], mhalf[0:C, :], ALU.pow).then_inc(S["rstd3_ready"], 1)

            def expand(t, s):
                pool.wait_ge(S["own_scaled"], T * t + s + 1)
                pool.wait_ge(S["pt_ready"], T * t + s + 1)
                pool.tensor_tensor(pn[:, s % 2, :, 0:PB * K].rearrange("p u (i k) -> p u i k", i=PB),
                                   e[:, s % 3, :, :].unsqueeze(2).to_broadcast([P, GB, PB, K]),
                                   oz[:, s % 2, :, :].unsqueeze(3).to_broadcast([P, GB, PB, K]), ALU.mult).then_inc(S["probs_ready"], 1)

            def iteration(t, final=True, second=True, first=True):
                for s in range(T + 1):
                    if s == 1 and final:
                        norms(1, t)
                    if s == 1 and second:
                        norms(0, t)
                    if s == 4 and final:
                        norm3(t)
                    if s and (first if s - 1 in L0 else second):
                        expand(t, s - 1)

            iteration(0, final=False, second=False)
            all_pass(pool, "passed_first")
            pool.sem_inc(S["probs_ready"], NG)
            with pool.Fori(1, nb) as t:
                iteration(t)
            all_pass(pool, "passed_last")
            pool.sem_inc(S["probs_ready"], NG)
            iteration(nb, first=False)
            norms(1, nb + 1)
            norm3(nb + 1)

        @block.scalar
        def _(act):
            def ctr16_copy(l):
                act.activation(ctr16[l][:, 0:N], ctr[l][:, 0:N], ACT.Copy).then_inc(L["ctr16_ready"][l], 1)

            def sorted_copy(l, n):
                act.wait_ge(L["sorted_in_psum"][l], n)
                act.activation(srt[:, :, :], ps_b[:, :].rearrange("p (j q) -> p j q", j=NC), ACT.Copy).then_inc(L["sorted_copied"][l], 1)

            def ext_copy(l, n):
                act.wait_ge(L["sorted_t_in_psum"][l], n)
                act.activation(ext[:, 5:5 + N], ps_a[:, :], ACT.Copy).then_inc(L["ext_ready"][l], 1)

            def h3_copy(t):
                act.wait_ge(S["h3_ready"], t)
                act.activation(h3[:, :], ps_b[0:C, :], ACT.Copy).then_inc(S["h3_copied"], 1)

            def y_copy(t, s):
                l, g, cgs, jg, jp = layer(s)
                O = OUTC[l]
                units = 1 + l
                k = GB // units
                for u in range(units):
                    n = yunit(s, u * k)
                    act.wait_ge(S["y_ready"], YU * t + n + 1)
                    if s >= 4 and u == 0:
                        act.wait_ge(S["h_ready"], T * t + s - 3)
                    act.activation(ys[:, s % 4, u * k:(u + 1) * k, 0:O],
                                   ps_y[n % 2][:, :].rearrange("p (u o) -> p u o", u=k), ACT.Copy).then_inc(S["y_copied"], 1)

            def exponentials(t, s):
                act.wait_ge(S["shifted"], T * t + s + 1)
                act.activation(e[:, s % 3, :, :], e[:, s % 3, :, :], ACT.Exp, scale=SC).then_inc(S["exp_ready"], 1)

            def h_copy(t, s):
                l, g, cgs, jg, jp = layer(s)
                act.wait_ge(S["h_ready"], T * t + s + 1)
                act.wait_ge(S["h_max_done"], T * t + s + 1)
                act.activation(hs[:, s % 2, 0:jp * K], ps_h[s % 2][:, 0:jp * K], ACT.Identity,
                               accum_out=sums[l][:, 0, g:g + 1]).then_inc(S["h_copied"], 1)
                act.wait_ge(S["h_copied"], T * t + s + 3)
                if not (isinstance(t, int) and t == 0 and s == 0) and s:
                    act.wait_ge(S["h_summed"], T * t + s)
                act.activation(sq[:, 0:jp * K], hs[:, s % 2, 0:jp * K], ACT.Square,
                               accum_out=sums[l][:, 1, g:g + 1]).then_inc(S["h_summed"], 1)

            def iteration(t, final=True, second=True, first=True, ahead=True):
                on = lambda s: 0 <= s < T and (first if s in L0 else second)
                for s in range(T + 4):
                    if s == 3 and final:
                        h3_copy(t)
                    if s == 3 and second:
                        act.wait_ge(S["ctr1_in_psum"], t)
                        act.activation(ctr[1][:, 0:N], ps_a[:, :], ACT.Copy).then_inc(S["ctr1_ready"], 1)
                        act.wait_ge(S["ctr1_ready"], t)
                        ctr16_copy(1)
                    if s == 6 and second:
                        sorted_copy(1, t)
                    if s == 7 and second:
                        ext_copy(1, t)
                    if s == 15 and ahead:
                        act.wait_ge(S["input_loaded"], 64 * t + 128)
                        act.wait_ge(S["h_ready"], T * t + NG)
                        ctr16_copy(0)
                    if s == 17 and ahead:
                        sorted_copy(0, t + 2)
                    if s == 18 and ahead:
                        ext_copy(0, t + 2)
                    if on(s):
                        y_copy(t, s)
                        exponentials(t, s)
                    if on(s - 4):
                        h_copy(t, s - 4)

            def skip(layer_, sems=("y_copied", "exp_ready", "h_copied", "h_summed")):
                for n in sems:
                    act.sem_inc(S[n], NG * (1 + layer_) if n == "y_copied" else NG)

            act.wait_ge(S["input_loaded"], 64)
            act.wait_ge(S["zero_ready"], GH)
            ctr16_copy(0)
            sorted_copy(0, 1)
            ext_copy(0, 1)
            iteration(0, final=False, second=False)
            all_pass(act, "passed_first")
            skip(1)
            with act.Fori(1, nb) as t:
                iteration(t)
            all_pass(act, "passed_last")
            skip(0)
            iteration(nb, first=False, ahead=False)
            h3_copy(nb + 1)

        @block.tensor
        def _(pe):
            ident = keep["ident"]

            def transpose_input(l, n, ready, count):
                pe.wait_ge(ready, count)
                for j in range(NC):
                    last = pe.transpose(ps_a[:, j * P:(j + 1) * P], ctr[l][:, j * P:(j + 1) * P], ident[:, :])
                last.then_inc(L["input_transposed"][l], 1)

            def count_ranks(t):
                for c in range(METHODS):
                    for j in range(NC):
                        at = ps_b[:, c * NC + j:c * NC + j + 1]
                        for i in range(NC):
                            if c == j == 0:
                                pe.wait_ge(S["compared"], NC * (t + 1) + i + 1)
                            pe.matmul(at, perm[:, c, i, j * P:(j + 1) * P], ones[:, :], start=i == 0, stop=False)
                        last = pe.matmul(at, tie[:, j, c, :], ones[:, :], start=False, stop=True)
                last.then_inc(S["counted"], 1)

            def sort(l, n):
                pe.wait_ge(L["perm_ready"][l], n)
                pe.wait_ge(L["split_ready"][l], n)
                for r in range(NC):
                    for p in range(METHODS):
                        at = ps_b[:, r * P:(r + 1) * P].rearrange("p (h m c) -> p h m c", h=GH, m=METHODS)[:, :, p, :]
                        for j in range(NC):
                            for part in range(3):
                                last = pe.matmul(at, perm[:, PERM[l][p], j, r * P:(r + 1) * P],
                                                 ft3[:, j, part, :].rearrange("p (h c) -> p h c", h=GH),
                                                 start=j == part == 0, stop=j == NC - 1 and part == 2)
                last.then_inc(L["sorted_in_psum"][l], 1)

            def transpose_sorted(l, n):
                pe.wait_ge(L["sorted_copied"][l], n)
                for r in range(NC):
                    last = pe.transpose(ps_a[:, r * P:(r + 1) * P], srt[:, r, :], ident[:, :])
                last.then_inc(L["sorted_t_in_psum"][l], 1)

            def totals(t):
                pe.wait_ge(S["s12_ready"], t)
                for l in range(2):
                    last = pe.matmul(ps_a[:, 2 * l:2 * l + 2], keep["same"][l][:, :], s12[:, l, :], start=True, stop=True)
                last.then_inc(S["totals_ready"], 1)

            def last_product(t):
                pe.wait_ge(S["norm_ready"], t)
                pe.wait_ge(S["final_loaded"], 32 * t)
                pe.matmul(ps_b[0:C, :], keep["w3"][:, 1, :], ctr[1][:, 0:N], start=True, stop=False, skip_group_check=True)
                pe.matmul(ps_b[0:C, :], keep["w3f"][:, :], fin0[:, :], start=False, stop=False, skip_group_check=True)
                for r in range(2):
                    at = r * (NPAD // 2)
                    w = min(NPAD // 2, N - at)
                    last = pe.matmul(ps_b[0:C, at:at + w], keep["w3"][:, 2 + r, :], fo[1][:, 0:w], start=False, stop=r == 1, skip_group_check=True)
                last.then_inc(S["h3_ready"], 1)

            def second_input(t):
                for cg in range(4):
                    at = cg * (NPAD // 4)
                    w = min(NPAD // 4, N - at)
                    last = pe.matmul(ps_a[:, at:at + w], keep["gather"][:, cg, :], fo[0][:, 0:w], start=True, stop=True)
                last.then_inc(S["ctr1_in_psum"], 1)

            def scores(t, s):
                l, g, cgs, jg, jp = layer(s)
                O = OUTC[l]
                jc = NBLK // cgs
                blocks = [cg * jc + g * jg + jj for cg in range(cgs) for jj in range(jg)]
                if g == 0:
                    pe.wait_ge(L["dif_ready"][l], t if l else t + 1)
                pe.wait_ge(S["scores_folded"], T * t + s + 1)
                bank = ps_s[s % 2]
                pe.matmul(bank[:, :], keep["ind"][:, :], keep["off"][:, :], start=True, stop=False, skip_group_check=True)
                for u, j in enumerate(blocks):
                    last = pe.matmul(bank[:, u * 32:u * 32 + 32], dbd[l][:, j].rearrange("p h c -> p (h c)"), dif[l][:, j, :],
                                     start=False, stop=u == GB - 1, skip_group_check=True)
                last.then_inc(S["scores_ready"], 1)
                k = GB // (1 + l)
                for u, j in enumerate(blocks):
                    n = yunit(s, u)
                    if u % k == 0:
                        pe.wait_ge(S["y_copied"], YU * t + n + 1)
                    bd = dbd[l][:, j].rearrange("p h c -> p (h c)")
                    at = ps_y[n % 2][:, (u % k) * O:(u % k) * O + O]
                    pe.matmul(at, bd, keep["wc"][l][:, 1, 0, :], start=True, stop=False)
                    last = pe.matmul(at, bd, keep["wc"][l][:, 1, 1, :], start=False, stop=True)
                    if u % k == k - 1:
                        last.then_inc(S["y_ready"], 1)

            def product(t, s):
                l, g, cgs, jg, jp = layer(s)
                O = OUTC[l]
                if g == 0:
                    pe.wait_ge(L["ctr16_ready"][l], t if l else t + 1)
                pe.wait_ge(S["pt_ready"], T * t + s + 3)
                pe.wait_ge(S["y_copied"], YU * t + yunit(s, GB - 1) + 3)
                pe.wait_ge(S["h_copied"], T * t + s + 1)
                bank = ps_h[s % 2]
                for cg in range(cgs):
                    pts = (cg * (NBLK // cgs) + g * jg) * PB
                    rows = slice(cg * O, cg * O + O)
                    mv = ctr16[l][:, pts:pts + jp].unsqueeze(2).to_broadcast([P, jp, K])
                    at = bank[rows, 0:jp * K].rearrange("p (i k) -> p i k", k=K)
                    pe.matmul(at, keep["wc"][l][:, 0, 0, :], mv, start=True, stop=False, skip_group_check=True)
                    pe.matmul(at, keep["wc"][l][:, 0, 1, :], mv, start=False, stop=False, skip_group_check=True)
                    for jj in range(jg):
                        u = cg * jg + jj
                        last = pe.matmul(bank[rows, jj * 30:jj * 30 + 30], ys[:, s % 4, u, 0:O], pt[:, s % 2, u * 32:u * 32 + 30],
                                         start=False, stop=jj == jg - 1, skip_group_check=True)
                last.then_inc(S["h_ready"], 1)

            def iteration(t, final=True, second=True, first=True, ahead=True):
                on = lambda s: 0 <= s < T and (first if s in L0 else second)
                for s in range(T + 3):
                    if s == 1 and final:
                        totals(t)
                    if s == 3 and final:
                        last_product(t)
                    if s == 3 and second:
                        second_input(t)
                    if s == 4 and second:
                        transpose_input(1, t, S["ctr1_ready"], t)
                    if s == 5 and second:
                        sort(1, t)
                    if s == 7 and second:
                        transpose_sorted(1, t)
                    if s == 13 and ahead:
                        count_ranks(t)
                    if s == 14 and ahead:
                        transpose_input(0, t + 2, S["input_loaded"], 64 * t + 128)
                    if s == 16 and ahead:
                        sort(0, t + 2)
                    if s == 18 and ahead:
                        transpose_sorted(0, t + 2)
                    if on(s):
                        scores(t, s)
                    if on(s - 3):
                        product(t, s - 3)

            def skip(l):
                pe.sem_inc(S["scores_ready"], NG)
                pe.sem_inc(S["y_ready"], NG * (1 + l))
                pe.sem_inc(S["h_ready"], NG)

            pe.wait_ge(S["zero_ready"], GH)
            transpose_input(0, 1, S["input_loaded"], 64)
            count_ranks(-1)
            sort(0, 1)
            transpose_sorted(0, 1)
            iteration(0, final=False, second=False)
            all_pass(pe, "passed_first")
            skip(1)
            with pe.Fori(1, nb) as t:
                iteration(t)
            all_pass(pe, "passed_last")
            skip(0)
            iteration(nb, first=False, ahead=False)
            totals(nb + 1)
            last_product(nb + 1)

        @block.vector
        def _(dve):
            chain = [None]

            def link(ins):
                chain[0](ins)

            def begin(n):
                dve.wait_ge(S["keys_loaded"], 16 * n)
                link(dve.tensor_copy(kcol[:, :, :], keep["keys"][:, :, :, bass.ds(n - 1, 1)].rearrange("p j m b -> p j (m b)")))

            def compare(i):
                for c in range(METHODS):
                    key = kcol[:, i, c:c + 1]
                    dve.tensor_scalar(out=perm[:, c, i, 0:(i + 1) * P], in0=krow[:, c, 0:(i + 1) * P], scalar1=key, scalar2=None, op0=ALU.is_gt)
                    if i < NC - 1:
                        dve.tensor_scalar(out=perm[:, c, i, (i + 1) * P:N], in0=krow[:, c, (i + 1) * P:N], scalar1=key, scalar2=None, op0=ALU.is_ge)
                    last = dve.scalar_tensor_tensor(out=tie[:, i, c, :], in0=krow[:, c, i * P:(i + 1) * P], scalar=key,
                                                    in1=keep["tri"][:, :], op0=ALU.is_equal, op1=ALU.mult)
                last.then_inc(S["compared"], 1)

            def ranks(t):
                link(dve.tensor_copy(rank[1][:, :, :], rank[0][:, :, :]))
                dve.wait_ge(S["counted"], t + 2)
                dve.tensor_copy(rank[0][:, :, :], ps_b[:, 0:METHODS * NC].rearrange("p (m j) -> p m j", m=METHODS)).then_inc(S["ranks_ready"], 1)
                dve.wait_ge(S["ranks_ready"], t + 2)

            def one_hot(l, c):
                for j in range(NC):
                    last = dve.tensor_scalar(out=perm[:, c, j, :], in0=keep["iota"][:, :], scalar1=rank[l][:, c, j:j + 1],
                                             scalar2=None, op0=ALU.is_equal)
                if c == METHODS - 1:
                    last.then_inc(L["perm_ready"][1 if l else 0], 1)

            def split(l, n):
                dve.wait_ge(L["input_transposed"][l], n)
                src = ps_a[:, :].rearrange("p (j h m c) -> p j h m c", j=NC, h=GH, m=METHODS)[:, :, :, 0, :]
                link(dve.tensor_copy(ftf[:, :, :].rearrange("p j (h c) -> p j h c", h=GH), src))
                link(dve.tensor_copy(ft3[:, :, 0, :], ftf[:, :, :]))
                link(dve.tensor_tensor(ftr[:, :, :], ftf[:, :, :], ft3[:, :, 0, :], ALU.subtract))
                link(dve.tensor_copy(ft3[:, :, 1, :], ftr[:, :, :]))
                link(dve.tensor_tensor(ftr[:, :, :], ftr[:, :, :], ft3[:, :, 1, :], ALU.subtract))
                dve.tensor_copy(ft3[:, :, 2, :], ftr[:, :, :]).then_inc(L["split_ready"][l], 1)

            def differences(l, n):
                dve.wait_ge(L["ext_ready"][l], n)
                link(dve.tensor_copy(ext[:, 5 + N:10 + N], ext[:, 4 + N:5 + N].to_broadcast([P, 5])))
                c3 = ctr[l][:, :].rearrange("p (j i) -> p j i", i=PB)
                d4 = dif[l][:, :, 0:PB * K].rearrange("p j (i k) -> p j i k", i=PB)
                full, rest = N // PB, N % PB
                link(dve.tensor_tensor(d4[:, 0:full], window(ext, 0, [[PB, full], [1, PB], [1, K]]),
                                       c3[:, 0:full].unsqueeze(3).to_broadcast([P, full, PB, K]), ALU.subtract))
                link(dve.tensor_tensor(d4[:, full, 0:rest], window(ext, full * PB, [[1, rest], [1, K]]),
                                       c3[:, full, 0:rest].unsqueeze(2).to_broadcast([P, rest, K]), ALU.subtract))
                for j, w in ((0, 3), (1, 2)):
                    link(dve.tensor_tensor(d4[:, j, 0:w], window(ext, 5, [[0, w], [1, K]]),
                                           c3[:, j, 0:w].unsqueeze(2).to_broadcast([P, w, K]), ALU.subtract))
                for i in range(4):
                    w = K - 6 - i
                    link(dve.tensor_tensor(d4[:, i // PB, i % PB, 6 + i:K], ext[:, 10 + i:11 + i].to_broadcast([P, w]),
                                           ctr[l][:, i:i + 1].to_broadcast([P, w]), ALU.subtract))

            def block_diagonal(l, h):
                rows = slice(32 * h, 32 * h + 32)
                last = dve.tensor_copy(dbd[l][rows, :, h, :], dif[l][rows, :, :])
                if h == GH - 1:
                    last.then_inc(L["dif_ready"][l], 1)

            def sum_up(t):
                dve.wait_ge(S["h_summed"], T * t)
                dve.tensor_reduce(out=s12[:, 0, :], in_=sums[0][:, :, :], axis=AX.X, op=ALU.add)
                dve.tensor_reduce(out=s12[:, 1, :], in_=sums[1][:, :, :], axis=AX.X, op=ALU.add).then_inc(S["s12_ready"], 1)

            def variances(t, layers):
                dve.wait_ge(S["totals_ready"], t)
                cnt = float(N * K)
                for l in layers:
                    v = st[l]
                    link(dve.tensor_scalar(out=v[:, 0:1], in0=ps_a[:, 2 * l:2 * l + 1], scalar1=1.0 / (cnt * WSCALE), scalar2=None, op0=ALU.mult))
                    link(dve.tensor_scalar(out=v[:, 1:2], in0=ps_a[:, 2 * l + 1:2 * l + 2], scalar1=1.0 / (cnt * WSCALE * WSCALE), scalar2=LN_EPS,
                                           op0=ALU.mult, op1=ALU.add))
                    link(dve.tensor_tensor(v[:, 2:3], v[:, 0:1], v[:, 0:1], ALU.mult))
                    dve.tensor_tensor(v[:, 3:4], v[:, 1:2], v[:, 2:3], ALU.subtract).then_inc(L["var_ready"][l], 1)
                for l in layers:
                    link(dve.tensor_tensor(st[l][:, 0:1], st[l][:, 0:1], keep["bias"][l][:, :], ALU.add))
                    link(dve.tensor_scalar(out=hm[l][:, :], in0=hm[l][:, :], scalar1=1.0 / WSCALE, scalar2=keep["bias"][l][:, 0:1],
                                           op0=ALU.mult, op1=ALU.add))

            def normalise(t, layers):
                for l in layers:
                    npt = NPAD * OUTC[l] // P
                    dve.wait_ge(L["rstd_ready"][l], t)
                    link(dve.tensor_scalar(out=hm[l][:, :], in0=hm[l][:, :], scalar1=st[l][:, 0:1], scalar2=st[l][:, 4:5],
                                           op0=ALU.subtract, op1=ALU.mult))
                    link(dve.tensor_scalar(out=f02[:, 0:npt], in0=hm[l][:, :], scalar1=0.2, scalar2=None, op0=ALU.mult))
                    last = dve.tensor_tensor(fo[l][:, :], hm[l][:, :], f02[:, 0:npt], ALU.max)
                    if l == layers[-1]:
                        last.then_inc(S["norm_ready"], 1)
                    else:
                        link(last)

            def variance3(t):
                dve.wait_ge(S["h3_copied"], t)
                link(dve.bn_stats(out=bst[:, :], in_=h3[:, :]))
                link(dve.bn_aggr(out=bmv[:, 0:2], in_=bst[:, :]))
                dve.tensor_scalar(out=bmv[:, 2:3], in0=bmv[:, 1:2], scalar1=LN_EPS, scalar2=None, op0=ALU.add).then_inc(S["var3_ready"], 1)

            def output(t):
                dve.wait_ge(S["rstd3_ready"], t)
                link(dve.tensor_scalar(out=h3[:, :], in0=h3[:, :], scalar1=bmv[:, 0:1], scalar2=bmv[:, 3:4], op0=ALU.subtract, op1=ALU.mult))
                link(dve.tensor_scalar(out=z02[:, :], in0=h3[:, :], scalar1=0.2, scalar2=None, op0=ALU.mult))
                link(dve.tensor_tensor(h3[:, :], h3[:, :], z02[:, :], ALU.max))
                dve.wait_ge(S["final_loaded"], 32 * t)
                dve.wait_ge(S["out_stored"], 16 * t)
                dve.tensor_tensor(xo[:, :], h3[:, :], xb[:, :], ALU.add).then_inc(S["out_ready"], 1)

            def fold(t, s):
                dve.wait_ge(S["scores_ready"], T * t + s + 1)
                sv = ps_s[s % 2][:, :].rearrange("p (u c) -> p u c", u=GB)[:, :, 0:PB * K].rearrange("p u (i k) -> p u k i", i=PB)
                dve.tensor_reduce(out=fs[:, s % 2, :, :], in_=sv, axis=AX.X, op=ALU.max).then_inc(S["scores_folded"], 1)
                dve.wait_ge(S["scores_folded"], T * t + s + 3)
                link(dve.tensor_reduce(out=mx[:, s % 2, :], in_=fs[:, s % 2, :, :], axis=AX.X, op=ALU.max))
                dve.tensor_tensor(e[:, s % 3, :, :], fs[:, s % 2, :, :], mx[:, s % 2, :].unsqueeze(2).to_broadcast([P, GB, K]),
                                  ALU.subtract).then_inc(S["shifted"], 1)

            def scale(t, s):
                dve.wait_ge(S["exp_ready"], T * t + s + 1)
                link(dve.tensor_reduce(out=zs[:, s % 2, :], in_=e[:, s % 3, :, :], axis=AX.X, op=ALU.add))
                link(dve.reciprocal(zs[:, s % 2, :], zs[:, s % 2, :]))
                dve.tensor_tensor(oz[:, s % 2, :, :], zs[:, s % 2, :].unsqueeze(2).to_broadcast([P, GB, PB]),
                                  own[:, :].unsqueeze(1).to_broadcast([P, GB, PB]), ALU.mult).then_inc(S["own_scaled"], 1)

            def flip(t, s):
                dve.wait_ge(S["probs_ready"], T * t + s + 1)
                if s >= 2:
                    dve.wait_ge(S["h_ready"], T * t + s - 1)
                dve.transpose(pt[:, s % 2, :], pn[:, s % 2, :, :].rearrange("p u c -> p (u c)")).then_inc(S["pt_ready"], 1)

            def window_max(t, s):
                l, g, cgs, jg, jp = layer(s)
                dve.wait_ge(S["h_copied"], T * t + s + 3)
                dve.tensor_reduce(out=hm[l][:, g * jp:(g + 1) * jp], in_=hs[:, s % 2, 0:jp * K].rearrange("p (i k) -> p i k", k=K),
                                  axis=AX.X, op=ALU.max).then_inc(S["h_max_done"], 1)

            def iteration(t, final=True, second=True, first=True, ahead=True):
                chain[0] = Chain(dve, s_d)
                on = lambda s: 0 <= s < T and (first if s in L0 else second)
                for s in range(T + 6):
                    if on(s):
                        fold(t, s)
                    if on(s - 1):
                        scale(t, s - 1)
                    if on(s - 2):
                        flip(t, s - 2)
                    if on(s - 5):
                        window_max(t, s - 5)
                    if s == 1 and final:
                        variances(t, (1, 0))
                    if s == 2 and final:
                        normalise(t, (1, 0))
                    if s == 1 and second:
                        one_hot(1, 0)
                        one_hot(1, 1)
                    if s == 3 and second:
                        one_hot(1, 2)
                        one_hot(1, 3)
                    if s == 4 and second:
                        split(1, t)
                    if s == 4 and final:
                        variance3(t)
                    if s == 5 and final:
                        output(t)
                    if s == 6 and ahead:
                        begin(t + 2)
                        if second:
                            dve.wait_ge(L["sorted_in_psum"][1], t)
                        compare(0)
                    if s == 7 and ahead:
                        compare(1)
                    if s == 8 and second:
                        differences(1, t)
                    if s in (9, 10) and second:
                        block_diagonal(1, 2 * (s - 9))
                        block_diagonal(1, 2 * (s - 9) + 1)
                    if s in (11, 12) and ahead:
                        compare(s - 9)
                    if s == 13 and ahead:
                        ranks(t)
                    if s in (14, 15) and ahead:
                        one_hot(0, 2 * (s - 14))
                        one_hot(0, 2 * (s - 14) + 1)
                    if s == 15 and ahead:
                        split(0, t + 2)
                    if s == 19 and ahead:
                        dve.wait_ge(S["y_ready"], YU * t + NG)
                        differences(0, t + 2)
                    if s in (20, 21) and ahead:
                        block_diagonal(0, 2 * (s - 20))
                        block_diagonal(0, 2 * (s - 20) + 1)

            def skip(l):
                for n in ("scores_folded", "shifted", "own_scaled", "pt_ready", "h_max_done"):
                    dve.sem_inc(S[n], NG)

            for n in ("scores_folded", "y_copied", "h_copied", "h_max_done", "pt_ready"):
                dve.sem_inc(S[n], 2)
            dve.sem_inc(S["out_ready"], 1)
            dve.sem_inc(S["out_stored"], 16)
            dve.wait_ge(S["zero_ready"], GH)
            chain[0] = Chain(dve, s_d)
            begin(1)
            for i in range(NC):
                compare(i)
            link(dve.memset(rank[0][:, :, :], 0.0))
            ranks(-1)
            for c in range(METHODS):
                one_hot(0, c)
            split(0, 1)
            differences(0, 1)
            for h in range(GH):
                block_diagonal(0, h)
            dve.sem_clear(s_d)
            iteration(0, final=False, second=False)
            all_pass(dve, "passed_first")
            skip(1)
            with dve.Fori(1, nb) as t:
                dve.sem_clear(s_d)
                sum_up(t)
                iteration(t)
            sum_up(nb)
            all_pass(dve, "passed_last")
            skip(0)
            dve.sem_clear(s_d)
            iteration(nb, first=False, ahead=False)
            link(dve.memset(f02[:, :], 0.0))
            dve.wait_ge(S["h_summed"], T * (nb + 1))
            dve.tensor_reduce(out=s12[:, 1, :], in_=sums[1][:, :, :], axis=AX.X, op=ALU.add).then_inc(S["s12_ready"], 1)
            variances(nb + 1, (1,))
            normalise(nb + 1, (1,))
            variance3(nb + 1)
            output(nb + 1)


def constants(nc, ctx):
    m = Memory(nc, ctx)
    return {
        "ident": m.sb("ident", [P, P]),
        "iota": m.sb("iota", [P, N], F16),
        "tri": m.sb("tri", [P, P]),
        "ind": m.sb("ind", [P, P], BF16),
        "off": m.sb("off", [P, 512], BF16),
        "same": [m.sb(f"same{l}", [P, P]) for l in range(2)],
        "gather": m.sb("gather", [P, 4, P]),
        "w3": m.sb("w3", [P, 4, C]),
        "w3f": m.sb("w3f", [C, C]),
        "keys": m.sb("keycols", [P, NC, METHODS, B + 1]),
        "wc": [m.sb(f"wc{l}", [P, 2, 2, OUTC[l]], F16) for l in range(2)],
        "bias": [m.sb(f"bias{l}", [P, 1]) for l in range(2)],
    }


def layernorm_transposed(dve, pool_hook, link, src, mv, stats, veps, rstd_ready, rstd, dst, var_ready):
    for t in range(NT):
        link(dve.bn_stats(out=stats[:, t, :], in_=src[:, t, :]))
        link(dve.bn_aggr(out=mv[:, t, :], in_=stats[:, t, :]))
        dve.tensor_scalar(out=veps[:, t:t + 1], in0=mv[:, t, 1:2], scalar1=LN_EPS, scalar2=None,
                          op0=ALU.add).then_inc(var_ready, 1)
    for t in range(NT):
        dve.wait_ge(rstd_ready, t + 1)
        dve.tensor_scalar(out=dst[:, t, :], in0=src[:, t, :], scalar1=mv[:, t, 0:1], scalar2=rstd[:, t:t + 1],
                          op0=ALU.subtract, op1=ALU.mult).then_inc(pool_hook, 1)


def self_attention(nc, a, keep, scratch):
    H, DN, DQ, DV = 32, 128, 192, 128
    HS = 4
    PAIRS = H // HS // 2
    HC = HS * DN
    SCALE = float(DQ) ** -0.5
    with ExitStack() as ctx:
        m = Memory(nc, ctx)
        hn = m.sb("a_hn", [P, NT, N])
        hT = m.sb("a_hT", [P, NC, TOK])
        stats = m.sb("a_stats", [P, NT, 6])
        mv = m.sb("a_mv", [P, NT, 2])
        veps = m.sb("a_veps", [P, NT])
        rstd = m.sb("a_rstd", [P, NT])
        mhalf = m.sb("a_mhalf", [P, NT])
        wq = m.sb("a_wq", [P, 2, NC, HS, DN])
        wk = m.sb("a_wk", [P, 2, NC, HC])
        wv = m.sb("a_wv", [P, 2, NC, HC])
        wo = m.sb("a_wo", [P, 2, HS, N])
        qT = m.sb("a_qT", [P, HS, TOK])
        kT = m.sb("a_kT", [P, HS, TOK])
        v = m.sb("a_v", [P, NT, HC])
        sc = m.sb("a_sc", [P, HS * NT, C])
        mx = m.sb("a_mx", [P, HS * NT])
        zs = m.sb("a_zs", [P, HS * NT])
        pbd = m.sb("a_pbd", [P, HS, NT, P])
        oT = m.sb("a_oT", [P, HS, TOK])
        causal = m.sb("a_causal", [P, C])
        x1, x2 = keep["x1"], keep["x2"]
        ps_out = [m.ps(f"a_out{t}") for t in range(NT)]
        ps_w = [m.ps(f"a_proj{i}") for i in range(2)]
        ps_s = m.ps("a_scores")
        ps_o = m.ps("a_heads")

        S = {n: m.sem("a_" + n) for n in (
            "x_loaded", "var_ready", "rstd_ready", "hn_ready", "hT_in_psum", "hT_ready", "causal_ready", "w_loaded_even",
            "w_loaded_odd", "w_used", "proj_ready", "proj_copied", "scores_ready", "scores_used", "shifted", "exp_ready", "pt_ready",
            "heads_ready", "heads_copied", "out_ready", "zero_ready")}
        loaded = (S["w_loaded_even"], S["w_loaded_odd"])
        s_d, s_g = m.sem("self_dve_step"), m.sem("self_pool_step")
        block = ctx.enter_context(nc.Block())
        NP_ = 2 * HS + NT

        @block.sync
        def _(sp):
            for t in range(NT):
                sp.dma_start(x1[:, t, :], scratch["x1"][C + t * P:C + (t + 1) * P, :]).then_inc(S["x_loaded"], 16)
            wq_d = a["L0_attn_wq"].rearrange("(k p) (s h d) -> s p k h d", p=P, h=HS, d=DQ)
            wk_d = a["L0_attn_wkv"][:, 0:H * DN].rearrange("(k p) (s d) -> s p k d", p=P, d=HC)
            wv_d = a["L0_attn_wkv"][:, H * DN:H * (DN + DV)].rearrange("(k p) (s d) -> s p k d", p=P, d=HC)
            wo_d = a["L0_attn_wo"].rearrange("(s h p) n -> s p h n", p=P, h=HS)
            with sp.Fori(0, PAIRS) as i:
                for r in range(2):
                    sp.wait_ge(S["w_used"], 2 * i + r + 1)
                    for k in range(NC):
                        sp.dma_start(wq[:, r, k], wq_d[2 * i + r][:, k, :, 0:DN]).then_inc(loaded[r], 16)
                    sp.dma_start(wk[:, r], wk_d[2 * i + r]).then_inc(loaded[r], 16)
                    sp.dma_start(wv[:, r], wv_d[2 * i + r]).then_inc(loaded[r], 16)
                    sp.dma_start(wo[:, r], wo_d[2 * i + r]).then_inc(loaded[r], 16)

        @block.gpsimd
        def _(pool):
            link = Chain(pool, s_g)
            link(pool.memset(mhalf[:, :], -0.5))
            link(pool.memset(causal[:, :], 0.0))
            for r in range(P // C):
                last = pool.affine_select(out=causal[r * C:(r + 1) * C, :], in_=causal[r * C:(r + 1) * C, :], compare_op=ALU.is_ge,
                                          fill=NEG, base=0, pattern=[[-1, C]], channel_multiplier=1)
            last.then_inc(S["causal_ready"], 1)
            pool.wait_ge(S["causal_ready"], 1)
            pool.memset(pbd[:, :, :, :], 0.0).then_inc(S["zero_ready"], 1)
            for t in range(NT):
                pool.wait_ge(S["var_ready"], t + 1)
                pool.tensor_tensor(rstd[:, t:t + 1], veps[:, t:t + 1], mhalf[:, t:t + 1], ALU.pow).then_inc(S["rstd_ready"], 1)

        @block.tensor
        def _(pe):
            for k in range(NC):
                for t in range(NT):
                    pe.wait_ge(S["hn_ready"], t + 1)
                    last = pe.transpose(ps_out[k][:, t * P:(t + 1) * P], hn[:, t, k * P:(k + 1) * P], keep["ident"][:, :])
                last.then_inc(S["hT_in_psum"], 1)
            pe.wait_ge(S["hT_ready"], NC)
            for t in range(NT):
                pe.matmul(ps_out[t][:, :], keep["ident"][:, :], x1[:, t, :], start=True, stop=False, skip_group_check=True)
            with pe.Fori(0, PAIRS) as i:
                for r in range(2):
                    pe.wait_ge(loaded[r], 7 * 16 * i + 7 * 16)
                    for w in range(2 * HS):
                        h = w % HS
                        pe.wait_ge(S["proj_copied"], NP_ * (2 * i + r) + w + 1)
                        for k in range(NC):
                            lhs = wq[:, r, k, h, :] if w < HS else wk[:, r, k, h * DN:(h + 1) * DN]
                            last = pe.matmul(ps_w[w % 2][:, :], lhs, hT[:, k, :], start=k == 0, stop=k == NC - 1)
                        last.then_inc(S["proj_ready"], 1)
                    pe.wait_ge(S["proj_copied"], NP_ * (2 * i + r) + 2 * HS + 2)
                    pe.wait_ge(S["scores_used"], 2 * i + r + 1)
                    for h in range(HS):
                        for t in range(NT):
                            for q in range(P // C):
                                tok = slice(t * P + q * C, t * P + q * C + C)
                                at = (h * NT + t) * C
                                last = pe.matmul(ps_s[q * C:(q + 1) * C, at:at + C], qT[:, h, tok], kT[:, h, tok], start=True, stop=True)
                    last.then_inc(S["scores_ready"], 1)
                    for t in range(NT):
                        w = 2 * HS + t
                        pe.wait_ge(S["proj_copied"], NP_ * (2 * i + r) + w + 1)
                        for k in range(NC):
                            last = pe.matmul(ps_w[w % 2][:, :], hT[:, k, t * P:(t + 1) * P], wv[:, r, k, :], start=k == 0, stop=k == NC - 1)
                        last.then_inc(S["proj_ready"], 1)
                    pe.wait_ge(S["pt_ready"], 2 * i + r + 1)
                    pe.wait_ge(S["proj_copied"], NP_ * (2 * i + r) + NP_ + 2)
                    for h in range(HS):
                        pe.wait_ge(S["heads_copied"], HS * (2 * i + r) + h + 1)
                        for t in range(NT):
                            last = pe.matmul(ps_o[:, t * P:(t + 1) * P], v[:, t, h * DV:(h + 1) * DV], pbd[:, h, t, :], start=True, stop=True)
                        last.then_inc(S["heads_ready"], 1)
                    pe.wait_ge(S["heads_copied"], HS * (2 * i + r) + HS + 1)
                    for t in range(NT):
                        for h in range(HS):
                            last = pe.matmul(ps_out[t][:, :], oT[:, h, t * P:(t + 1) * P], wo[:, r, h, :], start=False, stop=False,
                                             skip_group_check=True)
                    last.then_inc(S["w_used"], 1)

        @block.scalar
        def _(act):
            with act.Fori(0, PAIRS) as i:
                for r in range(2):
                    def copy(w):
                        act.wait_ge(S["proj_ready"], NP_ * (2 * i + r) + w + 1)
                        dst = qT[:, w, :] if w < HS else kT[:, w - HS, :] if w < 2 * HS else v[:, w - 2 * HS, :]
                        act.activation(dst, ps_w[w % 2][:, :], ACT.Copy).then_inc(S["proj_copied"], 1)

                    for w in range(2 * HS):
                        copy(w)
                    act.wait_ge(S["shifted"], 2 * i + r + 1)
                    act.activation(sc[:, :, :], sc[:, :, :], ACT.Exp, scale=SCALE).then_inc(S["exp_ready"], 1)
                    for t in range(NT):
                        copy(2 * HS + t)
                    for h in range(HS):
                        act.wait_ge(S["heads_ready"], HS * (2 * i + r) + h + 1)
                        act.activation(oT[:, h, :], ps_o[:, :], ACT.Copy).then_inc(S["heads_copied"], 1)

        @block.vector
        def _(dve):
            dve.sem_inc(S["w_used"], 2)
            dve.sem_inc(S["proj_copied"], 2)
            dve.sem_inc(S["scores_used"], 1)
            dve.sem_inc(S["heads_copied"], 1)
            link = Chain(dve, s_d)
            dve.wait_ge(S["x_loaded"], 16 * NT)
            layernorm_transposed(dve, S["hn_ready"], link, x1, mv, stats, veps, S["rstd_ready"], rstd, hn, S["var_ready"])
            for k in range(NC):
                dve.wait_ge(S["hT_in_psum"], k + 1)
                dve.tensor_copy(hT[:, k, :], ps_out[k][:, :]).then_inc(S["hT_ready"], 1)
            dve.wait_ge(S["causal_ready"], 1)
            dve.wait_ge(S["zero_ready"], 1)
            G = HS * NT
            with dve.Fori(0, PAIRS) as i:
                dve.sem_clear(s_d)
                link = Chain(dve, s_d)
                for r in range(2):
                    dve.wait_ge(S["scores_ready"], 2 * i + r + 1)
                    sv = ps_s[:, :].rearrange("p (g c) -> p g c", g=G)
                    dve.tensor_tensor(sc[:, :, :], sv, causal[:, :].unsqueeze(1).to_broadcast([P, G, C]), ALU.add).then_inc(S["scores_used"], 1)
                    dve.wait_ge(S["scores_used"], 2 * i + r + 2)
                    link(dve.tensor_reduce(out=mx[:, :], in_=sc[:, :, :], axis=AX.X, op=ALU.max))
                    dve.tensor_tensor(sc[:, :, :], sc[:, :, :], mx[:, :].unsqueeze(2).to_broadcast([P, G, C]), ALU.subtract).then_inc(S["shifted"], 1)
                    dve.wait_ge(S["exp_ready"], 2 * i + r + 1)
                    link(dve.tensor_reduce(out=zs[:, :], in_=sc[:, :, :], axis=AX.X, op=ALU.add))
                    link(dve.reciprocal(zs[:, :], zs[:, :]))
                    link(dve.tensor_tensor(sc[:, :, :], sc[:, :, :], zs[:, :].unsqueeze(2).to_broadcast([P, G, C]), ALU.mult))
                    for q in range(P // C):
                        rows = slice(q * C, (q + 1) * C)
                        last = dve.transpose(pbd[rows, :, :, q * C:(q + 1) * C].rearrange("p h t c -> p (h t) c"), sc[rows, :, :])
                    last.then_inc(S["pt_ready"], 1)
            dve.wait_ge(S["w_used"], 2 * PAIRS + 2)
            for t in range(NT):
                last = dve.tensor_copy(x2[:, t, :], ps_out[t][:, :])
            last.then_inc(S["out_ready"], 1)
            dve.wait_ge(S["out_ready"], 1)


def experts(nc, a, keep, scratch, out):
    E, GROUPS, INTER = 16, 4, 128
    with ExitStack() as ctx:
        m = Memory(nc, ctx)
        hn = m.sb("e_hn", [P, NT, N])
        hT = m.sb("e_hT", [P, NC, TOK])
        stats = m.sb("e_stats", [P, NT, 6])
        mv = m.sb("e_mv", [P, NT, 2])
        veps = m.sb("e_veps", [P, NT])
        rstd = m.sb("e_rstd", [P, NT])
        mhalf = m.sb("e_mhalf", [P, NT])
        rw = m.sb("e_rw", [P, NC, E])
        rb = m.sb("e_rb", [P, E])
        rbias = m.sb("e_rbias", [P, E])
        lg = m.sb("e_lg", [P, NT, E])
        gmax = m.sb("e_gmax", [P, NT, GROUPS])
        first = m.sb("e_first", [P, E])
        cand = m.sb("e_cand", [P, NT, E])
        pick = m.sb("e_pick", [P, NT, E])
        both = m.sb("e_both", [P, NT, E])
        gkeep = m.sb("e_gkeep", [P, NT, GROUPS])
        left = m.sb("e_left", [P, NT, E])
        t1 = m.sb("e_t1", [P, NT])
        t2 = m.sb("e_t2", [P, NT])
        gate = m.sb("e_gate", [P, NT, E + 1])
        gateT = m.sb("e_gateT", [E + 1, TOK])
        b3 = m.sb("e_b3", [E + 1, N])
        w1 = m.sb("e_w1", [P, 2, NC, INTER])
        w2 = m.sb("e_w2", [P, 2, NC, INTER])
        w3 = m.sb("e_w3", [P, 2, N])
        b1 = m.sb("e_b1", [P, 2, 1])
        b2 = m.sb("e_b2", [P, 2, 1])
        gb = m.sb("e_gb", [P, 2, TOK])
        up = m.sb("e_up", [P, 2, TOK])
        hh = m.sb("e_hh", [P, 2, TOK])
        y = m.sb("e_y", [P, NT, N])
        x2 = keep["x2"]
        ps_y = [m.ps(f"e_y{t}") for t in range(NT)]
        ps_u = [m.ps(f"e_u{i}") for i in range(2)]
        ps_v = [m.ps(f"e_v{i}") for i in range(2)]
        S = {n: m.sem("e_" + n) for n in (
            "small_loaded", "var_ready", "rstd_ready", "hn_ready", "hT_in_psum", "hT_ready", "logits_ready", "first_ready",
            "shifted", "exp_ready", "gate_ready", "gateT_in_psum", "gateT_ready", "gateT_stored", "w_loaded_even", "w_loaded_odd", "h_ready",
            "silu_ready", "gated_ready", "down_done", "bias_done", "y_ready", "stored")}
        loaded = (S["w_loaded_even"], S["w_loaded_odd"])
        s_d, s_g = m.sem("moe_dve_step"), m.sem("moe_pool_step")
        block = ctx.enter_context(nc.Block())
        NL = 6

        def bcast_rows(src):
            return bass.AP(src.tensor, src.offset, [[0, P]] + [list(k) for k in src.ap])

        @block.sync
        def _(sp):
            sp.dma_start(rw[:, :, :], a["L0_ffn_router_w"].rearrange("(k p) e -> p k e", p=P)).then_inc(S["small_loaded"], 16)
            sp.dma_start(rb[:, :], bcast_rows(a["L0_ffn_router_b"])).then_inc(S["small_loaded"], 16)
            sp.dma_start(rbias[:, :], bcast_rows(a["L0_ffn_router_bias"])).then_inc(S["small_loaded"], 16)
            sp.dma_start(b3[0:E, :], a["L0_ffn_eb3"]).then_inc(S["small_loaded"], 16)
            sp.dma_start(b3[E:E + 1, :], a["L0_ffn_sb3"].rearrange("(u n) -> u n", u=1)).then_inc(S["small_loaded"], 16)
            sp.wait_ge(S["gateT_ready"], 1)
            sp.dma_start(scratch["gates"], gateT[:, :]).then_inc(S["gateT_stored"], 16)
            sp.wait_ge(S["gateT_stored"], 16)

            def load(r, count, w1s, w2s, w3s, b1s, b2s, gs):
                sp.wait_ge(S["down_done"], count + 1)
                sp.dma_start(w1[:, r], w1s).then_inc(loaded[r], 16)
                sp.dma_start(w2[:, r], w2s).then_inc(loaded[r], 16)
                sp.dma_start(w3[:, r], w3s).then_inc(loaded[r], 16)
                with nc.allow_non_contiguous_dma(reason="a bias column"):
                    sp.dma_start(b1[:, r], b1s).then_inc(loaded[r], 16)
                    sp.dma_start(b2[:, r], b2s).then_inc(loaded[r], 16)
                sp.dma_start(gb[:, r], bcast_rows(gs)).then_inc(loaded[r], 16)

            col = lambda s: s.rearrange("(p u) -> p u", u=1)
            with sp.Fori(0, E // 2) as i:
                for r in range(2):
                    e = 2 * i + r
                    load(r, e, a["L0_ffn_ew1"].rearrange("e (k p) n -> e p k n", p=P)[e],
                         a["L0_ffn_ew2"].rearrange("e (k p) n -> e p k n", p=P)[e], a["L0_ffn_ew3"][e],
                         col(a["L0_ffn_eb1"][e]), col(a["L0_ffn_eb2"][e]), scratch["gates"][e])
            for r in range(2):
                cols = slice(r * INTER, (r + 1) * INTER)
                load(r, E + r, a["L0_ffn_sw1"][:, cols].rearrange("(k p) n -> p k n", p=P),
                     a["L0_ffn_sw2"][:, cols].rearrange("(k p) n -> p k n", p=P), a["L0_ffn_sw3"][cols, :],
                     col(a["L0_ffn_sb1"][cols]), col(a["L0_ffn_sb2"][cols]), scratch["gates"][E])
            for t in range(NT):
                sp.wait_ge(S["y_ready"], t + 1)
                sp.dma_start(out.rearrange("b c n -> (b c) n")[t * P:(t + 1) * P, :], y[:, t, :]).then_inc(S["stored"], 16)
            sp.wait_ge(S["stored"], 16 * NT)

        @block.gpsimd
        def _(pool):
            link = Chain(pool, s_g)
            link(pool.memset(mhalf[:, :], -0.5))
            for t in range(NT):
                pool.wait_ge(S["var_ready"], t + 1)
                pool.tensor_tensor(rstd[:, t:t + 1], veps[:, t:t + 1], mhalf[:, t:t + 1], ALU.pow).then_inc(S["rstd_ready"], 1)
            pool.iota(first[:, :], pattern=[[-1, E]], base=E, channel_multiplier=0,
                      allow_small_or_imprecise_dtypes=True).then_inc(S["first_ready"], 1)

        @block.tensor
        def _(pe):
            for k in range(NC):
                for t in range(NT):
                    pe.wait_ge(S["hn_ready"], t + 1)
                    last = pe.transpose(ps_y[k][:, t * P:(t + 1) * P], hn[:, t, k * P:(k + 1) * P], keep["ident"][:, :])
                last.then_inc(S["hT_in_psum"], 1)
            pe.wait_ge(S["hT_ready"], NC)
            pe.wait_ge(S["small_loaded"], 80)
            for t in range(NT):
                for k in range(NC):
                    last = pe.matmul(ps_u[0][:, t * E:(t + 1) * E], hT[:, k, t * P:(t + 1) * P], rw[:, k, :], start=k == 0, stop=k == NC - 1)
            last.then_inc(S["logits_ready"], 1)
            pe.wait_ge(S["gate_ready"], 1)
            for t in range(NT):
                last = pe.transpose(ps_v[0][0:E + 1, t * P:(t + 1) * P], gate[:, t, :], keep["ident"][:, :])
            last.then_inc(S["gateT_in_psum"], 1)
            pe.wait_ge(S["gateT_ready"], 1)
            for t in range(NT):
                pe.matmul(ps_y[t][:, :], gateT[:, t * P:(t + 1) * P], b3[:, :], start=True, stop=False, skip_group_check=True)

            def expert(r, n, nl):
                pe.wait_ge(loaded[r], nl)
                pe.wait_ge(S["gated_ready"], n + 1)
                for w, ps in ((w1, ps_u[r]), (w2, ps_v[r])):
                    for k in range(NC):
                        last = pe.matmul(ps[:, :], w[:, r, k, :], hT[:, k, :], start=k == 0, stop=k == NC - 1)
                last.then_inc(S["h_ready"], 1)
                pe.wait_ge(S["gated_ready"], n + 3)
                for t in range(NT):
                    last = pe.matmul(ps_y[t][:, :], hh[:, r, t * P:(t + 1) * P], w3[:, r, :], start=False, stop=False, skip_group_check=True)
                last.then_inc(S["down_done"], 1)

            with pe.Fori(0, E // 2) as i:
                for r in range(2):
                    expert(r, 2 * i + r, 16 * NL * i + 16 * NL)
            for r in range(2):
                expert(r, E + r, 16 * NL * (E // 2 + 1))

        @block.scalar
        def _(act):
            act.wait_ge(S["shifted"], 1)
            act.activation(lg[:, :, :], lg[:, :, :], ACT.Exp).then_inc(S["exp_ready"], 1)

            def expert(r, n, nl):
                act.wait_ge(loaded[r], nl)
                act.wait_ge(S["h_ready"], n + 1)
                act.wait_ge(S["gated_ready"], n + 1)
                act.activation(up[:, r, :], ps_u[r][:, :], ACT.Silu, bias=b1[:, r, 0:1]).then_inc(S["silu_ready"], 1)

            with act.Fori(0, E // 2) as i:
                for r in range(2):
                    expert(r, 2 * i + r, 16 * NL * i + 16 * NL)
            for r in range(2):
                expert(r, E + r, 16 * NL * (E // 2 + 1))

        @block.vector
        def _(dve):
            dve.sem_inc(S["down_done"], 2)
            dve.sem_inc(S["gated_ready"], 2)
            link = Chain(dve, s_d)
            layernorm_transposed(dve, S["hn_ready"], link, x2, mv, stats, veps, S["rstd_ready"], rstd, hn, S["var_ready"])
            for k in range(NC):
                dve.wait_ge(S["hT_in_psum"], k + 1)
                dve.tensor_copy(hT[:, k, :], ps_y[k][:, :]).then_inc(S["hT_ready"], 1)
            dve.wait_ge(S["small_loaded"], 80)
            dve.wait_ge(S["logits_ready"], 1)
            wide = lambda v, n: v.unsqueeze(2).to_broadcast([P, NT, n])
            link(dve.tensor_tensor(lg[:, :, :], ps_u[0][:, 0:NT * E].rearrange("p (t e) -> p t e", t=NT),
                                   rb[:, :].unsqueeze(1).to_broadcast([P, NT, E]), ALU.add))
            link(dve.tensor_reduce(out=t1[:, :], in_=lg[:, :, :], axis=AX.X, op=ALU.max))
            dve.tensor_tensor(lg[:, :, :], lg[:, :, :], wide(t1[:, :], E), ALU.subtract).then_inc(S["shifted"], 1)
            dve.wait_ge(S["exp_ready"], 1)
            link(dve.tensor_reduce(out=t1[:, :], in_=lg[:, :, :], axis=AX.X, op=ALU.add))
            link(dve.reciprocal(t2[:, :], t1[:, :]))
            link(dve.tensor_tensor(lg[:, :, :], lg[:, :, :], wide(t2[:, :], E), ALU.mult))
            link(dve.tensor_tensor(lg[:, :, :], lg[:, :, :], rbias[:, :].unsqueeze(1).to_broadcast([P, NT, E]), ALU.add))
            dve.wait_ge(S["first_ready"], 1)

            def top1(vals, n, into):
                fr = first[:, 0:n].unsqueeze(1).to_broadcast([P, NT, n])
                link(dve.tensor_reduce(out=t1[:, :], in_=vals, axis=AX.X, op=ALU.max))
                link(dve.tensor_tensor(cand[:, :, 0:n], vals, wide(t1[:, :], n), ALU.is_equal))
                link(dve.tensor_tensor(cand[:, :, 0:n], cand[:, :, 0:n], fr, ALU.mult))
                link(dve.tensor_reduce(out=t2[:, :], in_=cand[:, :, 0:n], axis=AX.X, op=ALU.max))
                link(dve.tensor_tensor(into, cand[:, :, 0:n], wide(t2[:, :], n), ALU.is_equal))

            def top2(vals, n, into):
                top1(vals, n, into)
                link(dve.tensor_scalar(out=left[:, :, 0:n], in0=into, scalar1=2 * NEG, scalar2=None, op0=ALU.mult))
                link(dve.tensor_tensor(left[:, :, 0:n], left[:, :, 0:n], vals, ALU.add))
                top1(left[:, :, 0:n], n, pick[:, :, 0:n])
                link(dve.tensor_tensor(into, into, pick[:, :, 0:n], ALU.add))

            GE = E // GROUPS
            link(dve.tensor_reduce(out=gmax[:, :, :], in_=lg[:, :, :].rearrange("p t (g e) -> p t g e", g=GROUPS), axis=AX.X, op=ALU.max))
            top2(gmax[:, :, :], GROUPS, gkeep[:, :, :])
            kb = gkeep[:, :, :].unsqueeze(3).to_broadcast([P, NT, GROUPS, GE])
            bv = both[:, :, :].rearrange("p t (g e) -> p t g e", g=GROUPS)
            link(dve.tensor_tensor(bv, lg[:, :, :].rearrange("p t (g e) -> p t g e", g=GROUPS), kb, ALU.mult))
            link(dve.tensor_scalar(out=gkeep[:, :, :], in0=gkeep[:, :, :], scalar1=1.0, scalar2=-NEG, op0=ALU.subtract, op1=ALU.mult))
            link(dve.tensor_tensor(bv, bv, kb, ALU.add))
            link(dve.memset(gate[:, :, :], 1.0))
            top2(both[:, :, :], E, gate[:, :, 0:E])
            dve.tensor_tensor(gate[:, :, 0:E], gate[:, :, 0:E], lg[:, :, :], ALU.mult).then_inc(S["gate_ready"], 1)
            dve.wait_ge(S["gateT_in_psum"], 1)
            dve.tensor_copy(gateT[:, :], ps_v[0][0:E + 1, :]).then_inc(S["gateT_ready"], 1)

            def expert(r, n, nl, link):
                dve.wait_ge(loaded[r], nl)
                dve.wait_ge(S["h_ready"], n + 1)
                dve.wait_ge(S["silu_ready"], n + 1)
                dve.wait_ge(S["down_done"], n + 1)
                link(dve.scalar_tensor_tensor(out=hh[:, r, :], in0=ps_v[r][:, :], scalar=b2[:, r, 0:1], in1=up[:, r, :],
                                              op0=ALU.add, op1=ALU.mult))
                dve.tensor_tensor(hh[:, r, :], hh[:, r, :], gb[:, r, :], ALU.mult).then_inc(S["gated_ready"], 1)

            with dve.Fori(0, E // 2) as i:
                dve.sem_clear(s_d)
                link = Chain(dve, s_d)
                for r in range(2):
                    expert(r, 2 * i + r, 16 * NL * i + 16 * NL, link)
            for r in range(2):
                expert(r, E + r, 16 * NL * (E // 2 + 1), link)
            dve.wait_ge(S["down_done"], E + 2 + 2)
            for t in range(NT):
                dve.tensor_tensor(y[:, t, :], ps_y[t][:, :], x2[:, t, :], ALU.add).then_inc(S["y_ready"], 1)


_INS = ["x", "ctx_4096"] + ["L0_xattn_" + n for n in ("W_lin1", "b_lin1", "W_lin2", "b_lin2", "W_conv1", "W_conv2", "W_conv3")] + [
    "L0_attn_wq", "L0_attn_wkv", "L0_attn_wo"] + ["L0_ffn_" + n for n in (
        "router_w", "router_b", "router_bias", "ew1", "eb1", "ew2", "eb2", "ew3", "eb3", "sw1", "sb1", "sw2", "sb2", "sw3", "sb3")]


def build(nc, a, out):
    scratch = {
        "feats": nc.dram_tensor("feats_rows", [TOK + 2 * C, N], F32, kind="Internal").ap(),
        "keys": nc.dram_tensor("key_rows", [METHODS, B + 1, N], F32, kind="Internal").ap(),
        "x": nc.dram_tensor("x_rows", [TOK + C, N], F32, kind="Internal").ap(),
        "x1": nc.dram_tensor("x1_rows", [TOK + C, N], F32, kind="Internal").ap(),
        "gates": nc.dram_tensor("gate_rows", [17, TOK], F32, kind="Internal").ap(),
    }
    with ExitStack() as ctx:
        with ExitStack() as graph:
            keep = constants(nc, graph)
            prepare(nc, a, keep, scratch)
            cross_attention(nc, a, keep, scratch)
        m = Memory(nc, ctx)
        late = {n: m.sb("late_" + n, s) for n, s in (("x1", [P, NT, N]), ("x2", [P, NT, N]), ("ident", [P, P]))}
        identity(nc, late["ident"])
        self_attention(nc, a, late, scratch)
        experts(nc, a, late, scratch, out)


def identity(nc, t):
    with nc.semaphore("late_ident") as done, nc.Block() as block:
        @block.gpsimd
        def _(pool):
            pool.memset(t[:, :], 0.0).then_inc(done, 1)
            pool.wait_ge(done, 1)
            pool.affine_select(out=t[:, :], in_=t[:, :], compare_op=ALU.not_equal, fill=1.0, base=0,
                               pattern=[[-1, P]], channel_multiplier=1).then_inc(done, 1)
            pool.wait_ge(done, 2)


def kernel(**inputs):
    import numpy as np
    import concourse.bacc as bacc
    from concourse.bass_utils import run_bass_kernel_spmd

    nc = bacc.Bacc("TRN2", target_bir_lowering=False, num_devices=1)
    arrays, args = {}, {}
    for name in _INS:
        arrays[name] = np.ascontiguousarray(inputs[name])
        args[name] = nc.dram_tensor(name, arrays[name].shape, F32, kind="ExternalInput").ap()
    out = nc.dram_tensor("out", (B, C, N), F32, kind="ExternalOutput").ap()
    build(nc, args, out)
    r = run_bass_kernel_spmd(nc, [arrays], core_ids=[0])
    return r.results[0]["out"]
```

```python
from contextlib import ExitStack

import concourse.bass as bass
from concourse import mybir

F32 = mybir.dt.float32
F16 = mybir.dt.float16
BF16 = mybir.dt.bfloat16
I32 = mybir.dt.int32
ALU = mybir.AluOpType
ACT = mybir.ActivationFunctionType
AX = mybir.AxisListType

P = 128
B, C, N = 16, 32, 512
TOK = B * C
NT = TOK // P
NC = N // P
K = 10
METHODS = 4
BITS = 10
HD = 32
GH = C * METHODS // HD
PB = 3
NG = 11
GB = 16
NBLK = NG * GB
NPAD = NBLK * PB
PERM = ([2, 0, 3, 1], [1, 3, 0, 2])
OUTC = (32, 64)
LN_EPS = 1e-5
WSCALE = 256.0
NEG = -1e30


def window(t, start, dims):
    a = t[:, start:start + 1]
    return bass.AP(a.tensor, a.offset, [list(a.ap[0])] + [list(d) for d in dims])


class Chain:

    def __init__(self, eng, sem):
        self.eng, self.sem, self.n = eng, sem, 0

    def __call__(self, ins):
        self.n += 1
        ins.then_inc(self.sem, 1)
        self.eng.wait_ge(self.sem, self.n)

    def beside(self, ins):
        self.n += 1
        ins.then_inc(self.sem, 1)
        if self.n > 1:
            self.eng.wait_ge(self.sem, self.n - 1)

    def settle(self):
        self.eng.wait_ge(self.sem, self.n)


class Memory:
    def __init__(self, nc, ctx):
        self.nc, self.ctx = nc, ctx

    def sb(self, name, shape, dt=F32):
        return self.ctx.enter_context(self.nc.sbuf_tensor(name, shape, dt))

    def ps(self, name):
        return self.ctx.enter_context(self.nc.psum_tensor(name, [P, 512], F32))

    def sem(self, name):
        return self.ctx.enter_context(self.nc.semaphore(name))


def prepare(nc, a, keep, scratch):
    with ExitStack() as ctx:
        m = Memory(nc, ctx)
        xt = m.sb("p_x", [P, NT, N])
        ft = m.sb("p_f", [P, NT, N])
        stats = m.sb("p_stats", [P, NT, 6])
        mv = m.sb("p_mv", [P, NT, 2])
        veps = m.sb("p_veps", [P, NT])
        rstd = m.sb("p_rstd", [P, NT])
        mhalf = m.sb("p_mhalf", [P, NT])
        R48 = 3 * B
        co = m.sb("p_co", [R48, N])
        cmin = m.sb("p_cmin", [R48, 1])
        cmax = m.sb("p_cmax", [R48, 1])
        top = m.sb("p_top", [R48, 1])
        cscale = m.sb("p_cscale", [R48, 1])
        dq = m.sb("p_dq", [R48, 10])
        qv = m.sb("p_qv", [R48, N])
        qi = m.sb("p_qi", [R48, N], I32)
        qf = m.sb("p_qf", [R48, N])
        gt = m.sb("p_gt", [R48, N])
        X = m.sb("p_X", [P, 3, NC, 2, B], I32)
        Y = m.sb("p_Y", [P, 3, NC, 2, B], I32)
        mk3 = m.sb("p_mk3", [P, 3, NC, 2, B], I32)
        mn2 = m.sb("p_mn2", [P, 2, NC, 2, B], I32)
        mn = m.sb("p_mn", [P, NC, 2, B], I32)
        uu = m.sb("p_uu", [P, NC, 2, B], I32)
        tt = m.sb("p_tt", [P, NC, 2, B], I32)
        sp = m.sb("p_sp", [P, 3, NC, 2, B], I32)
        kt = m.sb("p_kt", [P, NC, METHODS, B], I32)
        kr = m.sb("p_kr", [METHODS * B, N])
        wl = [m.sb(f"p_wl{i}", [64, 256]) for i in range(2)]
        wr = [m.sb(f"p_wr{i}", [64, 2, GH, METHODS, 8]) for i in range(2)]
        wct = [m.sb(f"p_wct{i}", [64, P]) for i in range(2)]
        bl = [m.sb(f"p_bl{i}", [64, 1]) for i in range(2)]
        wf = m.sb("p_wf", [P, 2, 2, 64])
        ps_q = m.ps("pp_q")
        ps_k = m.ps("pp_k")
        ps_w = m.ps("pp_w")

        s_x = m.sem("x_loaded")
        s_c = m.sem("coords_loaded")
        s_w = m.sem("small_weights_loaded")
        s_feat = m.sem("features_ready")
        s_fout = m.sem("features_stored")
        s_var = m.sem("variance_ready")
        s_rstd = m.sem("rstd_ready")
        s_id = m.sem("identity_ready")
        s_q = m.sem("quantised")
        s_qt = m.sem("coords_transposed")
        s_key = m.sem("keys_ready")
        s_kt = m.sem("keys_transposed")
        s_kr = m.sem("key_rows_ready")
        s_wr = m.sem("weights_reordered")
        s_wp = m.sem("weight_product_ready")
        s_d = m.sem("prepare_dve_step")
        s_g = m.sem("prepare_pool_step")
        block = ctx.enter_context(nc.Block())

        @block.sync
        def _(sp_):
            for c in range(3):
                sp_.dma_start(co[c * B:(c + 1) * B, :], a["ctx_4096"][:, c, :]).then_inc(s_c, 16)
            for t in range(NT):
                sp_.dma_start(xt[:, t, :], a["x"].rearrange("b c n -> (b c) n")[t * P:(t + 1) * P, :]).then_inc(s_x, 16)
            for t in range(NT):
                sp_.wait_ge(s_feat, t + 1)
                sp_.dma_start(scratch["feats"][C + t * P:C + (t + 1) * P, :], ft[:, t, :]).then_inc(s_fout, 16)
                sp_.dma_start(scratch["x"][C + t * P:C + (t + 1) * P, :], xt[:, t, :]).then_inc(s_fout, 16)
            sp_.dma_start(scratch["feats"][0:C, :], ft[0:C, 0, :]).then_inc(s_fout, 16)
            sp_.dma_start(scratch["feats"][C + TOK:2 * C + TOK, :], ft[0:C, 0, :]).then_inc(s_fout, 16)
            sp_.dma_start(scratch["x"][0:C, :], xt[0:C, 0, :]).then_inc(s_fout, 16)
            sp_.wait_ge(s_kr, 1)
            for c in range(METHODS):
                sp_.dma_start(scratch["keys"][c, 0:B], kr[c * B:(c + 1) * B, :]).then_inc(s_fout, 16)
                sp_.dma_start(scratch["keys"][c, B:B + 1], kr[c * B:c * B + 1, :]).then_inc(s_fout, 16)
            sp_.wait_ge(s_fout, 16 * (2 * NT + 3 + 2 * METHODS))

        @block.gpsimd
        def _(pool):
            link = Chain(pool, s_g)
            link(pool.memset(keep["ident"][:, :], 0.0))
            pool.affine_select(out=keep["ident"][:, :], in_=keep["ident"][:, :], compare_op=ALU.not_equal, fill=1.0,
                               base=0, pattern=[[-1, P]], channel_multiplier=1).then_inc(s_id, 1)
            link(pool.memset(mhalf[:, :], -0.5))
            for t in range(NT):
                pool.wait_ge(s_var, t + 1)
                pool.tensor_tensor(rstd[:, t:t + 1], veps[:, t:t + 1], mhalf[:, t:t + 1], ALU.pow).then_inc(s_rstd, 1)
            pool.iota(keep["iota"][:, :], pattern=[[1, N]], base=0, channel_multiplier=0,
                      allow_small_or_imprecise_dtypes=True)
            link(pool.memset(keep["tri"][:, :], 1.0))
            link(pool.affine_select(out=keep["tri"][:, :], in_=keep["tri"][:, :], compare_op=ALU.is_gt, fill=0.0,
                                    base=0, pattern=[[1, P]], channel_multiplier=-1))
            ind = keep["ind"]
            link(pool.memset(ind[:, :], 1.0))
            iv = ind[:, :].rearrange("p (h c) -> p h c", h=GH)
            link(pool.affine_select(out=iv, in_=iv, compare_op=ALU.is_ge, fill=0.0, base=0,
                                    pattern=[[0, GH], [1, 32]], channel_multiplier=-K))
            link(pool.affine_select(out=iv, in_=iv, compare_op=ALU.is_ge, fill=0.0, base=K - 1,
                                    pattern=[[0, GH], [-1, 32]], channel_multiplier=K))
            off = keep["off"]
            link(pool.memset(off[:, :], 0.0))
            ov = off[:, :].rearrange("p (u c) -> p u c", u=GB)
            link(pool.affine_select(out=ov, in_=ov, compare_op=ALU.is_ge, fill=NEG, base=0,
                                    pattern=[[0, GB], [1, 32]], channel_multiplier=-K))
            link(pool.affine_select(out=ov, in_=ov, compare_op=ALU.is_ge, fill=NEG, base=K - 1,
                                    pattern=[[0, GB], [-1, 32]], channel_multiplier=K))
            for l, o in enumerate(OUTC):
                t = keep["same"][l]
                link(pool.memset(t[:, :], 0.0))
                for d in range(-(P // o) + 1, P // o):
                    link(pool.affine_select(out=t[:, :], in_=t[:, :], compare_op=ALU.not_equal, fill=1.0,
                                            base=-d * o, pattern=[[-1, P]], channel_multiplier=1))
            for cg in range(4):
                t = keep["gather"][:, cg, :]
                link(pool.memset(t, 0.0))
                v = t.rearrange("p (h m c) -> p h m c", h=GH, m=METHODS)
                link(pool.affine_select(out=v, in_=v, compare_op=ALU.not_equal, fill=1.0, base=-32 * cg,
                                        pattern=[[-8, GH], [0, METHODS], [-1, 8]], channel_multiplier=1))
            for l in range(2):
                pool.memset(keep["dif"][l][:, :, :].rearrange("p j c -> p (j c)").bitcast(F32), 0.0)
                pool.memset(keep["dbd"][l][:, :, :, :].rearrange("p j h c -> p (j h c)").bitcast(F32), 0.0)

        @block.scalar
        def _(act):
            with nc.allow_non_contiguous_dma(reason="small weights, transposed once"):
                for i, (w, cv, b) in enumerate((("L0_xattn_W_lin1", "L0_xattn_W_conv1", "L0_xattn_b_lin1"),
                                                ("L0_xattn_W_lin2", "L0_xattn_W_conv2", "L0_xattn_b_lin2"))):
                    act.dma_start(wl[i][:, :], a[w]).then_inc(s_w, 16)
                    o = OUTC[i]
                    for r in range(P // o):
                        act.dma_start(wct[i][:, r * o:(r + 1) * o], a[cv].rearrange("o e -> e o")).then_inc(s_w, 16)
                    act.dma_start(bl[i][:, :], a[b].rearrange("(e u) -> e u", u=1)).then_inc(s_w, 16)
                act.wait_ge(s_d, 1)
                act.dma_start(keep["w3f"][:, :], a["L0_xattn_W_conv3"][:, 0:C].rearrange("o c -> c o")).then_inc(s_w, 16)
                for i in range(1, 2):
                    for h in range(GH):
                        act.dma_start(keep["w3"][32 * h:32 * h + 8, i, :],
                                      a["L0_xattn_W_conv3"][:, 32 * i + 8 * h:32 * i + 8 * h + 8].rearrange("o c -> c o")).then_inc(s_w, 16)
                for r in range(2):
                    act.dma_start(keep["w3"][64 * r:64 * r + 64, 2 + r, :],
                                  a["L0_xattn_W_conv3"][:, 64:128].rearrange("o c -> c o")).then_inc(s_w, 16)
            act.wait_ge(s_w, 16 * (4 + 2 + 4 + 4 + 1 + 2))

        @block.tensor
        def _(pe):
            pe.wait_ge(s_id, 1)
            pe.wait_ge(s_q, 1)
            for j in range(NC):
                last = pe.transpose(ps_q[:, j * 64:j * 64 + R48], qf[:, j * P:(j + 1) * P], keep["ident"][0:R48, 0:R48])
            last.then_inc(s_qt, 1)
            pe.wait_ge(s_key, 1)
            for j in range(NC):
                last = pe.transpose(ps_k[0:METHODS * B, j * P:(j + 1) * P],
                                    kt[:, j].rearrange("p m b -> p (m b)").bitcast(F32), keep["ident"][:, :])
            last.then_inc(s_kt, 1)
            pe.wait_ge(s_wr, 1)
            for i, o in enumerate(OUTC):
                for part in range(2):
                    at = (2 * i + part) * 64
                    pe.matmul(ps_w[:, at:at + o], wr[i][:, part].rearrange("e h m c -> e (h m c)"), wct[i][:, 0:o],
                              start=True, stop=True)
                last = pe.matmul(ps_w[:, 256 + i:257 + i], wct[i][:, :], bl[i][:, :], start=True, stop=True)
            last.then_inc(s_wp, 1)

        @block.vector
        def _(dve):
            link = Chain(dve, s_d)
            link(dve.memset(keep["w3"][:, :, :], 0.0))
            link(dve.memset(top[:, :], float(2 ** BITS - 1)))
            dve.wait_ge(s_c, 48)
            link(dve.tensor_reduce(out=cmin[:, :], in_=co[:, :], axis=AX.X, op=ALU.min))
            link(dve.tensor_reduce(out=cmax[:, :], in_=co[:, :], axis=AX.X, op=ALU.max))
            link(dve.tensor_scalar(out=cmax[:, :], in0=cmax[:, :], scalar1=cmin[:, 0:1], scalar2=1e-6,
                                   op0=ALU.subtract, op1=ALU.add))
            num, rng, inv, quo, rh, rl, qh, ql, res, prod = (dq[:, i:i + 1] for i in range(10))
            link(dve.tensor_copy(rng, cmax[:, :]))
            link(dve.reciprocal(inv, rng))
            link(dve.tensor_tensor(quo, top[:, :], inv, ALU.mult))
            for whole, high, low in ((rng, rh, rl), (quo, qh, ql)):
                link(dve.tensor_scalar(out=high.bitcast(I32), in0=whole.bitcast(I32), scalar1=-4096, scalar2=None,
                                       op0=ALU.bitwise_and))
                link(dve.tensor_tensor(low, whole, high, ALU.subtract))
            link(dve.tensor_copy(res, top[:, :]))
            for x_, y_ in ((qh, rh), (qh, rl), (ql, rh), (ql, rl)):
                link(dve.tensor_tensor(prod, x_, y_, ALU.mult))
                link(dve.tensor_tensor(res, res, prod, ALU.subtract))
            link(dve.tensor_tensor(res, res, inv, ALU.mult))
            link(dve.tensor_tensor(cscale[:, :], quo, res, ALU.add))
            link(dve.tensor_scalar(out=qv[:, :], in0=co[:, :], scalar1=cmin[:, 0:1], scalar2=cscale[:, 0:1],
                                   op0=ALU.subtract, op1=ALU.mult))
            link(dve.tensor_copy(qi[:, :], qv[:, :]))
            link(dve.tensor_copy(qf[:, :], qi[:, :]))
            link(dve.tensor_tensor(gt[:, :], qf[:, :], qv[:, :], ALU.is_gt))
            link(dve.tensor_tensor(qf[:, :], qf[:, :], gt[:, :], ALU.subtract))
            dve.tensor_scalar(out=qf[:, :], in0=qf[:, :], scalar1=0.0, scalar2=float(2 ** BITS - 1),
                              op0=ALU.max, op1=ALU.min).then_inc(s_q, 1)
            for t in range(NT):
                dve.wait_ge(s_x, 16 * NT)
                link(dve.bn_stats(out=stats[:, t, :], in_=xt[:, t, :]))
                link(dve.bn_aggr(out=mv[:, t, :], in_=stats[:, t, :]))
                dve.tensor_scalar(out=veps[:, t:t + 1], in0=mv[:, t, 1:2], scalar1=LN_EPS, scalar2=None,
                                  op0=ALU.add).then_inc(s_var, 1)
            for t in range(NT):
                dve.wait_ge(s_rstd, t + 1)
                dve.tensor_scalar(out=ft[:, t, :], in0=xt[:, t, :], scalar1=mv[:, t, 0:1], scalar2=rstd[:, t:t + 1],
                                  op0=ALU.subtract, op1=ALU.mult).then_inc(s_feat, 1)
            dve.wait_ge(s_qt, 1)
            for v, order in enumerate(((0, 1, 2), (1, 0, 2))):
                for i, c in enumerate(order):
                    src = ps_q[:, 0:NC * 64].rearrange("p (j q) -> p j q", j=NC)[:, :, c * B:(c + 1) * B]
                    link(dve.tensor_copy(X[:, i, :, v, :], src))

            def both(step):
                for v in range(2):
                    link.beside(step(v))

            def spread(src, dst):
                cur = src
                for sh, mask in ((16, 0x030000FF), (8, 0x0300F00F), (4, 0x030C30C3), (2, 0x09249249)):
                    both(lambda v: dve.scalar_tensor_tensor(out=dst[:, :, :, v, :], in0=cur[:, :, :, v, :], scalar=sh, in1=cur[:, :, :, v, :],
                                                            op0=ALU.logical_shift_left, op1=ALU.bitwise_or))
                    both(lambda v: dve.tensor_scalar(out=dst[:, :, :, v, :], in0=dst[:, :, :, v, :], scalar1=mask, scalar2=None,
                                                     op0=ALU.bitwise_and))
                    cur = dst

            def interleave(kind):
                both(lambda v: dve.scalar_tensor_tensor(out=uu[:, :, v, :], in0=sp[:, 0, :, v, :], scalar=2, in1=sp[:, 2, :, v, :],
                                                        op0=ALU.logical_shift_left, op1=ALU.bitwise_or))
                both(lambda v: dve.scalar_tensor_tensor(out=uu[:, :, v, :], in0=sp[:, 1, :, v, :], scalar=1, in1=uu[:, :, v, :],
                                                        op0=ALU.logical_shift_left, op1=ALU.bitwise_or))
                both(lambda v: dve.tensor_scalar(out=tt[:, :, v, :], in0=uu[:, :, v, :], scalar1=2, scalar2=31,
                                                 op0=ALU.logical_shift_left, op1=ALU.arith_shift_right))
                both(lambda v: dve.tensor_scalar(out=tt[:, :, v, :], in0=tt[:, :, v, :], scalar1=-1, scalar2=-1073741825,
                                                 op0=ALU.bitwise_xor, op1=ALU.bitwise_and))
                both(lambda v: dve.tensor_tensor(kt[:, :, 2 * kind + v, :], uu[:, :, v, :], tt[:, :, v, :], ALU.bitwise_xor))

            spread(X, sp)
            interleave(0)
            for q in range(BITS - 1, 0, -1):
                low = (1 << q) - 1
                both(lambda v: dve.tensor_scalar(out=mk3[:, :, :, v, :], in0=X[:, :, :, v, :], scalar1=31 - q, scalar2=31,
                                                 op0=ALU.logical_shift_left, op1=ALU.arith_shift_right))
                both(lambda v: dve.tensor_scalar(out=mn2[:, :, :, v, :], in0=mk3[:, 1:3, :, v, :], scalar1=-1, scalar2=low,
                                                 op0=ALU.bitwise_xor, op1=ALU.bitwise_and))
                for i in range(3):
                    if i:
                        both(lambda v: dve.tensor_tensor(uu[:, :, v, :], X[:, 0, :, v, :], X[:, i, :, v, :], ALU.bitwise_xor))
                        both(lambda v: dve.tensor_tensor(uu[:, :, v, :], uu[:, :, v, :], mn2[:, i - 1, :, v, :], ALU.bitwise_and))
                        both(lambda v: dve.tensor_tensor(X[:, 0:i + 1:i, :, v, :], X[:, 0:i + 1:i, :, v, :],
                                                         uu[:, :, v, :].unsqueeze(1).to_broadcast([P, 2, NC, B]), ALU.bitwise_xor))
                    both(lambda v: dve.scalar_tensor_tensor(out=X[:, 0, :, v, :], in0=mk3[:, i, :, v, :], scalar=low, in1=X[:, 0, :, v, :],
                                                            op0=ALU.bitwise_and, op1=ALU.bitwise_xor))
            for i in (1, 2):
                both(lambda v: dve.tensor_tensor(X[:, i, :, v, :], X[:, i, :, v, :], X[:, i - 1, :, v, :], ALU.bitwise_xor))
            link.settle()
            link(dve.memset(mn[:], 0))
            for q in range(BITS - 1, 0, -1):
                link.beside(dve.tensor_scalar(out=mk3[:, q % 3], in0=X[:, 2], scalar1=31 - q, scalar2=31,
                                              op0=ALU.logical_shift_left, op1=ALU.arith_shift_right))
                if q < BITS - 1:
                    link.beside(dve.scalar_tensor_tensor(out=mn[:], in0=mk3[:, (q + 1) % 3], scalar=(1 << (q + 1)) - 1, in1=mn[:],
                                                         op0=ALU.bitwise_and, op1=ALU.bitwise_xor))
            link.settle()
            link(dve.scalar_tensor_tensor(out=mn[:], in0=mk3[:, 1], scalar=1, in1=mn[:], op0=ALU.bitwise_and, op1=ALU.bitwise_xor))
            both(lambda v: dve.tensor_tensor(Y[:, :, :, v, :], X[:, :, :, v, :],
                                             mn[:, :, v, :].unsqueeze(1).to_broadcast([P, 3, NC, B]), ALU.bitwise_xor))
            spread(Y, sp)
            interleave(1)
            link.settle()
            dve.tensor_copy(keep["keys"][:, :, :, 0:B], kt[:].bitcast(F32)).then_inc(s_key, 1)
            link(dve.memset(keep["keys"][:, :, :, B:B + 1], 1.0))
            dve.wait_ge(s_kt, 1)
            dve.tensor_copy(kr[:, :], ps_k[0:METHODS * B, :]).then_inc(s_kr, 1)
            dve.wait_ge(s_w, 16 * (4 + 2 + 4 + 4 + 1 + 2))
            for i in range(2):
                for part in range(2):
                    src = wl[i][:, part * P:(part + 1) * P].rearrange("e (h c m) -> e h m c", h=GH, m=METHODS)
                    last = dve.tensor_copy(wr[i][:, part], src)
                    if i == part == 1:
                        last.then_inc(s_wr, 1)
            dve.wait_ge(s_wp, 1)
            for i, o in enumerate(OUTC):
                for part in range(2):
                    at = (2 * i + part) * 64
                    hi, lo = keep["wc"][i][:, part, 0, :], keep["wc"][i][:, part, 1, :]
                    link(dve.tensor_scalar(out=wf[:, i, part, 0:o], in0=ps_w[:, at:at + o], scalar1=WSCALE, scalar2=None,
                                           op0=ALU.mult))
                    link(dve.tensor_copy(hi, wf[:, i, part, 0:o]))
                    link(dve.tensor_tensor(lo, wf[:, i, part, 0:o], hi, ALU.subtract))
                link(dve.tensor_copy(keep["bias"][i][:, :], ps_w[:, 256 + i:257 + i]))


def cross_attention(nc, a, keep, scratch, nb=B):
    with ExitStack() as ctx:
        m = Memory(nc, ctx)
        T = 2 * NG
        krow = m.sb("krow", [P, METHODS, N])
        kcol = m.sb("kcol", [P, NC, METHODS])
        tie = m.sb("tie", [P, NC, METHODS, P], BF16)
        rank = [m.sb(f"rank{i}", [P, METHODS, NC]) for i in range(2)]
        perm = m.sb("perm", [P, METHODS, NC, N], BF16)
        ones = m.sb("ones", [P, 1], BF16)
        ctr = [m.sb(f"ctr{l}", [P, NPAD]) for l in range(2)]
        ctr16 = [m.sb(f"ctr16_{l}", [P, NPAD], F16) for l in range(2)]
        ftf = m.sb("ftf", [P, NC, C])
        ftr = m.sb("ftr", [P, NC, C])
        ft3 = m.sb("ft3", [P, NC, 3, C], BF16)
        srt = m.sb("srt", [P, NC, P])
        ext = m.sb("ext", [P, NPAD + 16])
        dif, dbd = keep["dif"], keep["dbd"]
        own = m.sb("own", [P, PB])
        fs = m.sb("fs", [P, 2, GB, K])
        mx = m.sb("mx", [P, 2, GB])
        e = m.sb("e", [P, 4, GB, K])
        zs = m.sb("zs", [P, 2, GB])
        iz = m.sb("iz", [P, 2, GB])
        oz = m.sb("oz", [P, 2, GB, PB])
        pn = m.sb("pn", [P, 2, GB, 32])
        pt = m.sb("pt", [P, 2, 512])
        ys = m.sb("ys", [P, 5, GB, 64])
        hs = m.sb("hs", [P, 2, 240])
        sq = m.sb("sq", [P, 240])
        hm = [m.sb(f"hm{l}", [P, NPAD * OUTC[l] // P]) for l in range(2)]
        fo = [m.sb(f"fo{l}", [P, NPAD * OUTC[l] // P]) for l in range(2)]
        sums = [m.sb(f"sums{l}", [P, 2, NG]) for l in range(2)]
        s12 = m.sb("s12", [P, 2, 2])
        st = [m.sb(f"st{l}", [P, 6]) for l in range(2)]
        mhalf = m.sb("mhalf", [P, 1])
        fin0 = m.sb("fin0", [C, N])
        xb = m.sb("xb", [C, N])
        h3a = m.sb("h3a", [P, N])
        h3 = m.sb("h3", [C, N])
        bst = m.sb("bst", [C, 6])
        bmv = m.sb("bmv", [C, 4])
        ps_s = [m.ps(f"ps_s{i}") for i in range(2)]
        ps_y = [m.ps(f"ps_y{i}") for i in range(2)]
        ps_h = [m.ps(f"ps_h{i}") for i in range(2)]
        ps_a = m.ps("ps_a")
        ps_b = m.ps("ps_b")

        names = (
            "keys_loaded", "input_loaded", "final_loaded", "out_stored",
            "scores_ready", "scores_folded", "max_ready", "shifted", "exp_ready", "y_ready", "y_copied", "sum_ready", "inverse_ready", "own_scaled", "probs_ready",
            "pt_ready", "h_ready", "h_copied", "h_summed", "h_max_done",
            "compared", "counted", "ranks_ready",
            "h3a_ready", "h3a_copied", "h3_ready", "h3_copied", "var3_ready", "rstd3_ready",
            "ctr1_in_psum", "ctr1_ready", "out_ready", "zero_ready",
            "passed_first", "passed_last")
        S = {n: m.sem("b_" + n) for n in names}
        L = {n: [m.sem(f"b{l}_{n}") for l in range(2)] for n in (
            "input_transposed", "split_ready", "perm_ready", "differences_ready", "edges_written", "sorted_in_psum", "sorted_copied", "sorted_t_in_psum",
            "ext_ready", "dif_ready", "ctr16_ready", "s12_ready", "totals_ready", "var_ready", "rstd_ready", "norm_ready")}
        s_d = m.sem("cross_dve_step")
        s_g = m.sem("cross_pool_step")
        block = ctx.enter_context(nc.Block())
        SC = float(HD) ** -0.5
        L0, L1 = range(0, NG), range(NG, T)

        PRODUCT, COPY, MAX = 4, 5, 6

        def layer(x):
            s = x % T
            l = s // NG
            cgs = P // OUTC[l]
            return l, s % NG, cgs, GB // cgs, GB // cgs * PB

        def yunit(x, u):
            s = x % T
            return (s if s < NG else NG + 2 * (s - NG) + u // 8) - (YU if x < 0 else 0)

        YU = 3 * NG

        def ring(size):
            rounds = T // size
            return [i for r in range(rounds) for i in range(size + (r < T % size))]

        E_RING, PT_RING, YS_RING = ring(3), ring(2), ring(PRODUCT)

        def all_pass(eng, name):
            eng.sem_inc(S[name], 1)
            eng.wait_ge(S[name], 4)


        @block.sync
        def _(sp):
            def rows(name, b):
                return scratch[name].rearrange("(b c) n -> b c n", c=C)[b]

            def load_ahead(t):
                src = scratch["keys"].rearrange("m b n -> b m n")[t + 1]
                if not (isinstance(t, int) and t < 0):
                    sp.wait_ge(S["ranks_ready"], t + 1)
                sp.dma_start(krow[:, :, :], bass.AP(src.tensor, src.offset, [[0, P]] + [list(k) for k in src.ap])).then_inc(S["keys_loaded"], 16)
                if not (isinstance(t, int) and t < 0):
                    sp.wait_ge(L["dif_ready"][0], t + 1)
                    sp.wait_ge(L["ctr16_ready"][0], t + 1)
                for h in range(GH):
                    src = scratch["feats"].rearrange("(b h c) n -> b h c n", h=GH, c=8)[t + 2, h]
                    sp.dma_start(ctr[0][32 * h:32 * h + 32, 0:N],
                                 bass.AP(src.tensor, src.offset, [[0, METHODS]] + [list(k) for k in src.ap])).then_inc(S["input_loaded"], 16)

            def load_final(t):
                sp.wait_ge(S["out_ready"], t)
                sp.dma_start(fin0[:, :], rows("feats", t - 1)).then_inc(S["final_loaded"], 16)
                sp.dma_start(xb[:, :], rows("x", t - 1)).then_inc(S["final_loaded"], 16)

            def store(t):
                sp.wait_ge(S["out_ready"], t + 1)
                sp.dma_start(rows("x1", t - 1), h3[:, :]).then_inc(S["out_stored"], 16)

            load_ahead(-1)
            load_ahead(0)
            with sp.Fori(1, nb) as t:
                load_final(t)
                load_ahead(t)
                store(t)
            load_final(nb)
            store(nb)
            load_final(nb + 1)
            store(nb + 1)
            sp.wait_ge(S["out_stored"], 16 * (nb + 2))

        @block.gpsimd
        def _(pool):
            link = Chain(pool, s_g)
            pool.memset(mhalf[:, :], -0.5)
            pool.memset(ctr[0][:, N:NPAD], 0.0)
            pool.memset(ctr[1][:, :], 0.0)
            pool.memset(ctr16[0][:, N:NPAD], 0.0)
            pool.memset(ctr16[1][:, :], 0.0)
            pool.memset(hm[1][:, :], 0.0)
            pool.memset(sums[1][:, :, :], 0.0)
            pool.memset(ext[:, :], 0.0)
            pool.memset(h3a[:, :], 0.0)
            pool.memset(ones[:, :], 1.0)
            pool.memset(pn[:, :, :, :], 0.0)
            pool.memset(pt[:, :, :], 0.0)
            pool.memset(ys[:, :, :, :], 0.0)
            pool.memset(hs[:, :, :], 0.0)
            pool.memset(e[:, :, :, :], 1.0)
            link(pool.memset(own[:, :], 1.0))
            for h in range(GH):
                ov = own[32 * h:32 * h + 32, :]
                link(pool.affine_select(out=ov, in_=ov, compare_op=ALU.is_ge, fill=0.0, base=0,
                                        pattern=[[-K, PB]], channel_multiplier=1))
                pool.affine_select(out=ov, in_=ov, compare_op=ALU.is_ge, fill=0.0, base=K - 1,
                                   pattern=[[K, PB]], channel_multiplier=-1).then_inc(S["zero_ready"], 1)
                pool.wait_ge(S["zero_ready"], h + 1)
            
            def norms(l, n):
                pool.wait_ge(L["var_ready"][l], n)
                pool.tensor_tensor(st[l][:, 4:5], st[l][:, 3:4], mhalf[:, :], ALU.pow).then_inc(L["rstd_ready"][l], 1)

            def differences(l, n, part, used):
                full, rest = N // PB, N % PB
                c3 = ctr[l][:, :].rearrange("p (j i) -> p j i", i=PB)
                d4 = dif[l][:, :, 0:PB * K].rearrange("p j (i k) -> p j i k", i=PB)
                if part == 0:
                    pool.wait_ge(L["ext_ready"][l], n)
                    if used is not None:
                        pool.wait_ge(S["y_ready"], used)
                    pool.tensor_tensor(d4[:, 0:2], window(ext, 5, [[0, 2], [0, PB], [1, K]]),
                                       c3[:, 0:2].unsqueeze(3).to_broadcast([P, 2, PB, K]), ALU.subtract).then_inc(L["edges_written"][l], 1)
                parts = 4
                lo, hi = max(2, full * part // parts), full * (part + 1) // parts
                pool.tensor_tensor(d4[:, lo:hi], window(ext, lo * PB, [[PB, hi - lo], [1, PB], [1, K]]),
                                   c3[:, lo:hi].unsqueeze(3).to_broadcast([P, hi - lo, PB, K]), ALU.subtract)
                if part == parts - 1:
                    last = pool.tensor_tensor(d4[:, full, 0:rest], window(ext, full * PB, [[1, rest], [1, K]]),
                                              c3[:, full, 0:rest].unsqueeze(2).to_broadcast([P, rest, K]), ALU.subtract)
                    pool.wait_ge(L["edges_written"][l], n)
                    for i in range(4):
                        w = K - 6 - i
                        last = pool.tensor_tensor(d4[:, i // PB, i % PB, 6 + i:K], ext[:, 10 + i:11 + i].to_broadcast([P, w]),
                                                  ctr[l][:, i:i + 1].to_broadcast([P, w]), ALU.subtract)
                    last.then_inc(L["differences_ready"][l], 1)

            def norm3(n):
                pool.wait_ge(S["var3_ready"], n)
                pool.tensor_tensor(bmv[:, 3:4], bmv[:, 2:3], mhalf[0:C, :], ALU.pow).then_inc(S["rstd3_ready"], 1)

            def shift(t, s):
                pool.wait_ge(S["max_ready"], T * t + s + 1)
                pool.tensor_tensor(e[:, E_RING[s], :, :], fs[:, s % 2, :, :], mx[:, s % 2, :].unsqueeze(2).to_broadcast([P, GB, K]),
                                  ALU.subtract).then_inc(S["shifted"], 1)

            def scale(t, x):
                pool.wait_ge(S["inverse_ready"], T * t + x + 1)
                pool.tensor_tensor(oz[:, x % 2, :, :], iz[:, x % 2, :].unsqueeze(2).to_broadcast([P, GB, PB]),
                                  own[:, :].unsqueeze(1).to_broadcast([P, GB, PB]), ALU.mult).then_inc(S["own_scaled"], 1)

            def expand(t, x):
                pool.wait_ge(S["own_scaled"], T * t + x + 1)
                pool.wait_ge(S["pt_ready"], T * t + x + 1)
                pool.tensor_tensor(pn[:, x % 2, :, 0:PB * K].rearrange("p u (i k) -> p u i k", i=PB),
                                   e[:, E_RING[x], :, :].unsqueeze(2).to_broadcast([P, GB, PB, K]),
                                   oz[:, x % 2, :, :].unsqueeze(3).to_broadcast([P, GB, PB, K]), ALU.mult).then_inc(S["probs_ready"], 1)

            def iteration(t, carry=True, first=True, second=True):
                on = lambda x: carry if x < 0 else first if x in L0 else second and x in L1
                for s in range(T if first else T + 1):
                    if s == MAX and not first:
                        all_pass(pool, "passed_last")
                        pool.sem_inc(S["shifted"], NG)
                        pool.sem_inc(S["own_scaled"], NG)
                        pool.sem_inc(S["probs_ready"], NG)
                    if s == 8 and second:
                        norms(1, t)
                    if s == 13 and second:
                        norm3(t)
                    if s == 18 and first:
                        norms(0, t + 1)
                    if s < T and on(s):
                        shift(t, s)
                    if on(s - 1):
                        scale(t, s - 1)
                        expand(t, s - 1)
                    for part in {6: (0, 1, 2), 7: (3,)}.get(s, ()) if second else ():
                        differences(1, t, part, YU * t)
                    for part in {15: (0,), 16: (1, 2), 17: (3,)}.get(s, ()) if first else ():
                        differences(0, t + 2, part, YU * t + NG)

            for part in range(4):
                differences(0, 1, part, None)
            iteration(0, carry=False, second=False)
            all_pass(pool, "passed_first")
            pool.sem_inc(S["shifted"], NG)
            pool.sem_inc(S["own_scaled"], NG - 1)
            pool.sem_inc(S["probs_ready"], NG - 1)
            with pool.Fori(1, nb) as t:
                iteration(t)
            iteration(nb, first=False)
            norms(1, nb + 1)
            norm3(nb + 1)

        @block.scalar
        def _(act):
            def ctr16_copy(l):
                act.activation(ctr16[l][:, 0:N], ctr[l][:, 0:N], ACT.Copy).then_inc(L["ctr16_ready"][l], 1)

            def sorted_copy(l, n):
                act.wait_ge(L["sorted_in_psum"][l], n)
                act.activation(srt[:, :, :], ps_b[:, :].rearrange("p (j q) -> p j q", j=NC), ACT.Copy).then_inc(L["sorted_copied"][l], 1)

            def ext_copy(l, n):
                act.wait_ge(L["sorted_t_in_psum"][l], n)
                act.activation(ext[:, 5:5 + N], ps_a[:, :], ACT.Copy)
                act.activation(ext[:, 5 + N:10 + N], ps_a[:, N - 1:N].to_broadcast([P, 5]), ACT.Copy).then_inc(L["ext_ready"][l], 1)

            def h3a_copy(t):
                act.wait_ge(S["h3a_ready"], t)
                act.activation(h3a[0:C, :], ps_b[0:C, :], ACT.Copy).then_inc(S["h3a_copied"], 1)

            def h3_copy(t):
                act.wait_ge(S["h3_ready"], t)
                act.wait_ge(S["out_stored"], 16 * t)
                act.activation(h3[:, :], ps_b[0:C, :], ACT.Copy).then_inc(S["h3_copied"], 1)

            def y_copy(t, s):
                l, g, cgs, jg, jp = layer(s)
                O = OUTC[l]
                units = 1 + l
                k = GB // units
                for u in range(units):
                    n = yunit(s, u * k)
                    act.wait_ge(S["y_ready"], YU * t + n + 1)
                    if u == 0 and not (isinstance(t, int) and t == 0 and s < PRODUCT):
                        act.wait_ge(S["h_ready"], T * t + s - PRODUCT + 1)
                    act.activation(ys[:, YS_RING[s], u * k:(u + 1) * k, 0:O],
                                   ps_y[n % 2][:, :].rearrange("p (u o) -> p u o", u=k), ACT.Copy).then_inc(S["y_copied"], 1)

            def exponentials(t, s):
                act.wait_ge(S["shifted"], T * t + s + 1)
                act.activation(e[:, E_RING[s], :, :], e[:, E_RING[s], :, :], ACT.Exp, scale=SC).then_inc(S["exp_ready"], 1)

            def h_copy(t, x):
                l, g, cgs, jg, jp = layer(x)
                act.wait_ge(S["h_ready"], T * t + x + 1)
                act.wait_ge(S["h_max_done"], T * t + x + 1)
                act.activation(hs[:, x % 2, 0:jp * K], ps_h[x % 2][:, 0:jp * K], ACT.Identity,
                               accum_out=sums[l][:, 0, g:g + 1]).then_inc(S["h_copied"], 1)
                act.wait_ge(S["h_copied"], T * t + x + 3)
                if not (isinstance(t, int) and t == 0 and x == 0):
                    act.wait_ge(S["h_summed"], T * t + x)
                act.activation(sq[:, 0:jp * K], hs[:, x % 2, 0:jp * K], ACT.Square,
                               accum_out=sums[l][:, 1, g:g + 1]).then_inc(S["h_summed"], 1)

            def iteration(t, carry=True, first=True, second=True):
                on = lambda x: carry if x < 0 else first if x in L0 else second and x in L1
                for s in range(T if first else T + COPY):
                    if s == MAX and not first:
                        all_pass(act, "passed_last")
                        skip(NG, NG, NG)
                    if s == 0 and second:
                        h3a_copy(t)
                    if s == 0 and second:
                        act.wait_ge(S["ctr1_in_psum"], t)
                        act.activation(ctr[1][:, 0:N], ps_a[:, :], ACT.Copy).then_inc(S["ctr1_ready"], 1)
                    if s == 4 and second:
                        act.wait_ge(S["ctr1_ready"], t)
                        act.wait_ge(S["h_ready"], T * t)
                        ctr16_copy(1)
                    if s == 4 and second:
                        sorted_copy(1, t)
                    if s == 4 and second:
                        ext_copy(1, t)
                    if s == 11 and second:
                        h3_copy(t)
                    if s == 15 and first:
                        act.wait_ge(S["input_loaded"], 64 * t + 128)
                        act.wait_ge(S["h_ready"], T * t + NG)
                        ctr16_copy(0)
                    if s == 14 and first:
                        sorted_copy(0, t + 2)
                    if s == 15 and first:
                        ext_copy(0, t + 2)
                    if on(s - COPY):
                        h_copy(t, s - COPY)
                    if s < T and on(s):
                        y_copy(t, s)
                        exponentials(t, s)

            def skip(y, exps, h):
                act.sem_inc(S["y_copied"], y)
                act.sem_inc(S["exp_ready"], exps)
                act.sem_inc(S["h_copied"], h)
                act.sem_inc(S["h_summed"], h)

            act.wait_ge(S["input_loaded"], 64)
            act.wait_ge(S["zero_ready"], GH)
            ctr16_copy(0)
            sorted_copy(0, 1)
            ext_copy(0, 1)
            iteration(0, carry=False, second=False)
            all_pass(act, "passed_first")
            skip(2 * NG, NG, NG - COPY)
            with act.Fori(1, nb) as t:
                iteration(t)
            iteration(nb, first=False)
            h3a_copy(nb + 1)
            h3_copy(nb + 1)

        @block.tensor
        def _(pe):
            ident = keep["ident"]

            def transpose_input(l, n, ready, count):
                pe.wait_ge(ready, count)
                for j in range(NC):
                    last = pe.transpose(ps_a[:, j * P:(j + 1) * P], ctr[l][:, j * P:(j + 1) * P], ident[:, :])
                last.then_inc(L["input_transposed"][l], 1)

            def count_ranks(t, final):
                if final:
                    pe.wait_ge(L["var_ready"][1], t)
                for c in range(METHODS):
                    for j in range(NC):
                        at = ps_b[:, c * NC + j:c * NC + j + 1]
                        for i in range(NC):
                            if c == j == 0:
                                pe.wait_ge(S["compared"], NC * (t + 1) + i + 1)
                            pe.matmul(at, perm[:, c, i, j * P:(j + 1) * P], ones[:, :], start=i == 0, stop=False)
                        last = pe.matmul(at, tie[:, j, c, :], ones[:, :], start=False, stop=True)
                last.then_inc(S["counted"], 1)

            def sort(l, n, chunks, bank_left=None, count=None):
                if bank_left is not None:
                    pe.wait_ge(bank_left, count)
                pe.wait_ge(L["perm_ready"][l], n)
                pe.wait_ge(L["split_ready"][l], n)
                for r in chunks:
                    for p in range(METHODS):
                        at = ps_b[:, r * P:(r + 1) * P].rearrange("p (h m c) -> p h m c", h=GH, m=METHODS)[:, :, p, :]
                        for j in range(NC):
                            for part in range(3):
                                last = pe.matmul(at, perm[:, PERM[l][p], j, r * P:(r + 1) * P],
                                                 ft3[:, j, part, :].rearrange("p (h c) -> p h c", h=GH),
                                                 start=j == part == 0, stop=j == NC - 1 and part == 2)
                if r == NC - 1:
                    last.then_inc(L["sorted_in_psum"][l], 1)

            def transpose_sorted(l, n):
                pe.wait_ge(L["sorted_copied"][l], n)
                for r in range(NC):
                    last = pe.transpose(ps_a[:, r * P:(r + 1) * P], srt[:, r, :], ident[:, :])
                last.then_inc(L["sorted_t_in_psum"][l], 1)

            def totals(l, n):
                pe.wait_ge(L["s12_ready"][l], n)
                pe.matmul(ps_b[:, 0:2], keep["same"][l][:, :], s12[:, l, :], start=True, stop=True).then_inc(L["totals_ready"][l], 1)

            def product_of_inputs(t):
                pe.wait_ge(L["var_ready"][0], min(t, nb) if isinstance(t, int) else t)
                pe.wait_ge(S["final_loaded"], 32 * t)
                pe.matmul(ps_b[0:C, :], keep["w3"][:, 1, :], ctr[1][:, 0:N], start=True, stop=False, skip_group_check=True)
                pe.matmul(ps_b[0:C, :], keep["w3f"][:, :], fin0[:, :], start=False, stop=True, skip_group_check=True).then_inc(S["h3a_ready"], 1)

            def last_product(t, ranked=None):
                pe.wait_ge(L["norm_ready"][1], t)
                pe.wait_ge(S["h3a_copied"], t)
                if ranked is not None:
                    pe.wait_ge(S["ranks_ready"], ranked)
                pe.matmul(ps_b[0:C, :], ident[:, 0:C], h3a[:, :], start=True, stop=False, skip_group_check=True)
                for r in range(2):
                    at = r * (NPAD // 2)
                    w = min(NPAD // 2, N - at)
                    last = pe.matmul(ps_b[0:C, at:at + w], keep["w3"][:, 2 + r, :], fo[1][:, 0:w], start=False, stop=r == 1, skip_group_check=True)
                last.then_inc(S["h3_ready"], 1)

            def second_input(t):
                pe.wait_ge(L["norm_ready"][0], t)
                for cg in range(4):
                    at = cg * (NPAD // 4)
                    w = min(NPAD // 4, N - at)
                    last = pe.matmul(ps_a[:, at:at + w], keep["gather"][:, cg, :], fo[0][:, 0:w], start=True, stop=True)
                last.then_inc(S["ctr1_in_psum"], 1)

            def scores(t, s):
                l, g, cgs, jg, jp = layer(s)
                O = OUTC[l]
                jc = NBLK // cgs
                blocks = [cg * jc + g * jg + jj for cg in range(cgs) for jj in range(jg)]
                if g == 0:
                    pe.wait_ge(L["dif_ready"][l], t if l else t + 1)
                pe.wait_ge(S["scores_folded"], T * t + s + 1)
                bank = ps_s[s % 2]
                pe.matmul(bank[:, :], keep["ind"][:, :], keep["off"][:, :], start=True, stop=False, skip_group_check=True)
                for u, j in enumerate(blocks):
                    last = pe.matmul(bank[:, u * 32:u * 32 + 32], dbd[l][:, j].rearrange("p h c -> p (h c)"), dif[l][:, j, :],
                                     start=False, stop=u == GB - 1, skip_group_check=True)
                last.then_inc(S["scores_ready"], 1)
                k = GB // (1 + l)
                for u, j in enumerate(blocks):
                    n = yunit(s, u)
                    if u % k == 0:
                        pe.wait_ge(S["y_copied"], YU * t + n + (2 if n == 0 and not (isinstance(t, int) and t == 0) else 1))
                    bd = dbd[l][:, j].rearrange("p h c -> p (h c)")
                    at = ps_y[n % 2][:, (u % k) * O:(u % k) * O + O]
                    pe.matmul(at, bd, keep["wc"][l][:, 1, 0, :], start=True, stop=False)
                    last = pe.matmul(at, bd, keep["wc"][l][:, 1, 1, :], start=False, stop=True)
                    if u % k == k - 1:
                        last.then_inc(S["y_ready"], 1)

            def product(t, s):
                l, g, cgs, jg, jp = layer(s)
                O = OUTC[l]
                if g == 0:
                    pe.wait_ge(L["ctr16_ready"][l], t if l else t + 1)
                pe.wait_ge(S["pt_ready"], T * t + s + 3)
                pe.wait_ge(S["y_copied"], YU * t + yunit(s, GB - 1) + 3)
                pe.wait_ge(S["h_copied"], T * t + s + 1)
                bank = ps_h[s % 2]
                for cg in range(cgs):
                    pts = (cg * (NBLK // cgs) + g * jg) * PB
                    rows = slice(cg * O, cg * O + O)
                    mv = ctr16[l][:, pts:pts + jp].unsqueeze(2).to_broadcast([P, jp, K])
                    at = bank[rows, 0:jp * K].rearrange("p (i k) -> p i k", k=K)
                    pe.matmul(at, keep["wc"][l][:, 0, 0, :], mv, start=True, stop=False, skip_group_check=True)
                    pe.matmul(at, keep["wc"][l][:, 0, 1, :], mv, start=False, stop=False, skip_group_check=True)
                    for jj in range(jg):
                        u = cg * jg + jj
                        last = pe.matmul(bank[rows, jj * 30:jj * 30 + 30], ys[:, YS_RING[s], u, 0:O], pt[:, PT_RING[s], u * 32:u * 32 + 30],
                                         start=False, stop=jj == jg - 1, skip_group_check=True)
                last.then_inc(S["h_ready"], 1)

            def iteration(t, carry=True, first=True, second=True):
                on = lambda x: carry if x < 0 else first if x in L0 else second and x in L1
                for s in range(T if first else T + PRODUCT):
                    if s == MAX and not first:
                        all_pass(pe, "passed_last")
                        skip(NG, NG, NG)
                    if on(s - PRODUCT):
                        product(t, s - PRODUCT)
                    if s < T and on(s):
                        scores(t, s)
                    if s == 0 and second:
                        product_of_inputs(t)
                    if s == 0 and second:
                        second_input(t)
                    if s == 1 and second:
                        transpose_input(1, t, S["ctr1_ready"], t)
                    for r in {2: (0, 1), 3: (2, 3)}.get(s, ()) if second else ():
                        sort(1, t, (r,))
                    if s == 4 and second:
                        transpose_sorted(1, t)
                    if s == 7 and second:
                        totals(1, t)
                    if s == 8 and first:
                        count_ranks(t, second)
                    if s == 10 and second:
                        last_product(t, t + 2 if first else None)
                    if s == 11 and first:
                        transpose_input(0, t + 2, S["input_loaded"], 64 * t + 128)
                    for r in {13: (0, 1), 14: (2, 3)}.get(s, ()) if first else ():
                        sort(0, t + 2, (r,), S["h3_copied"] if second else None, t)
                    if s == 14 and first:
                        transpose_sorted(0, t + 2)
                    if s == 17 and first:
                        totals(0, t + 1)

            def skip(scores_, y, h):
                pe.sem_inc(S["scores_ready"], scores_)
                pe.sem_inc(S["y_ready"], y)
                pe.sem_inc(S["h_ready"], h)

            pe.wait_ge(S["zero_ready"], GH)
            transpose_input(0, 1, S["input_loaded"], 64)
            count_ranks(-1, False)
            sort(0, 1, range(NC))
            transpose_sorted(0, 1)
            iteration(0, carry=False, second=False)
            all_pass(pe, "passed_first")
            skip(NG, 2 * NG, NG - PRODUCT)
            with pe.Fori(1, nb) as t:
                iteration(t)
            iteration(nb, first=False)
            product_of_inputs(nb + 1)
            pe.wait_ge(S["h3a_copied"], nb + 1)
            totals(1, nb + 1)
            last_product(nb + 1)

        @block.vector
        def _(dve):
            chain = [None]

            def link(ins):
                chain[0](ins)

            def begin(n):
                dve.wait_ge(S["keys_loaded"], 16 * n)
                link(dve.tensor_copy(kcol[:, :, :], keep["keys"][:, :, :, bass.ds(n - 1, 1)].rearrange("p j m b -> p j (m b)")))

            def compare(i):
                for c in range(METHODS):
                    key = kcol[:, i, c:c + 1]
                    dve.tensor_scalar(out=perm[:, c, i, 0:(i + 1) * P], in0=krow[:, c, 0:(i + 1) * P], scalar1=key, scalar2=None, op0=ALU.is_gt)
                    if i < NC - 1:
                        dve.tensor_scalar(out=perm[:, c, i, (i + 1) * P:N], in0=krow[:, c, (i + 1) * P:N], scalar1=key, scalar2=None, op0=ALU.is_ge)
                    last = dve.scalar_tensor_tensor(out=tie[:, i, c, :], in0=krow[:, c, i * P:(i + 1) * P], scalar=key,
                                                    in1=keep["tri"][:, :], op0=ALU.is_equal, op1=ALU.mult)
                last.then_inc(S["compared"], 1)

            def ranks(t):
                link(dve.tensor_copy(rank[1][:, :, :], rank[0][:, :, :]))
                dve.wait_ge(S["counted"], t + 2)
                dve.tensor_copy(rank[0][:, :, :], ps_b[:, 0:METHODS * NC].rearrange("p (m j) -> p m j", m=METHODS)).then_inc(S["ranks_ready"], 1)
                dve.wait_ge(S["ranks_ready"], t + 2)

            def one_hot(l, c):
                for j in range(NC):
                    last = dve.tensor_scalar(out=perm[:, c, j, :], in0=keep["iota"][:, :], scalar1=rank[l][:, c, j:j + 1],
                                             scalar2=None, op0=ALU.is_equal)
                if c == METHODS - 1:
                    last.then_inc(L["perm_ready"][1 if l else 0], 1)

            def split(l, n):
                dve.wait_ge(L["input_transposed"][l], n)
                src = ps_a[:, :].rearrange("p (j h m c) -> p j h m c", j=NC, h=GH, m=METHODS)[:, :, :, 0, :]
                link(dve.tensor_copy(ftf[:, :, :].rearrange("p j (h c) -> p j h c", h=GH), src))
                link(dve.tensor_copy(ft3[:, :, 0, :], ftf[:, :, :]))
                link(dve.tensor_tensor(ftr[:, :, :], ftf[:, :, :], ft3[:, :, 0, :], ALU.subtract))
                link(dve.tensor_copy(ft3[:, :, 1, :], ftr[:, :, :]))
                link(dve.tensor_tensor(ftr[:, :, :], ftr[:, :, :], ft3[:, :, 1, :], ALU.subtract))
                dve.tensor_copy(ft3[:, :, 2, :], ftr[:, :, :]).then_inc(L["split_ready"][l], 1)

            def block_diagonal(l, n, h):
                if h == 0:
                    dve.wait_ge(L["differences_ready"][l], n)
                rows = slice(32 * h, 32 * h + 32)
                last = dve.tensor_copy(dbd[l][rows, :, h, :], dif[l][rows, :, :])
                if h == GH - 1:
                    last.then_inc(L["dif_ready"][l], 1)

            def sum_up(l, n, steps):
                dve.wait_ge(S["h_summed"], steps)
                dve.tensor_reduce(out=s12[:, l, :], in_=sums[l][:, :, :], axis=AX.X, op=ALU.add).then_inc(L["s12_ready"][l], 1)

            def variances(l, n):
                dve.wait_ge(L["totals_ready"][l], n)
                cnt = float(N * K)
                v = st[l]
                link(dve.tensor_scalar(out=v[:, 0:1], in0=ps_b[:, 0:1], scalar1=1.0 / (cnt * WSCALE), scalar2=None, op0=ALU.mult))
                link(dve.tensor_scalar(out=v[:, 1:2], in0=ps_b[:, 1:2], scalar1=1.0 / (cnt * WSCALE * WSCALE), scalar2=LN_EPS,
                                       op0=ALU.mult, op1=ALU.add))
                link(dve.tensor_tensor(v[:, 2:3], v[:, 0:1], v[:, 0:1], ALU.mult))
                dve.tensor_tensor(v[:, 3:4], v[:, 1:2], v[:, 2:3], ALU.subtract).then_inc(L["var_ready"][l], 1)
                link(dve.tensor_tensor(v[:, 0:1], v[:, 0:1], keep["bias"][l][:, :], ALU.add))
                link(dve.tensor_scalar(out=hm[l][:, :], in0=hm[l][:, :], scalar1=1.0 / WSCALE, scalar2=keep["bias"][l][:, 0:1],
                                       op0=ALU.mult, op1=ALU.add))

            def normalise(l, n):
                dve.wait_ge(L["rstd_ready"][l], n)
                link(dve.tensor_scalar(out=hm[l][:, :], in0=hm[l][:, :], scalar1=st[l][:, 0:1], scalar2=st[l][:, 4:5],
                                       op0=ALU.subtract, op1=ALU.mult))
                dve.scalar_tensor_tensor(out=fo[l][:, :], in0=hm[l][:, :], scalar=0.2, in1=hm[l][:, :],
                                         op0=ALU.mult, op1=ALU.max).then_inc(L["norm_ready"][l], 1)

            def variance3(t):
                dve.wait_ge(S["h3_copied"], t)
                link(dve.bn_stats(out=bst[:, :], in_=h3[:, :]))
                link(dve.bn_aggr(out=bmv[:, 0:2], in_=bst[:, :]))
                dve.tensor_scalar(out=bmv[:, 2:3], in0=bmv[:, 1:2], scalar1=LN_EPS, scalar2=None, op0=ALU.add).then_inc(S["var3_ready"], 1)

            def output(t):
                dve.wait_ge(S["rstd3_ready"], t)
                link(dve.tensor_scalar(out=h3[:, :], in0=h3[:, :], scalar1=bmv[:, 0:1], scalar2=bmv[:, 3:4], op0=ALU.subtract, op1=ALU.mult))
                link(dve.scalar_tensor_tensor(out=h3[:, :], in0=h3[:, :], scalar=0.2, in1=h3[:, :], op0=ALU.mult, op1=ALU.max))
                dve.wait_ge(S["final_loaded"], 32 * t)
                dve.tensor_tensor(h3[:, :], h3[:, :], xb[:, :], ALU.add).then_inc(S["out_ready"], 1)

            def fold(t, s):
                dve.wait_ge(S["scores_ready"], T * t + s + 1)
                sv = ps_s[s % 2][:, :].rearrange("p (u c) -> p u c", u=GB)[:, :, 0:PB * K].rearrange("p u (i k) -> p u k i", i=PB)
                dve.tensor_reduce(out=fs[:, s % 2, :, :], in_=sv, axis=AX.X, op=ALU.max).then_inc(S["scores_folded"], 1)

            def maxima(t, s):
                dve.wait_ge(S["scores_folded"], T * t + s + 3)
                dve.tensor_reduce(out=mx[:, s % 2, :], in_=fs[:, s % 2, :, :], axis=AX.X, op=ALU.max).then_inc(S["max_ready"], 1)

            def add_up(t, x):
                dve.wait_ge(S["exp_ready"], T * t + x + 1)
                dve.tensor_reduce(out=zs[:, x % 2, :], in_=e[:, E_RING[x], :, :], axis=AX.X, op=ALU.add).then_inc(S["sum_ready"], 1)

            def invert(t, x):
                dve.wait_ge(S["sum_ready"], T * t + x + 1)
                dve.reciprocal(iz[:, x % 2, :], zs[:, x % 2, :]).then_inc(S["inverse_ready"], 1)

            def flip(t, s):
                dve.wait_ge(S["probs_ready"], T * t + s + 1)
                if not (isinstance(t, int) and t == 0 and s < 2):
                    dve.wait_ge(S["h_ready"], T * t + s - 1)
                dve.transpose(pt[:, PT_RING[s], :], pn[:, s % 2, :, :].rearrange("p u c -> p (u c)")).then_inc(S["pt_ready"], 1)

            def window_max(t, s):
                l, g, cgs, jg, jp = layer(s)
                dve.wait_ge(S["h_copied"], T * t + s + 3)
                dve.tensor_reduce(out=hm[l][:, g * jp:(g + 1) * jp], in_=hs[:, s % 2, 0:jp * K].rearrange("p (i k) -> p i k", k=K),
                                  axis=AX.X, op=ALU.max).then_inc(S["h_max_done"], 1)

            def iteration(t, carry=True, first=True, second=True):
                chain[0] = Chain(dve, s_d)
                on = lambda x: carry if x < 0 else first if x in L0 else second and x in L1
                for s in range(T if first else T + MAX):
                    new, old = s < T and on(s), on(s - 1)
                    if new:
                        fold(t, s)
                    if old:
                        add_up(t, s - 1)
                    if new:
                        maxima(t, s)
                    if old:
                        invert(t, s - 1)
                    if on(s - 2):
                        flip(t, s - 2)
                    if on(s - MAX):
                        window_max(t, s - MAX)
                    if second:
                        if s == 0:
                            split(1, t)
                        if s == MAX:
                            sum_up(1, t, T * t)
                        if s == 7:
                            variances(1, t)
                        if s == 9:
                            normalise(1, t)
                        for h in {8: (0, 1), 9: (2, 3)}.get(s, ()):
                            block_diagonal(1, t, h)
                        if s == 13:
                            variance3(t)
                        if s == 13:
                            output(t)
                    if s == MAX and not first:
                        all_pass(dve, "passed_last")
                        skip(NG, NG, NG, NG)
                    if first:
                        if s == 4:
                            begin(t + 2)
                            if second:
                                dve.wait_ge(L["sorted_in_psum"][1], t)
                        for i in {4: (0,), 5: (1,), 6: (2,), 7: (3,)}.get(s, ()):
                            compare(i)
                        if s == 8:
                            ranks(t)
                        for c in {10: (0, 1), 11: (2, 3)}.get(s, ()):
                            one_hot(0, c)
                        if s == 11:
                            split(0, t + 2)
                        if s == 14:
                            dve.wait_ge(L["sorted_in_psum"][0], t + 2)
                        for c in {14: (0,), 15: (1,), 16: (2,), 17: (3,)}.get(s, ()):
                            one_hot(1, c)
                        if s == 17:
                            sum_up(0, t + 1, T * t + NG)
                        if s == 18:
                            variances(0, t + 1)
                        if s == 18:
                            normalise(0, t + 1)
                        for h in {19: (0, 1), 20: (2, 3)}.get(s, ()):
                            block_diagonal(0, t + 2, h)

            def skip(folds, own_, flips, maxima):
                dve.sem_inc(S["scores_folded"], folds)
                dve.sem_inc(S["max_ready"], folds)
                dve.sem_inc(S["sum_ready"], own_)
                dve.sem_inc(S["inverse_ready"], own_)
                dve.sem_inc(S["pt_ready"], flips)
                dve.sem_inc(S["h_max_done"], maxima)

            for n in ("scores_folded", "y_copied", "h_copied", "h_max_done", "pt_ready"):
                dve.sem_inc(S[n], 2)
            dve.sem_inc(S["out_ready"], 1)
            dve.sem_inc(S["out_stored"], 16)
            chain[0] = Chain(dve, s_d)
            for bank in ps_h:
                link(dve.memset(bank[:, :], 0.0))
            begin(1)
            for i in range(NC):
                compare(i)
            link(dve.memset(rank[0][:, :, :], 0.0))
            dve.wait_ge(S["zero_ready"], GH)
            ranks(-1)
            for c in range(METHODS):
                one_hot(0, c)
            split(0, 1)
            for h in range(GH):
                block_diagonal(0, 1, h)
            dve.sem_clear(s_d)
            iteration(0, carry=False, second=False)
            all_pass(dve, "passed_first")
            skip(NG, NG - 1, NG - 2, NG - MAX)
            with dve.Fori(1, nb) as t:
                dve.sem_clear(s_d)
                iteration(t)
            dve.sem_clear(s_d)
            iteration(nb, first=False)
            sum_up(1, nb + 1, T * (nb + 1))
            variances(1, nb + 1)
            normalise(1, nb + 1)
            variance3(nb + 1)
            output(nb + 1)


def constants(nc, ctx):
    m = Memory(nc, ctx)
    return {
        "ident": m.sb("ident", [P, P]),
        "iota": m.sb("iota", [P, N], F16),
        "tri": m.sb("tri", [P, P]),
        "ind": m.sb("ind", [P, P], BF16),
        "off": m.sb("off", [P, 512], BF16),
        "same": [m.sb(f"same{l}", [P, P]) for l in range(2)],
        "gather": m.sb("gather", [P, 4, P]),
        "dif": [m.sb(f"dif{l}", [P, NBLK, 32], F16) for l in range(2)],
        "dbd": [m.sb(f"dbd{l}", [P, NBLK, GH, 32], F16) for l in range(2)],
        "w3": m.sb("w3", [P, 4, C]),
        "w3f": m.sb("w3f", [C, C]),
        "keys": m.sb("keycols", [P, NC, METHODS, B + 1]),
        "wc": [m.sb(f"wc{l}", [P, 2, 2, OUTC[l]], F16) for l in range(2)],
        "bias": [m.sb(f"bias{l}", [P, 1]) for l in range(2)],
    }


def layernorm_transposed(dve, pool_hook, link, src, mv, stats, veps, rstd_ready, rstd, dst, var_ready):
    for t in range(NT):
        link(dve.bn_stats(out=stats[:, t, :], in_=src[:, t, :]))
        link(dve.bn_aggr(out=mv[:, t, :], in_=stats[:, t, :]))
        dve.tensor_scalar(out=veps[:, t:t + 1], in0=mv[:, t, 1:2], scalar1=LN_EPS, scalar2=None,
                          op0=ALU.add).then_inc(var_ready, 1)
    for t in range(NT):
        dve.wait_ge(rstd_ready, t + 1)
        dve.tensor_scalar(out=dst[:, t, :], in0=src[:, t, :], scalar1=mv[:, t, 0:1], scalar2=rstd[:, t:t + 1],
                          op0=ALU.subtract, op1=ALU.mult).then_inc(pool_hook, 1)


def self_attention(nc, a, keep, scratch):
    H, DN, DQ, DV = 32, 128, 192, 128
    HS = 4
    HC = HS * DN
    SCALE = float(DQ) ** -0.5
    with ExitStack() as ctx:
        m = Memory(nc, ctx)
        hn = m.sb("a_hn", [P, NT, N])
        hT = [m.sb(f"a_hT{i}", [P, NC, TOK], F16) for i in range(2)]
        stats = m.sb("a_stats", [P, NT, 6])
        mv = m.sb("a_mv", [P, NT, 2])
        veps = m.sb("a_veps", [P, NT])
        rstd = m.sb("a_rstd", [P, NT])
        mhalf = m.sb("a_mhalf", [P, NT])
        WM = 4 * HC
        stage = m.sb("a_stage", [P, 4, WM])
        w16 = [m.sb(f"a_w16_{i}", [P, 4, WM], F16) for i in range(2)]
        qT = m.sb("a_qT", [P, HS, TOK])
        kT = m.sb("a_kT", [P, HS, TOK])
        v = m.sb("a_v", [P, NT, HC])
        sc = m.sb("a_sc", [P, HS * NT, C])
        mx = m.sb("a_mx", [P, HS * NT])
        zs = m.sb("a_zs", [P, HS * NT])
        pbd = m.sb("a_pbd", [P, HS, NT, P])
        oT = [m.sb(f"a_oT{i}", [P, HS, TOK], F16) for i in range(2)]
        causal = m.sb("a_causal", [P, C])
        empty = m.sb("a_empty", [P, P], F16)
        x1, x2 = keep["x1"], keep["x2"]
        ps_out = [m.ps(f"a_out{t}") for t in range(NT)]
        ps_w = [m.ps(f"a_proj{i}") for i in range(2)]
        ps_s = m.ps("a_scores")
        ps_o = m.ps("a_heads")

        S = {n: m.sem("a_" + n) for n in (
            "x_loaded", "var_ready", "rstd_ready", "hn_ready", "hT_in_psum", "hT_ready", "causal_ready", "wq_loaded",
            "wk_loaded", "wv_loaded", "wo_loaded", "high_ready", "low_ready", "w_used", "proj_ready", "proj_copied", "scores_ready",
            "scores_used", "shifted", "exp_ready", "pt_ready", "heads_ready", "heads_high", "heads_copied", "out_ready", "zero_ready")}
        loaded = (S["wq_loaded"], S["wk_loaded"], S["wv_loaded"], S["wo_loaded"])
        LOADS = (NC, 1, 1, 1)
        TERMS = ((0, 0), (0, 1), (1, 0))
        s_d, s_g = m.sem("self_dve_step"), m.sem("self_pool_step")
        block = ctx.enter_context(nc.Block())
        NP_ = 2 * HS + NT

        @block.sync
        def _(sp):
            for t in range(NT):
                sp.dma_start(x1[:, t, :], scratch["x1"][C + t * P:C + (t + 1) * P, :]).then_inc(S["x_loaded"], 16)
            wq_d = a["L0_attn_wq"].rearrange("(k p) (s h d) -> s p k h d", p=P, h=HS, d=DQ)
            wk_d = a["L0_attn_wkv"][:, 0:H * DN].rearrange("(k p) (s d) -> s p k d", p=P, d=HC)
            wv_d = a["L0_attn_wkv"][:, H * DN:H * (DN + DV)].rearrange("(k p) (s d) -> s p k d", p=P, d=HC)
            wo_d = a["L0_attn_wo"].rearrange("(s h p) n -> s p h n", p=P, h=HS)
            def load(n, w):
                sp.wait_ge(S["low_ready"], 4 * n + w + 1)
                if w == 0:
                    wq = stage[:, 0, :].rearrange("p (k h d) -> p k h d", k=NC, h=HS)
                    for k in range(NC):
                        sp.dma_start(wq[:, k], wq_d[n][:, k, :, 0:DN]).then_inc(loaded[0], 16)
                else:
                    src = (wk_d, wv_d, wo_d)[w - 1][n]
                    sp.dma_start(stage[:, w, :].rearrange("p (k d) -> p k d", k=4), src).then_inc(loaded[w], 16)

            with sp.Fori(0, H // HS) as n:
                for w in range(4):
                    load(n, w)

        @block.gpsimd
        def _(pool):
            link = Chain(pool, s_g)
            pool.memset(mhalf[:, :], -0.5)
            link(pool.memset(empty[:, :], 0.0))
            link(pool.memset(causal[:, :], 0.0))
            for r in range(P // C):
                last = pool.affine_select(out=causal[r * C:(r + 1) * C, :], in_=causal[r * C:(r + 1) * C, :], compare_op=ALU.is_ge,
                                          fill=NEG, base=0, pattern=[[-1, C]], channel_multiplier=1)
            last.then_inc(S["causal_ready"], 1)
            pool.wait_ge(S["causal_ready"], 1)
            pool.memset(pbd[:, :, :, :], 0.0).then_inc(S["zero_ready"], 1)
            for t in range(NT):
                pool.wait_ge(S["var_ready"], t + 1)
                pool.tensor_tensor(rstd[:, t:t + 1], veps[:, t:t + 1], mhalf[:, t:t + 1], ALU.pow).then_inc(S["rstd_ready"], 1)

        @block.tensor
        def _(pe):
            for k in range(NC):
                for t in range(NT):
                    pe.wait_ge(S["hn_ready"], t + 1)
                    last = pe.transpose(ps_out[k][:, t * P:(t + 1) * P], hn[:, t, k * P:(k + 1) * P], keep["ident"][:, :])
                last.then_inc(S["hT_in_psum"], 1)
            pe.wait_ge(S["hT_ready"], NC)
            for t in range(NT):
                pe.matmul(ps_out[t][:, :], empty[:, :], hT[0][:, 0, :], start=True, stop=False, skip_group_check=True)
            with pe.Fori(0, H // HS) as n:
                for w in range(2 * HS):
                    h, mat = w % HS, w // HS
                    if h == 0:
                        pe.wait_ge(S["low_ready"], 4 * n + mat + 5)
                    pe.wait_ge(S["proj_copied"], NP_ * n + w + 1)
                    for k in range(NC):
                        for j, (wp, ap) in enumerate(TERMS):
                            at = k * HC + h * DN
                            last = pe.matmul(ps_w[w % 2][:, :], w16[wp][:, mat, at:at + DN], hT[ap][:, k, :],
                                             start=k == j == 0, stop=k == NC - 1 and j == 2)
                    last.then_inc(S["proj_ready"], 1)
                pe.wait_ge(S["proj_copied"], NP_ * n + 2 * HS + 2)
                pe.wait_ge(S["scores_used"], n + 1)
                for h in range(HS):
                    for t in range(NT):
                        for q in range(P // C):
                            tok = slice(t * P + q * C, t * P + q * C + C)
                            at = (h * NT + t) * C
                            last = pe.matmul(ps_s[q * C:(q + 1) * C, at:at + C], qT[:, h, tok], kT[:, h, tok], start=True, stop=True)
                last.then_inc(S["scores_ready"], 1)
                pe.wait_ge(S["low_ready"], 4 * n + 2 + 5)
                for t in range(NT):
                    w = 2 * HS + t
                    pe.wait_ge(S["proj_copied"], NP_ * n + w + 1)
                    for k in range(NC):
                        for j, (wp, ap) in enumerate(TERMS):
                            last = pe.matmul(ps_w[w % 2][:, :], hT[ap][:, k, t * P:(t + 1) * P], w16[wp][:, 2, k * HC:(k + 1) * HC],
                                             start=k == j == 0, stop=k == NC - 1 and j == 2)
                    last.then_inc(S["proj_ready"], 1)
                pe.wait_ge(S["pt_ready"], n + 1)
                pe.wait_ge(S["proj_copied"], NP_ * n + NP_ + 2)
                for h in range(HS):
                    pe.wait_ge(S["heads_copied"], HS * n + h + 1)
                    for t in range(NT):
                        last = pe.matmul((ps_o, ps_s)[h % 2][:, t * P:(t + 1) * P], v[:, t, h * DV:(h + 1) * DV], pbd[:, h, t, :],
                                         start=True, stop=True)
                    last.then_inc(S["heads_ready"], 1)
                pe.wait_ge(S["low_ready"], 4 * n + 3 + 5)
                pe.wait_ge(S["heads_copied"], HS * n + HS + 2)
                for t in range(NT):
                    for h in range(HS):
                        for wp, ap in TERMS:
                            last = pe.matmul(ps_out[t][:, :], oT[ap][:, h, t * P:(t + 1) * P], w16[wp][:, 3, h * N:(h + 1) * N],
                                             start=False, stop=False, skip_group_check=True)
                last.then_inc(S["w_used"], 1)

        @block.scalar
        def _(act):
            with act.Fori(0, H // HS) as n:
                def copy(w):
                    act.wait_ge(S["proj_ready"], NP_ * n + w + 1)
                    dst = qT[:, w, :] if w < HS else kT[:, w - HS, :] if w < 2 * HS else v[:, w - 2 * HS, :]
                    act.activation(dst, ps_w[w % 2][:, :], ACT.Copy, scale=1.0 / WSCALE).then_inc(S["proj_copied"], 1)

                for w in range(4):
                    act.wait_ge(loaded[w], 16 * LOADS[w] * n + 16 * LOADS[w])
                    if w == 3:
                        act.wait_ge(S["w_used"], n + 1)
                    act.activation(w16[0][:, w, :], stage[:, w, :], ACT.Copy, scale=WSCALE).then_inc(S["high_ready"], 1)
                for w in range(2 * HS):
                    copy(w)
                act.wait_ge(S["shifted"], n + 1)
                act.activation(sc[:, :, :], sc[:, :, :], ACT.Exp, scale=SCALE).then_inc(S["exp_ready"], 1)
                for t in range(NT):
                    copy(2 * HS + t)
                for h in range(HS):
                    act.wait_ge(S["heads_ready"], HS * n + h + 1)
                    act.activation(oT[0][:, h, :], (ps_o, ps_s)[h % 2][:, :], ACT.Copy).then_inc(S["heads_high"], 1)

        @block.vector
        def _(dve):
            dve.sem_inc(S["w_used"], 1)
            dve.sem_inc(S["low_ready"], 4)
            dve.sem_inc(S["proj_copied"], 2)
            dve.sem_inc(S["scores_used"], 1)
            dve.sem_inc(S["heads_copied"], 2)
            link = Chain(dve, s_d)
            dve.wait_ge(S["x_loaded"], 16 * NT)
            layernorm_transposed(dve, S["hn_ready"], link, x1, mv, stats, veps, S["rstd_ready"], rstd, hn, S["var_ready"])
            for k in range(NC):
                dve.wait_ge(S["hT_in_psum"], k + 1)
                link(dve.tensor_copy(hT[0][:, k, :], ps_out[k][:, :]))
                dve.tensor_tensor(hT[1][:, k, :], ps_out[k][:, :], hT[0][:, k, :], ALU.subtract).then_inc(S["hT_ready"], 1)
            dve.wait_ge(S["causal_ready"], 1)
            dve.wait_ge(S["zero_ready"], 1)
            G = HS * NT
            with dve.Fori(0, H // HS) as n:
                dve.sem_clear(s_d)
                link = Chain(dve, s_d)
                for w in range(4):
                    dve.wait_ge(S["high_ready"], 4 * n + w + 1)
                    dve.scalar_tensor_tensor(out=w16[1][:, w, :], in0=stage[:, w, :], scalar=WSCALE, in1=w16[0][:, w, :],
                                             op0=ALU.mult, op1=ALU.subtract).then_inc(S["low_ready"], 1)
                dve.wait_ge(S["scores_ready"], n + 1)
                sv = ps_s[:, :].rearrange("p (g c) -> p g c", g=G)
                dve.tensor_tensor(sc[:, :, :], sv, causal[:, :].unsqueeze(1).to_broadcast([P, G, C]), ALU.add).then_inc(S["scores_used"], 1)
                dve.wait_ge(S["scores_used"], n + 2)
                link(dve.tensor_reduce(out=mx[:, :], in_=sc[:, :, :], axis=AX.X, op=ALU.max))
                dve.tensor_tensor(sc[:, :, :], sc[:, :, :], mx[:, :].unsqueeze(2).to_broadcast([P, G, C]), ALU.subtract).then_inc(S["shifted"], 1)
                dve.wait_ge(S["exp_ready"], n + 1)
                link(dve.tensor_reduce(out=zs[:, :], in_=sc[:, :, :], axis=AX.X, op=ALU.add))
                link(dve.reciprocal(zs[:, :], zs[:, :]))
                link(dve.tensor_tensor(sc[:, :, :], sc[:, :, :], zs[:, :].unsqueeze(2).to_broadcast([P, G, C]), ALU.mult))
                for q in range(P // C):
                    rows = slice(q * C, (q + 1) * C)
                    last = dve.transpose(pbd[rows, :, :, q * C:(q + 1) * C].rearrange("p h t c -> p (h t) c"), sc[rows, :, :])
                last.then_inc(S["pt_ready"], 1)
                for h in range(HS):
                    dve.wait_ge(S["heads_high"], HS * n + h + 1)
                    dve.tensor_tensor(oT[1][:, h, :], (ps_o, ps_s)[h % 2][:, :], oT[0][:, h, :], ALU.subtract).then_inc(S["heads_copied"], 1)
            dve.wait_ge(S["w_used"], H // HS + 1)
            for t in range(NT):
                last = dve.scalar_tensor_tensor(out=x2[:, t, :], in0=ps_out[t][:, :], scalar=1.0 / WSCALE, in1=x1[:, t, :],
                                                op0=ALU.mult, op1=ALU.add)
            last.then_inc(S["out_ready"], 1)
            dve.wait_ge(S["out_ready"], 1)


def experts(nc, a, keep, scratch, out):
    E, GROUPS, INTER = 16, 4, 128
    with ExitStack() as ctx:
        m = Memory(nc, ctx)
        hn = m.sb("e_hn", [P, NT, N])
        hT = m.sb("e_hT", [P, NC, TOK])
        h16 = [m.sb(f"e_h16_{i}", [P, NC, TOK], F16) for i in range(2)]
        stats = m.sb("e_stats", [P, NT, 6])
        mv = m.sb("e_mv", [P, NT, 2])
        veps = m.sb("e_veps", [P, NT])
        rstd = m.sb("e_rstd", [P, NT])
        mhalf = m.sb("e_mhalf", [P, NT])
        rw = m.sb("e_rw", [P, NC, E])
        rb = m.sb("e_rb", [P, E])
        rbias = m.sb("e_rbias", [P, E])
        lg = m.sb("e_lg", [P, NT, E])
        gmax = m.sb("e_gmax", [P, NT, GROUPS])
        first = m.sb("e_first", [P, E])
        cand = m.sb("e_cand", [P, NT, E])
        pick = m.sb("e_pick", [P, NT, E])
        both = m.sb("e_both", [P, NT, E])
        gkeep = m.sb("e_gkeep", [P, NT, GROUPS])
        left = m.sb("e_left", [P, NT, E])
        t1 = m.sb("e_t1", [P, NT])
        t2 = m.sb("e_t2", [P, NT])
        gate = m.sb("e_gate", [P, NT, E + 1])
        gateT = m.sb("e_gateT", [E + 1, TOK])
        b3 = m.sb("e_b3", [E + 1, N])
        SLOTS = 4
        w12 = m.sb("e_w12", [P, SLOTS, 2, NC * INTER])
        w16 = [m.sb(f"e_w16_{i}", [P, 2, 2, NC * INTER], F16) for i in range(2)]
        w3 = m.sb("e_w3", [P, SLOTS, N])
        b1 = m.sb("e_b1", [P, SLOTS, 1])
        b2 = m.sb("e_b2", [P, SLOTS, 1])
        b2s = m.sb("e_b2s", [P, 2, 1])
        gb = m.sb("e_gb", [P, SLOTS, TOK])
        up = m.sb("e_up", [P, 2, TOK])
        hh = m.sb("e_hh", [P, 2, TOK])
        y = m.sb("e_y", [P, NT, N])
        x2 = keep["x2"]
        ps_y = [m.ps(f"e_y{t}") for t in range(NT)]
        ps_u = [m.ps(f"e_u{i}") for i in range(2)]
        ps_v = [m.ps(f"e_v{i}") for i in range(2)]
        S = {n: m.sem("e_" + n) for n in (
            "small_loaded", "var_ready", "rstd_ready", "hn_ready", "hT_in_psum", "hT_ready", "logits_ready", "first_ready",
            "shifted", "exp_ready", "gate_ready", "gateT_in_psum", "gateT_ready", "gateT_stored", "gates_loaded_0", "gates_loaded_1", "gates_loaded_2",
            "gates_loaded_3", "w_loaded_0", "w_loaded_1", "w_loaded_2", "w_loaded_3", "high_ready",
            "low_ready", "h_ready",
            "silu_ready", "gated_ready", "down_done", "bias_done", "y_ready", "stored")}
        loaded = [S[f"w_loaded_{r}"] for r in range(SLOTS)]
        gates_loaded = [S[f"gates_loaded_{r}"] for r in range(SLOTS)]
        TERMS = ((0, 0), (0, 1), (1, 0))
        s_d, s_g = m.sem("moe_dve_step"), m.sem("moe_pool_step")
        block = ctx.enter_context(nc.Block())
        NL = 5
        LAST = 16 * NL * (E // SLOTS + 1)

        def bcast_rows(src):
            return bass.AP(src.tensor, src.offset, [[0, P]] + [list(k) for k in src.ap])

        @block.sync
        def _(sp):
            sp.dma_start(rw[:, :, :], a["L0_ffn_router_w"].rearrange("(k p) e -> p k e", p=P)).then_inc(S["small_loaded"], 16)
            sp.dma_start(rb[:, :], bcast_rows(a["L0_ffn_router_b"])).then_inc(S["small_loaded"], 16)
            sp.dma_start(rbias[:, :], bcast_rows(a["L0_ffn_router_bias"])).then_inc(S["small_loaded"], 16)
            sp.dma_start(b3[0:E, :], a["L0_ffn_eb3"]).then_inc(S["small_loaded"], 16)
            sp.dma_start(b3[E:E + 1, :], a["L0_ffn_sb3"].rearrange("(u n) -> u n", u=1)).then_inc(S["small_loaded"], 16)
            def load(r, w1s, w2s, w3s, b1s, b2s):
                sp.dma_start(w12[:, r, 0].rearrange("p (k n) -> p k n", k=NC), w1s).then_inc(loaded[r], 16)
                sp.dma_start(w12[:, r, 1].rearrange("p (k n) -> p k n", k=NC), w2s).then_inc(loaded[r], 16)
                sp.dma_start(w3[:, r], w3s).then_inc(loaded[r], 16)
                with nc.allow_non_contiguous_dma(reason="a bias column"):
                    sp.dma_start(b1[:, r], b1s).then_inc(loaded[r], 16)
                    sp.dma_start(b2[:, r], b2s).then_inc(loaded[r], 16)

            def load_gates(r, gs):
                sp.dma_start(gb[:, r], bcast_rows(gs)).then_inc(gates_loaded[r], 16)

            def load_expert(r, e):
                load(r, a["L0_ffn_ew1"].rearrange("e (k p) n -> e p k n", p=P)[e],
                     a["L0_ffn_ew2"].rearrange("e (k p) n -> e p k n", p=P)[e], a["L0_ffn_ew3"][e],
                     col(a["L0_ffn_eb1"][e]), col(a["L0_ffn_eb2"][e]))

            col = lambda s: s.rearrange("(p u) -> p u", u=1)
            for r in range(SLOTS):
                load_expert(r, r)
            sp.wait_ge(S["gateT_ready"], 1)
            sp.dma_start(scratch["gates"], gateT[:, :]).then_inc(S["gateT_stored"], 16)
            sp.wait_ge(S["gateT_stored"], 16)
            for r in range(SLOTS):
                load_gates(r, scratch["gates"][r])
            with sp.Fori(1, E // SLOTS) as i:
                for r in range(SLOTS):
                    sp.wait_ge(S["down_done"], SLOTS * i + r + 1)
                    load_expert(r, SLOTS * i + r)
                    load_gates(r, scratch["gates"][SLOTS * i + r])
            for r in range(2):
                cols = slice(r * INTER, (r + 1) * INTER)
                sp.wait_ge(S["down_done"], E + r + 1)
                load(r, a["L0_ffn_sw1"][:, cols].rearrange("(k p) n -> p k n", p=P),
                     a["L0_ffn_sw2"][:, cols].rearrange("(k p) n -> p k n", p=P), a["L0_ffn_sw3"][cols, :],
                     col(a["L0_ffn_sb1"][cols]), col(a["L0_ffn_sb2"][cols]))
                load_gates(r, scratch["gates"][E])
            for t in range(NT):
                sp.wait_ge(S["y_ready"], t + 1)
                sp.dma_start(out.rearrange("b c n -> (b c) n")[t * P:(t + 1) * P, :], y[:, t, :]).then_inc(S["stored"], 16)
            sp.wait_ge(S["stored"], 16 * NT)

        @block.gpsimd
        def _(pool):
            link = Chain(pool, s_g)
            link(pool.memset(mhalf[:, :], -0.5))
            for t in range(NT):
                pool.wait_ge(S["var_ready"], t + 1)
                pool.tensor_tensor(rstd[:, t:t + 1], veps[:, t:t + 1], mhalf[:, t:t + 1], ALU.pow).then_inc(S["rstd_ready"], 1)
            pool.iota(first[:, :], pattern=[[-1, E]], base=E, channel_multiplier=0,
                      allow_small_or_imprecise_dtypes=True).then_inc(S["first_ready"], 1)

        @block.tensor
        def _(pe):
            for k in range(NC):
                for t in range(NT):
                    pe.wait_ge(S["hn_ready"], t + 1)
                    last = pe.transpose(ps_y[k][:, t * P:(t + 1) * P], hn[:, t, k * P:(k + 1) * P], keep["ident"][:, :])
                last.then_inc(S["hT_in_psum"], 1)
            pe.wait_ge(S["hT_ready"], NC)
            pe.wait_ge(S["small_loaded"], 80)
            for t in range(NT):
                for k in range(NC):
                    last = pe.matmul(ps_u[1][:, t * E:(t + 1) * E], hT[:, k, t * P:(t + 1) * P], rw[:, k, :], start=k == 0, stop=k == NC - 1)
            last.then_inc(S["logits_ready"], 1)
            def up_product(r, n):
                pe.wait_ge(S["low_ready"], n + 1)
                pe.wait_ge(S["gated_ready"], n + 1)
                for w, ps in ((0, ps_u[r % 2]), (1, ps_v[r % 2])):
                    for k in range(NC):
                        for j, (wp, ap) in enumerate(TERMS):
                            last = pe.matmul(ps[:, :], w16[wp][:, r % 2, w, k * INTER:(k + 1) * INTER], h16[ap][:, k, :],
                                             start=k == j == 0, stop=k == NC - 1 and j == 2)
                last.then_inc(S["h_ready"], 1)

            def down_product(r, n, nl):
                pe.wait_ge(loaded[r], nl)
                pe.wait_ge(S["gated_ready"], n + 3)
                for t in range(NT):
                    last = pe.matmul(ps_y[t][:, :], hh[:, r % 2, t * P:(t + 1) * P], w3[:, r, :], start=False, stop=False, skip_group_check=True)
                last.then_inc(S["down_done"], 1)

            up_product(0, 0)
            pe.wait_ge(S["gate_ready"], 1)
            for t in range(NT):
                last = pe.transpose(ps_v[1][0:E + 1, t * P:(t + 1) * P], gate[:, t, :], keep["ident"][:, :])
            last.then_inc(S["gateT_in_psum"], 1)
            pe.wait_ge(S["gateT_ready"], 1)
            for t in range(NT):
                pe.matmul(ps_y[t][:, :], gateT[:, t * P:(t + 1) * P], b3[:, :], start=True, stop=False, skip_group_check=True)
            with pe.Fori(0, E // SLOTS) as i:
                for r in range(SLOTS):
                    up_product((r + 1) % SLOTS, SLOTS * i + r + 1)
                    down_product(r, SLOTS * i + r, 16 * NL * i + 16 * NL)
            up_product(1, E + 1)
            for r in range(2):
                down_product(r, E + r, LAST)

        @block.scalar
        def _(act):

            def split_high(r, nl):
                act.wait_ge(loaded[r], nl)
                act.activation(w16[0][:, r % 2, :, :], w12[:, r, :, :], ACT.Copy, scale=WSCALE).then_inc(S["high_ready"], 1)

            def silu(r, n):
                act.wait_ge(S["h_ready"], n + 1)
                act.wait_ge(S["gated_ready"], n + 1)
                act.activation(up[:, r % 2, :], ps_u[r % 2][:, :], ACT.Silu, bias=b1[:, r, 0:1], scale=1.0 / WSCALE).then_inc(S["silu_ready"], 1)

            split_high(0, 16 * NL)
            act.wait_ge(S["shifted"], 1)
            act.activation(lg[:, :, :], lg[:, :, :], ACT.Exp).then_inc(S["exp_ready"], 1)
            with act.Fori(0, E // SLOTS) as i:
                for r in range(SLOTS):
                    split_high((r + 1) % SLOTS, 16 * NL * i + 16 * NL * (1 if r < SLOTS - 1 else 2))
                    silu(r, SLOTS * i + r)
            split_high(1, LAST)
            for r in range(2):
                silu(r, E + r)

        @block.vector
        def _(dve):
            dve.sem_inc(S["down_done"], SLOTS)
            dve.sem_inc(S["gated_ready"], 2)
            link = Chain(dve, s_d)
            layernorm_transposed(dve, S["hn_ready"], link, x2, mv, stats, veps, S["rstd_ready"], rstd, hn, S["var_ready"])
            for k in range(NC):
                dve.wait_ge(S["hT_in_psum"], k + 1)
                link(dve.tensor_copy(hT[:, k, :], ps_y[k][:, :]))
                link(dve.tensor_copy(h16[0][:, k, :], hT[:, k, :]))
                dve.tensor_tensor(h16[1][:, k, :], hT[:, k, :], h16[0][:, k, :], ALU.subtract).then_inc(S["hT_ready"], 1)
            def split_low(r, n):
                dve.wait_ge(S["high_ready"], n + 1)
                dve.scalar_tensor_tensor(out=w16[1][:, r % 2, :, :], in0=w12[:, r, :, :], scalar=WSCALE, in1=w16[0][:, r % 2, :, :],
                                         op0=ALU.mult, op1=ALU.subtract).then_inc(S["low_ready"], 1)
                link(dve.tensor_scalar(out=b2s[:, r % 2, :], in0=b2[:, r, :], scalar1=WSCALE, scalar2=None, op0=ALU.mult))

            split_low(0, 0)
            dve.wait_ge(S["small_loaded"], 80)
            dve.wait_ge(S["logits_ready"], 1)
            wide = lambda v, n: v.unsqueeze(2).to_broadcast([P, NT, n])
            link(dve.tensor_tensor(lg[:, :, :], ps_u[1][:, 0:NT * E].rearrange("p (t e) -> p t e", t=NT),
                                   rb[:, :].unsqueeze(1).to_broadcast([P, NT, E]), ALU.add))
            link(dve.tensor_reduce(out=t1[:, :], in_=lg[:, :, :], axis=AX.X, op=ALU.max))
            dve.tensor_tensor(lg[:, :, :], lg[:, :, :], wide(t1[:, :], E), ALU.subtract).then_inc(S["shifted"], 1)
            dve.wait_ge(S["exp_ready"], 1)
            link(dve.tensor_reduce(out=t1[:, :], in_=lg[:, :, :], axis=AX.X, op=ALU.add))
            link(dve.reciprocal(t2[:, :], t1[:, :]))
            link(dve.tensor_tensor(lg[:, :, :], lg[:, :, :], wide(t2[:, :], E), ALU.mult))
            link(dve.tensor_tensor(lg[:, :, :], lg[:, :, :], rbias[:, :].unsqueeze(1).to_broadcast([P, NT, E]), ALU.add))
            dve.wait_ge(S["first_ready"], 1)

            def top1(vals, n, into):
                fr = first[:, 0:n].unsqueeze(1).to_broadcast([P, NT, n])
                link(dve.tensor_reduce(out=t1[:, :], in_=vals, axis=AX.X, op=ALU.max))
                link(dve.tensor_tensor(cand[:, :, 0:n], vals, wide(t1[:, :], n), ALU.is_equal))
                link(dve.tensor_tensor(cand[:, :, 0:n], cand[:, :, 0:n], fr, ALU.mult))
                link(dve.tensor_reduce(out=t2[:, :], in_=cand[:, :, 0:n], axis=AX.X, op=ALU.max))
                link(dve.tensor_tensor(into, cand[:, :, 0:n], wide(t2[:, :], n), ALU.is_equal))

            def top2(vals, n, into):
                top1(vals, n, into)
                link(dve.tensor_scalar(out=left[:, :, 0:n], in0=into, scalar1=2 * NEG, scalar2=None, op0=ALU.mult))
                link(dve.tensor_tensor(left[:, :, 0:n], left[:, :, 0:n], vals, ALU.add))
                top1(left[:, :, 0:n], n, pick[:, :, 0:n])
                link(dve.tensor_tensor(into, into, pick[:, :, 0:n], ALU.add))

            GE = E // GROUPS
            link(dve.tensor_reduce(out=gmax[:, :, :], in_=lg[:, :, :].rearrange("p t (g e) -> p t g e", g=GROUPS), axis=AX.X, op=ALU.max))
            top2(gmax[:, :, :], GROUPS, gkeep[:, :, :])
            kb = gkeep[:, :, :].unsqueeze(3).to_broadcast([P, NT, GROUPS, GE])
            bv = both[:, :, :].rearrange("p t (g e) -> p t g e", g=GROUPS)
            link(dve.tensor_tensor(bv, lg[:, :, :].rearrange("p t (g e) -> p t g e", g=GROUPS), kb, ALU.mult))
            link(dve.tensor_scalar(out=gkeep[:, :, :], in0=gkeep[:, :, :], scalar1=1.0, scalar2=-NEG, op0=ALU.subtract, op1=ALU.mult))
            link(dve.tensor_tensor(bv, bv, kb, ALU.add))
            link(dve.memset(gate[:, :, :], 1.0))
            top2(both[:, :, :], E, gate[:, :, 0:E])
            dve.tensor_tensor(gate[:, :, 0:E], gate[:, :, 0:E], lg[:, :, :], ALU.mult).then_inc(S["gate_ready"], 1)
            dve.wait_ge(S["gateT_in_psum"], 1)
            dve.tensor_copy(gateT[:, :], ps_v[1][0:E + 1, :]).then_inc(S["gateT_ready"], 1)

            def gated(r, n, ng):
                dve.wait_ge(gates_loaded[r], ng)
                dve.wait_ge(S["h_ready"], n + 1)
                dve.wait_ge(S["silu_ready"], n + 1)
                dve.wait_ge(S["down_done"], n + SLOTS - 1)
                link(dve.scalar_tensor_tensor(out=hh[:, r % 2, :], in0=ps_v[r % 2][:, :], scalar=b2s[:, r % 2, 0:1], in1=up[:, r % 2, :],
                                              op0=ALU.add, op1=ALU.mult))
                dve.scalar_tensor_tensor(out=hh[:, r % 2, :], in0=hh[:, r % 2, :], scalar=1.0 / WSCALE, in1=gb[:, r, :],
                                         op0=ALU.mult, op1=ALU.mult).then_inc(S["gated_ready"], 1)

            with dve.Fori(0, E // SLOTS) as i:
                dve.sem_clear(s_d)
                link = Chain(dve, s_d)
                for r in range(SLOTS):
                    split_low((r + 1) % SLOTS, SLOTS * i + r + 1)
                    gated(r, SLOTS * i + r, 16 * i + 16)
            split_low(1, E + 1)
            for r in range(2):
                gated(r, E + r, 16 * (E // SLOTS + 1))
            dve.wait_ge(S["down_done"], E + 2 + SLOTS)
            for t in range(NT):
                dve.tensor_tensor(y[:, t, :], ps_y[t][:, :], x2[:, t, :], ALU.add).then_inc(S["y_ready"], 1)


_INS = ["x", "ctx_4096"] + ["L0_xattn_" + n for n in ("W_lin1", "b_lin1", "W_lin2", "b_lin2", "W_conv1", "W_conv2", "W_conv3")] + [
    "L0_attn_wq", "L0_attn_wkv", "L0_attn_wo"] + ["L0_ffn_" + n for n in (
        "router_w", "router_b", "router_bias", "ew1", "eb1", "ew2", "eb2", "ew3", "eb3", "sw1", "sb1", "sw2", "sb2", "sw3", "sb3")]


def build(nc, a, out):
    scratch = {
        "feats": nc.dram_tensor("feats_rows", [TOK + 2 * C, N], F32, kind="Internal").ap(),
        "keys": nc.dram_tensor("key_rows", [METHODS, B + 1, N], F32, kind="Internal").ap(),
        "x": nc.dram_tensor("x_rows", [TOK + C, N], F32, kind="Internal").ap(),
        "x1": nc.dram_tensor("x1_rows", [TOK + C, N], F32, kind="Internal").ap(),
        "gates": nc.dram_tensor("gate_rows", [17, TOK], F32, kind="Internal").ap(),
    }
    with ExitStack() as ctx:
        with ExitStack() as graph:
            keep = constants(nc, graph)
            prepare(nc, a, keep, scratch)
            cross_attention(nc, a, keep, scratch)
        m = Memory(nc, ctx)
        late = {n: m.sb("late_" + n, s) for n, s in (("x1", [P, NT, N]), ("x2", [P, NT, N]), ("ident", [P, P]))}
        identity(nc, late["ident"])
        self_attention(nc, a, late, scratch)
        experts(nc, a, late, scratch, out)


def identity(nc, t):
    with nc.semaphore("late_ident") as done, nc.Block() as block:
        @block.gpsimd
        def _(pool):
            pool.memset(t[:, :], 0.0).then_inc(done, 1)
            pool.wait_ge(done, 1)
            pool.affine_select(out=t[:, :], in_=t[:, :], compare_op=ALU.not_equal, fill=1.0, base=0,
                               pattern=[[-1, P]], channel_multiplier=1).then_inc(done, 1)
            pool.wait_ge(done, 2)


def kernel(**inputs):
    import numpy as np
    import concourse.bacc as bacc
    from concourse.bass_utils import run_bass_kernel_spmd

    nc = bacc.Bacc("TRN2", target_bir_lowering=False, num_devices=1)
    arrays, args = {}, {}
    for name in _INS:
        arrays[name] = np.ascontiguousarray(inputs[name])
        args[name] = nc.dram_tensor(name, arrays[name].shape, F32, kind="ExternalInput").ap()
    out = nc.dram_tensor("out", (B, C, N), F32, kind="ExternalOutput").ap()
    build(nc, args, out)
    r = run_bass_kernel_spmd(nc, [arrays], core_ids=[0])
    return r.results[0]["out"]
```
